# Optimizing a Trainium2 kernel written in Bass

```python
import numpy as np
import jax
import jax.numpy as jnp

def _softmax(x, axis=-1):
    return jax.nn.softmax(x, axis=axis)
def _gelu(x):
    return jax.nn.gelu(x, approximate=True)
def _silu(x):
    return jax.nn.silu(x)
def _sigmoid(x):
    return jax.nn.sigmoid(x)
def _layernorm(x, axis=-1, eps=1e-5):
    m = jnp.mean(x, axis=axis, keepdims=True)
    v = jnp.var(x, axis=axis, keepdims=True)
    return (x - m) / jnp.sqrt(v + eps)
def _scatter_add(tgt, idx, src, axis=0):
    return tgt.at[idx].add(src)
def _segment_sum(src, seg, n):
    return jax.ops.segment_sum(src, seg, n)

kernel_name = 'mk_conv_seq_d4_conv_nchw256_16eb74'

def setup_inputs(seed: int = 0):
    np.random.seed(seed)
    _w = jnp.asarray
    def _rec_inputs():
        import jax
        import jax.numpy as jnp
        _gk = jax.random.key(seed)
        x = -0.0002928 + 1 * jax.random.normal(jax.random.fold_in(_gk, 1), (4, 256, 64, 64), jnp.float32)
        return x
    x = _rec_inputs()
    def _L0_conv_setup():
        import jax, jax.numpy as jnp
        import numpy as np
        RY = jnp.array([-1.0, -1.0, -1.0, 0.0, 0.0, 0.0, 1.0, 1.0, 1.0], dtype=jnp.float32)
        RX = jnp.array([-1.0, 0.0, 1.0, -1.0, 0.0, 1.0, -1.0, 0.0, 1.0], dtype=jnp.float32)

        def conv2d(x, w, b):
            out = jax.lax.conv_general_dilated(x, w, window_strides=(1, 1), padding=((1, 1), (1, 1)), dimension_numbers=('NCHW', 'OIHW', 'NCHW'))
            return out + b[None, :, None, None]

        def group_norm(x, gamma, beta, num_groups, eps=1e-05):
            N, C, H, W = x.shape
            xg = x.reshape(N, num_groups, C // num_groups, H, W)
            mu = xg.mean(axis=(2, 3, 4), keepdims=True)
            var = xg.var(axis=(2, 3, 4), keepdims=True)
            xn = ((xg - mu) * jax.lax.rsqrt(var + eps)).reshape(N, C, H, W)
            return xn * gamma[None, :, None, None] + beta[None, :, None, None]

        def build_offset(tm, tr):
            m00, m01, m10, m11 = (tm[:, 0], tm[:, 1], tm[:, 2], tm[:, 3])
            ry = RY[None, :, None, None]
            rx = RX[None, :, None, None]
            dy = m00[:, None] * ry + m01[:, None] * rx - ry + tr[:, 0:1]
            dx = m10[:, None] * ry + m11[:, None] * rx - rx + tr[:, 1:2]
            return (dy, dx)

        def bilinear_sample(img, py, px):
            N, C, H, W = img.shape
            K = py.shape[1]
            y0f = jnp.floor(py)
            x0f = jnp.floor(px)
            wy1 = py - y0f
            wx1 = px - x0f
            wy0 = 1.0 - wy1
            wx0 = 1.0 - wx1
            y0 = y0f.astype(jnp.int32)
            x0 = x0f.astype(jnp.int32)
            img_flat = img.reshape(N, C, H * W)

            def gather(yi, xi):
                valid = ((yi >= 0) & (yi < H) & (xi >= 0) & (xi < W)).astype(img.dtype)
                idx = jnp.clip(yi, 0, H - 1) * W + jnp.clip(xi, 0, W - 1)
                flat = idx.reshape(N, 1, K * H * W)
                vals = jnp.take_along_axis(img_flat, jnp.broadcast_to(flat, (N, C, K * H * W)), axis=2)
                return vals.reshape(N, C, K, H, W) * valid[:, None]
            v00 = gather(y0, x0)
            v01 = gather(y0, x0 + 1)
            v10 = gather(y0 + 1, x0)
            v11 = gather(y0 + 1, x0 + 1)
            return v00 * (wy0 * wx0)[:, None] + v01 * (wy0 * wx1)[:, None] + v10 * (wy1 * wx0)[:, None] + v11 * (wy1 * wx1)[:, None]

        def deform_conv(x, dy, dx, w, pad=1, dil=1):
            N, C, H, W = x.shape
            k = jnp.arange(9)
            ki = (k // 3).astype(x.dtype)[None, :, None, None]
            kj = (k % 3).astype(x.dtype)[None, :, None, None]
            hh = jnp.arange(H, dtype=x.dtype)[None, None, :, None]
            ww = jnp.arange(W, dtype=x.dtype)[None, None, None, :]
            py = hh - pad + dil * ki + dy
            px = ww - pad + dil * kj + dx
            sampled = bilinear_sample(x, py, px)
            return jnp.einsum('nckhw,ock->nohw', sampled, w.reshape(w.shape[0], C, 9))
        key = jax.random.key(seed)
        ks = jax.random.split(key, 16)
        N, C, H, W = (4, 256, 64, 64)
        x = jax.random.normal(ks[0], (N, C, H, W), jnp.float32)

        def p(k, shape, s):
            return jax.random.normal(k, shape, jnp.float32) * s
        s_off = 0.01
        s_dc = 1.0 / np.sqrt(C * 9.0)
        return {'x': x, 'w_tm1': p(ks[1], (4, C, 3, 3), s_off), 'b_tm1': jnp.zeros((4,), jnp.float32), 'w_tr1': p(ks[2], (2, C, 3, 3), s_off), 'b_tr1': jnp.zeros((2,), jnp.float32), 'w_dc1': p(ks[3], (C, C, 3, 3), s_dc), 'g1': jnp.ones((C,), jnp.float32), 'be1': jnp.zeros((C,), jnp.float32), 'w_tm2': p(ks[4], (4, C, 3, 3), s_off), 'b_tm2': jnp.zeros((4,), jnp.float32), 'w_tr2': p(ks[5], (2, C, 3, 3), s_off), 'b_tr2': jnp.zeros((2,), jnp.float32), 'w_dc2': p(ks[6], (C, C, 3, 3), s_dc), 'g2': jnp.ones((C,), jnp.float32), 'be2': jnp.zeros((C,), jnp.float32)}
    _L0_conv_all = _L0_conv_setup()
    _L0_conv_in = {k: v for k, v in _L0_conv_all.items() if k in ('w_tm1', 'b_tm1', 'w_tr1', 'b_tr1', 'w_dc1', 'g1', 'be1', 'w_tm2', 'b_tm2', 'w_tr2', 'b_tr2', 'w_dc2', 'g2', 'be2', )}
    del _L0_conv_all

    def _L1_conv_setup():
        import jax, jax.numpy as jnp
        import numpy as np
        B, C, H, W = (8, 256, 64, 64)
        IC = C // 2
        key = jax.random.key(seed)
        k0, k1, k2, k3, k4 = jax.random.split(key, 5)
        s = 0.05
        return {'x': jax.random.normal(k0, (B, C, H, W), dtype=jnp.float32), 'w_theta': jax.random.normal(k1, (IC, C), dtype=jnp.float32) * s, 'w_phi': jax.random.normal(k2, (IC, C), dtype=jnp.float32) * s, 'w_g': jax.random.normal(k3, (IC, C), dtype=jnp.float32) * s, 'w_mask': jax.random.normal(k4, (C, IC), dtype=jnp.float32) * s}
    _L1_conv_all = _L1_conv_setup()
    _L1_conv_in = {k: v for k, v in _L1_conv_all.items() if k in ('w_theta', 'w_phi', 'w_g', 'w_mask', )}
    del _L1_conv_all

    def _L2_conv_setup():
        import jax, jax.numpy as jnp
        import numpy as np
        from jax import lax
        EPS = 1e-05
        P, H_DIM = (32, 4)
        C = 256

        def _bn_nchw(x, g, b):
            m = jnp.mean(x, axis=(0, 2, 3), keepdims=True)
            v = jnp.var(x, axis=(0, 2, 3), keepdims=True)
            return (x - m) * (g[None, :, None, None] / jnp.sqrt(v + EPS)) + b[None, :, None, None]

        def _bn_paths(x, g, b):
            m = jnp.mean(x, axis=(0, 3, 4), keepdims=True)
            v = jnp.var(x, axis=(0, 3, 4), keepdims=True)
            return (x - m) * (g[None, :, :, None, None] / jnp.sqrt(v + EPS)) + b[None, :, :, None, None]
        key = jax.random.key(seed)
        ks = jax.random.split(key, 8)
        B, H, W = (4, 56, 56)
        x = jax.random.normal(ks[0], (B, C, H, W), dtype=jnp.float32)
        w1 = jax.random.normal(ks[1], (P * H_DIM, C), dtype=jnp.float32) * 0.01
        b1 = jax.random.normal(ks[2], (P * H_DIM,), dtype=jnp.float32) * 0.01
        w2 = jax.random.normal(ks[3], (P * H_DIM, H_DIM, 3, 3), dtype=jnp.float32) * 0.01
        b2 = jax.random.normal(ks[4], (P * H_DIM,), dtype=jnp.float32) * 0.01
        w3 = jax.random.normal(ks[5], (P, C, H_DIM), dtype=jnp.float32) * 0.01
        b3 = jax.random.normal(ks[6], (P, C), dtype=jnp.float32) * 0.01
        g1 = jnp.ones((P * H_DIM,), jnp.float32)
        be1 = jnp.zeros((P * H_DIM,), jnp.float32)
        g2 = jnp.ones((P * H_DIM,), jnp.float32)
        be2 = jnp.zeros((P * H_DIM,), jnp.float32)
        g3 = jnp.ones((P, C), jnp.float32)
        be3 = jnp.zeros((P, C), jnp.float32)
        g4 = jnp.ones((C,), jnp.float32)
        be4 = jnp.zeros((C,), jnp.float32)
        return {'x': x, 'w1': w1, 'b1': b1, 'g1': g1, 'be1': be1, 'w2': w2, 'b2': b2, 'g2': g2, 'be2': be2, 'w3': w3, 'b3': b3, 'g3': g3, 'be3': be3, 'g4': g4, 'be4': be4}
    _L2_conv_all = _L2_conv_setup()
    _L2_conv_in = {k: v for k, v in _L2_conv_all.items() if k in ('w1', 'b1', 'g1', 'be1', 'w2', 'b2', 'g2', 'be2', 'w3', 'b3', 'g3', 'be3', 'g4', 'be4', )}
    del _L2_conv_all

    def _L3_conv_setup():
        import jax, jax.numpy as jnp
        import numpy as np
        from jax import lax
        ALPHA = 0.1
        key = jax.random.key(seed)
        k1, k2, k3 = jax.random.split(key, 3)
        B, C, H, W, K = (16, 256, 80, 80, 3)
        x = jax.random.normal(k1, (B, C, H, W), dtype=jnp.float32)
        conv_w = jax.random.normal(k2, (C, 1, K), dtype=jnp.float32) * 0.1
        conv_b = jax.random.normal(k3, (C,), dtype=jnp.float32) * 0.1
        return {'x': x, 'conv_w': conv_w, 'conv_b': conv_b}
    _L3_conv_all = _L3_conv_setup()
    _L3_conv_in = {k: v for k, v in _L3_conv_all.items() if k in ('conv_w', 'conv_b', )}
    del _L3_conv_all

    return {
        "x": x,
        "L0_conv_w_tm1": _L0_conv_in["w_tm1"],
        "L0_conv_b_tm1": _L0_conv_in["b_tm1"],
        "L0_conv_w_tr1": _L0_conv_in["w_tr1"],
        "L0_conv_b_tr1": _L0_conv_in["b_tr1"],
        "L0_conv_w_dc1": _L0_conv_in["w_dc1"],
        "L0_conv_g1": _L0_conv_in["g1"],
        "L0_conv_be1": _L0_conv_in["be1"],
        "L0_conv_w_tm2": _L0_conv_in["w_tm2"],
        "L0_conv_b_tm2": _L0_conv_in["b_tm2"],
        "L0_conv_w_tr2": _L0_conv_in["w_tr2"],
        "L0_conv_b_tr2": _L0_conv_in["b_tr2"],
        "L0_conv_w_dc2": _L0_conv_in["w_dc2"],
        "L0_conv_g2": _L0_conv_in["g2"],
        "L0_conv_be2": _L0_conv_in["be2"],
        "L1_conv_w_theta": _L1_conv_in["w_theta"],
        "L1_conv_w_phi": _L1_conv_in["w_phi"],
        "L1_conv_w_g": _L1_conv_in["w_g"],
        "L1_conv_w_mask": _L1_conv_in["w_mask"],
        "L2_conv_w1": _L2_conv_in["w1"],
        "L2_conv_b1": _L2_conv_in["b1"],
        "L2_conv_g1": _L2_conv_in["g1"],
        "L2_conv_be1": _L2_conv_in["be1"],
        "L2_conv_w2": _L2_conv_in["w2"],
        "L2_conv_b2": _L2_conv_in["b2"],
        "L2_conv_g2": _L2_conv_in["g2"],
        "L2_conv_be2": _L2_conv_in["be2"],
        "L2_conv_w3": _L2_conv_in["w3"],
        "L2_conv_b3": _L2_conv_in["b3"],
        "L2_conv_g3": _L2_conv_in["g3"],
        "L2_conv_be3": _L2_conv_in["be3"],
        "L2_conv_g4": _L2_conv_in["g4"],
        "L2_conv_be4": _L2_conv_in["be4"],
        "L3_conv_conv_w": _L3_conv_in["conv_w"],
        "L3_conv_conv_b": _L3_conv_in["conv_b"],
    }

def reference(x, L0_conv_w_tm1, L0_conv_b_tm1, L0_conv_w_tr1, L0_conv_b_tr1, L0_conv_w_dc1, L0_conv_g1, L0_conv_be1, L0_conv_w_tm2, L0_conv_b_tm2, L0_conv_w_tr2, L0_conv_b_tr2, L0_conv_w_dc2, L0_conv_g2, L0_conv_be2, L1_conv_w_theta, L1_conv_w_phi, L1_conv_w_g, L1_conv_w_mask, L2_conv_w1, L2_conv_b1, L2_conv_g1, L2_conv_be1, L2_conv_w2, L2_conv_b2, L2_conv_g2, L2_conv_be2, L2_conv_w3, L2_conv_b3, L2_conv_g3, L2_conv_be3, L2_conv_g4, L2_conv_be4, L3_conv_conv_w, L3_conv_conv_b):
    import jax
    import jax.numpy as jnp
    def _L0_conv_ref(x, w_tm1, b_tm1, w_tr1, b_tr1, w_dc1, g1, be1, w_tm2, b_tm2, w_tr2, b_tr2, w_dc2, g2, be2):
        import jax, jax.numpy as jnp
        import numpy as np
        RY = jnp.array([-1.0, -1.0, -1.0, 0.0, 0.0, 0.0, 1.0, 1.0, 1.0], dtype=jnp.float32)
        RX = jnp.array([-1.0, 0.0, 1.0, -1.0, 0.0, 1.0, -1.0, 0.0, 1.0], dtype=jnp.float32)

        def conv2d(x, w, b):
            out = jax.lax.conv_general_dilated(x, w, window_strides=(1, 1), padding=((1, 1), (1, 1)), dimension_numbers=('NCHW', 'OIHW', 'NCHW'))
            return out + b[None, :, None, None]

        def group_norm(x, gamma, beta, num_groups, eps=1e-05):
            N, C, H, W = x.shape
            xg = x.reshape(N, num_groups, C // num_groups, H, W)
            mu = xg.mean(axis=(2, 3, 4), keepdims=True)
            var = xg.var(axis=(2, 3, 4), keepdims=True)
            xn = ((xg - mu) * jax.lax.rsqrt(var + eps)).reshape(N, C, H, W)
            return xn * gamma[None, :, None, None] + beta[None, :, None, None]

        def build_offset(tm, tr):
            m00, m01, m10, m11 = (tm[:, 0], tm[:, 1], tm[:, 2], tm[:, 3])
            ry = RY[None, :, None, None]
            rx = RX[None, :, None, None]
            dy = m00[:, None] * ry + m01[:, None] * rx - ry + tr[:, 0:1]
            dx = m10[:, None] * ry + m11[:, None] * rx - rx + tr[:, 1:2]
            return (dy, dx)

        def bilinear_sample(img, py, px):
            N, C, H, W = img.shape
            K = py.shape[1]
            y0f = jnp.floor(py)
            x0f = jnp.floor(px)
            wy1 = py - y0f
            wx1 = px - x0f
            wy0 = 1.0 - wy1
            wx0 = 1.0 - wx1
            y0 = y0f.astype(jnp.int32)
            x0 = x0f.astype(jnp.int32)
            img_flat = img.reshape(N, C, H * W)

            def gather(yi, xi):
                valid = ((yi >= 0) & (yi < H) & (xi >= 0) & (xi < W)).astype(img.dtype)
                idx = jnp.clip(yi, 0, H - 1) * W + jnp.clip(xi, 0, W - 1)
                flat = idx.reshape(N, 1, K * H * W)
                vals = jnp.take_along_axis(img_flat, jnp.broadcast_to(flat, (N, C, K * H * W)), axis=2)
                return vals.reshape(N, C, K, H, W) * valid[:, None]
            v00 = gather(y0, x0)
            v01 = gather(y0, x0 + 1)
            v10 = gather(y0 + 1, x0)
            v11 = gather(y0 + 1, x0 + 1)
            return v00 * (wy0 * wx0)[:, None] + v01 * (wy0 * wx1)[:, None] + v10 * (wy1 * wx0)[:, None] + v11 * (wy1 * wx1)[:, None]

        def deform_conv(x, dy, dx, w, pad=1, dil=1):
            N, C, H, W = x.shape
            k = jnp.arange(9)
            ki = (k // 3).astype(x.dtype)[None, :, None, None]
            kj = (k % 3).astype(x.dtype)[None, :, None, None]
            hh = jnp.arange(H, dtype=x.dtype)[None, None, :, None]
            ww = jnp.arange(W, dtype=x.dtype)[None, None, None, :]
            py = hh - pad + dil * ki + dy
            px = ww - pad + dil * kj + dx
            sampled = bilinear_sample(x, py, px)
            return jnp.einsum('nckhw,ock->nohw', sampled, w.reshape(w.shape[0], C, 9))
        GROUPS = 32
        residual = x
        dy1, dx1 = build_offset(conv2d(x, w_tm1, b_tm1), conv2d(x, w_tr1, b_tr1))
        out = deform_conv(x, dy1, dx1, w_dc1)
        out = jax.nn.relu(group_norm(out, g1, be1, GROUPS))
        dy2, dx2 = build_offset(conv2d(out, w_tm2, b_tm2), conv2d(out, w_tr2, b_tr2))
        out = deform_conv(out, dy2, dx2, w_dc2)
        out = group_norm(out, g2, be2, GROUPS)
        return jax.nn.relu(out + residual)

    def _L1_conv_ref(x, w_theta, w_phi, w_g, w_mask):
        import jax, jax.numpy as jnp
        import numpy as np
        B, C, H, W = (8, 256, 64, 64)
        IC = C // 2
        b, c, h, w = x.shape
        ic = c // 2
        theta = jnp.einsum('oc,bchw->bohw', w_theta, x)
        phi = jnp.einsum('oc,bchw->bohw', w_phi, x)
        g = jnp.einsum('oc,bchw->bohw', w_g, x)
        n = ic * h * w // c
        x_theta = theta.reshape(b, c, n).transpose(0, 2, 1)
        x_phi = phi.reshape(b, c, n)
        x_g = g.reshape(b, c, n).transpose(0, 2, 1)
        attn = jnp.matmul(x_theta, x_phi)
        attn = jax.nn.softmax(attn, axis=1)
        out = jnp.matmul(attn, x_g)
        out = out.transpose(0, 2, 1).reshape(b, ic, h, w)
        mask = jnp.einsum('oc,bchw->bohw', w_mask, out)
        return mask + x

    def _L2_conv_ref(x, w1, b1, g1, be1, w2, b2, g2, be2, w3, b3, g3, be3, g4, be4):
        import jax, jax.numpy as jnp
        import numpy as np
        from jax import lax
        EPS = 1e-05
        P, H_DIM = (32, 4)
        C = 256

        def _bn_nchw(x, g, b):
            m = jnp.mean(x, axis=(0, 2, 3), keepdims=True)
            v = jnp.var(x, axis=(0, 2, 3), keepdims=True)
            return (x - m) * (g[None, :, None, None] / jnp.sqrt(v + EPS)) + b[None, :, None, None]

        def _bn_paths(x, g, b):
            m = jnp.mean(x, axis=(0, 3, 4), keepdims=True)
            v = jnp.var(x, axis=(0, 3, 4), keepdims=True)
            return (x - m) * (g[None, :, :, None, None] / jnp.sqrt(v + EPS)) + b[None, :, :, None, None]
        y = jnp.einsum('bchw,kc->bkhw', x, w1) + b1[None, :, None, None]
        y = jax.nn.relu(_bn_nchw(y, g1, be1))
        y = lax.conv_general_dilated(y, w2, window_strides=(1, 1), padding=[(1, 1), (1, 1)], feature_group_count=P, dimension_numbers=('NCHW', 'OIHW', 'NCHW'))
        y = y + b2[None, :, None, None]
        y = jax.nn.relu(_bn_nchw(y, g2, be2))
        B, _, Hh, Ww = y.shape
        y = y.reshape(B, P, H_DIM, Hh, Ww)
        y = jnp.einsum('bphxy,pch->bpcxy', y, w3) + b3[None, :, :, None, None]
        y = jax.nn.relu(_bn_paths(y, g3, be3))
        s = jnp.sum(y, axis=1) + x
        return _bn_nchw(s, g4, be4)

    def _L3_conv_ref(x, conv_w, conv_b):
        import jax, jax.numpy as jnp
        import numpy as np
        from jax import lax
        ALPHA = 0.1
        B, C, H, W = x.shape
        L = H * W
        xf = x.reshape(B, C, L)
        K = conv_w.shape[-1]
        pad = K // 2
        conv_out = lax.conv_general_dilated(xf, conv_w, window_strides=(1,), padding=[(pad, pad)], dimension_numbers=('NCH', 'OIH', 'NCH'), feature_group_count=C) + conv_b[None, :, None]
        xt = jnp.moveaxis(xf, 2, 0)

        def step(carry, xi):
            e = ALPHA * xi + (1.0 - ALPHA) * carry
            return (e, e)
        _, ema_rest = lax.scan(step, xt[0], xt[1:])
        ema = jnp.concatenate([xt[:1], ema_rest], axis=0)
        ema = jnp.moveaxis(ema, 0, 2)
        out = (conv_out + ema).reshape(B, C, H, W)
        return out + x

    def _gn(v, G=32, eps=1e-5):
        B_, C_, H_, W_ = v.shape
        g = v.reshape(B_, G, C_ // G, H_, W_)
        m = jnp.mean(g, axis=(2, 3, 4), keepdims=True)
        s = jnp.var(g, axis=(2, 3, 4), keepdims=True)
        return ((g - m) / jnp.sqrt(s + eps)).reshape(v.shape)

    def _ln_c(v, eps=1e-6):
        m = jnp.mean(v, axis=1, keepdims=True)
        s = jnp.var(v, axis=1, keepdims=True)
        return (v - m) / jnp.sqrt(s + eps)

    def _ln_t(v, eps=1e-5):
        m = jnp.mean(v, axis=-1, keepdims=True)
        s = jnp.var(v, axis=-1, keepdims=True)
        return (v - m) / jnp.sqrt(s + eps)

    def _to_tokens(v):
        B_, C_, H_, W_ = v.shape
        return v.reshape(B_, C_, H_ * W_).transpose(0, 2, 1)
    def _from_tokens(t, like):
        B_, C_, H_, W_ = like.shape
        return t.transpose(0, 2, 1).reshape(B_, C_, H_, W_)

    x = _L0_conv_ref(x, L0_conv_w_tm1, L0_conv_b_tm1, L0_conv_w_tr1, L0_conv_b_tr1, L0_conv_w_dc1, L0_conv_g1, L0_conv_be1, L0_conv_w_tm2, L0_conv_b_tm2, L0_conv_w_tr2, L0_conv_b_tr2, L0_conv_w_dc2, L0_conv_g2, L0_conv_be2)
    x = _L1_conv_ref(x, L1_conv_w_theta, L1_conv_w_phi, L1_conv_w_g, L1_conv_w_mask)
    x = _L2_conv_ref(x, L2_conv_w1, L2_conv_b1, L2_conv_g1, L2_conv_be1, L2_conv_w2, L2_conv_b2, L2_conv_g2, L2_conv_be2, L2_conv_w3, L2_conv_b3, L2_conv_g3, L2_conv_be3, L2_conv_g4, L2_conv_be4)
    x = _L3_conv_ref(x, L3_conv_conv_w, L3_conv_conv_b)
    return x


_drawn_inputs = setup_inputs


def setup_inputs(seed=0):
    import zlib

    import numpy as np

    out = dict(_drawn_inputs(seed))
    spreads = {'L0_conv_b_tm1': (0.0, 0.1),
     'L0_conv_b_tr1': (0.0, 0.1),
     'L0_conv_g1': (1.0, 0.2),
     'L0_conv_be1': (0.0, 0.1),
     'L0_conv_b_tm2': (0.0, 0.1),
     'L0_conv_b_tr2': (0.0, 0.1),
     'L0_conv_g2': (1.0, 0.2),
     'L0_conv_be2': (0.0, 0.1),
     'L2_conv_g1': (1.0, 0.2),
     'L2_conv_be1': (0.0, 0.1),
     'L2_conv_g2': (1.0, 0.2),
     'L2_conv_be2': (0.0, 0.1),
     'L2_conv_g3': (1.0, 0.2),
     'L2_conv_be3': (0.0, 0.1),
     'L2_conv_g4': (1.0, 0.2),
     'L2_conv_be4': (0.0, 0.1)}
    factors = {}
    for name, (base, spread) in spreads.items():
        noise = np.random.default_rng([zlib.crc32(name.encode()), seed]).standard_normal(out[name].shape)
        drawn = base * np.exp(spread * noise) if base else spread * noise
        out[name] = jnp.asarray(drawn.astype(out[name].dtype))
    for name, factor in factors.items():
        out[name] = (out[name] * factor).astype(out[name].dtype)
    return out
```

```python
from contextlib import ExitStack

import numpy as np

import concourse.bass as bass
from concourse import mybir

ALU = mybir.AluOpType
ACT = mybir.ActivationFunctionType
F32 = mybir.dt.float32
I32 = mybir.dt.int32
BF16 = mybir.dt.bfloat16

B, C, H, W = 4, 256, 64, 64
P = 128
CH = C // P
PIX = H * W
TAPS = 9
PITCH = W + 2
CELLS = PITCH * (H + 2)
PATCH = 4 * C
NTILE = PIX // P
GN_GROUP = 8
EPS = 1e-5
NOFF = 6
NPART = TAPS * NOFF
NPOS = 2 * TAPS

GROUP_TILES = 2
GROUP = GROUP_TILES * P
NGROUP = PIX // GROUP
GS = GROUP_TILES * TAPS
NS = NTILE * TAPS
SRING = 6
TRING = 3
LAG = 3


def order_of_phases():
    seq = [("P", 0, 0), ("P", 0, 1)]
    for b in range(B):
        seq += [("G", 0, b), ("P", 1, b)]
        if b + 2 < B:
            seq.append(("P", 0, b + 2))
    for b in range(B):
        seq += [("G", 1, b), ("F", 1, b)]
    return seq


def deformable_block(nc, x, wdc, woff, boff, gamma_beta, table, x1, consts):
    seq = order_of_phases()
    ordinal = {}
    for kind in "PGF":
        for n, ph in enumerate([ph for ph in seq if ph[0] == kind]):
            ordinal[ph] = n
    loads = {ph: n for n, ph in enumerate([ph for ph in seq if ph[:2] == ("P", 0) or ph[0] == "F"])}

    def before(ph, kind):
        return sum(q[0] == kind for q in seq[:seq.index(ph)])

    with ExitStack() as ctx:
        def sb(name, shape, dt=F32):
            return ctx.enter_context(nc.sbuf_tensor(name, shape, dt))

        def sem(name):
            return ctx.enter_context(nc.semaphore(name))

        ident = sb("ident", [P, P])
        gavg = sb("gavg", [P, P])
        sel = sb("sel", [P, NPOS])
        posbase = sb("posbase", [P, NTILE, NPOS])
        wdc_sb = sb("wdc_sb", [P, CH, TAPS, C])
        woff_sb = sb("woff_sb", [P, 2, CH, NPART])
        boff_sb = sb("boff_sb", [NPART, 2])
        gb_sb = sb("gb_sb", [P, 2, 2, CH])
        eps_sb = sb("eps_sb", [P, 1])
        xin = sb("xin", [P, CH, PIX])
        img = sb("img", [P, CH, PIX])
        turned = sb("turned", [P, 2, 4, C])
        pos = sb("pos", [P, NTILE, NPOS])
        posi = sb("posi", [P, NTILE, NPOS], I32)
        low = sb("low", [P, NTILE, NPOS])
        over = sb("over", [P, NTILE, NPOS])
        idxf = sb("idxf", [P, NTILE, TAPS])
        idx = sb("idx", [P, B, NTILE, TAPS], I32)
        wgt = sb("wgt", [P, B, NTILE, TAPS, 4])
        patch = sb("patch", [P, TAPS, PATCH])
        idx_now = sb("idx_now", [P, 2, TAPS], I32)
        wgt_now = sb("wgt_now", [P, 2, TAPS, 4])
        blend = sb("blend", [P, SRING, C])
        cols = sb("cols", [P, 2, CH, TAPS, GROUP])
        cols_flat = cols[:, :, :, :, :].rearrange("p a h k q -> p a (h k q)")
        part = cols_flat[:, 0, :]
        aligned = cols_flat[:, 1, :]
        stats = sb("stats", [P, CH, NGROUP, 6])
        mv = sb("mv", [P, CH, 2])
        mom = sb("mom", [P, 2, CH])
        gstat = sb("gstat", [P, 2, CH])
        small = sb("small", [P, 4, CH])
        scale = sb("scale", [P, CH])
        shift = sb("shift", [P, CH])

        bank = [ctx.enter_context(nc.psum_tensor(f"bank{i}", [P, 512], F32)) for i in range(8)]
        tbank = bank[0:TRING]
        obank = bank[3:5]
        partbank = bank[5:7]
        turnbank = [bank[7], bank[3]]
        posbank = bank[0:2]
        gnbank = bank[2]

        s_const = sem("const_loaded")
        s_w = sem("wdc_loaded")
        s_border = sem("table_border_written")
        s_x = sem("x_loaded")
        s_tab = [sem(f"table_written{i}") for i in range(2)]
        s_aln = sem("partials_aligned")
        s_gat = [sem(f"patch_gathered{k}") for k in range(TAPS)]
        s_out = sem("x1_stored")
        s_zero = sem("part_border_zeroed")
        s_pmm = sem("part_product")
        s_pev = sem("part_emptied")
        s_tmm = sem("turned_product")
        s_tev = sem("turned_emptied")
        s_posmm = sem("pos_product")
        s_dv = sem("vector_step")
        s_idx = sem("indices_ready")
        s_ic = sem("idx_copied")
        s_wc = sem("wgt_copied")
        s_mul = sem("corner0_weighted")
        s_st = sem("corner_added")
        s_blend = sem("blend_ready")
        s_tr = sem("sample_transposed")
        s_cols = sem("columns_ready")
        s_cv = sem("conv_product")
        s_oev = sem("conv_emptied")
        s_agg = sem("channel_moments")
        s_gn = sem("group_moments")
        s_var = sem("variance_ready")
        s_std = sem("deviation_ready")
        s_sc = sem("scale_ready")
        s_norm = sem("image_normalised")
        s_res = sem("residual_added")

        NCONST = 9
        block = ctx.enter_context(nc.Block())

        @block.sync
        def _(sp):
            zero = cols_flat
            o = 0
            sp.dma_start(ident[:, :], consts[:, 0:P]).then_inc(s_const, 16)
            sp.dma_start(gavg[:, :], consts[:, P:2 * P]).then_inc(s_const, 16)
            sp.dma_start(sel[:, :], consts[:, 2 * P:2 * P + NPOS]).then_inc(s_const, 16)
            sp.dma_start(posbase[:, :, :], consts[:, 2 * P + NPOS:2 * P + NPOS + NTILE * NPOS].rearrange(
                "p (t n) -> p t n", t=NTILE)).then_inc(s_const, 16)
            for l in range(2):
                sp.dma_start(woff_sb[:, l, :, :], woff[l].rearrange("(h p) m -> p h m", p=P)).then_inc(s_const, 16)
            sp.dma_start(gb_sb[:, :, :, :].rearrange("p l g h -> p (l g h)"), gamma_beta).then_inc(s_const, 16)

            def load_x(ph):
                n = loads[ph]
                if n > 0:
                    prev = [q for q, m in loads.items() if m == n - 1][0]
                    if prev[0] == "P":
                        sp.wait_ge(s_tmm, 16 * (ordinal[prev] + 1))
                    else:
                        sp.wait_ge(s_res, 4 * (ordinal[prev] + 1))
                sp.dma_start(xin[:, :, :], x[ph[2]].rearrange("(h p) n -> p h n", p=P)).then_inc(s_x, 16)

            load_x(seq[0])
            sp.wait_ge(s_zero, 2)
            for l in range(2):
                sp.dma_start(boff_sb[4 * NOFF:5 * NOFF, l:l + 1], boff[l]).then_inc(s_const, 16)
            for b in range(B):
                t = table[b].rearrange("(y x) n -> y x n", y=H + 2)
                sp.dma_start(t[:, W + 1, :], zero[0:H + 2, 0, 0:PATCH]).then_inc(s_border, 16)
                for col, side in ((0, 0), (W, 1)):
                    sp.dma_start(t[:, col, :].rearrange("y (r c n) -> y r c n", r=2, c=2)[:, :, side, :],
                                 zero[0:H + 2, 0, 0:2 * C].rearrange("p (r n) -> p r n", r=2)).then_inc(s_border, 16)
                for row, r in ((0, 0), (H, 1), (H + 1, 0), (H + 1, 1)):
                    for side in range(2):
                        lo = (2 * r + side) * C
                        sp.dma_start(t[row, 1 - side:1 - side + W, lo:lo + C], zero[0:W, 0, 0:C]).then_inc(s_border, 16)
            load_done = {seq[0]}

            for ph in seq:
                kind, l, b = ph
                if kind == "P":
                    n = ordinal[ph]
                    t = table[b].rearrange("(y x) n -> y x n", y=H + 2)
                    if ph in loads and ph not in load_done:
                        load_x(ph)
                        load_done.add(ph)
                    sp.wait_ge(s_pev, 8 * (n + 1))
                    if before(ph, "G"):
                        sp.wait_ge(s_cv, 2 * NGROUP * before(ph, "G"))
                    if n > 0:
                        sp.wait_ge(s_posmm, 2 * n)
                    for k in range(TAPS):
                        rows = slice(NOFF * k, NOFF * k + NOFF)
                        sp.dma_start(aligned[rows, 0:PIX].rearrange("m (y x) -> m y x", x=W),
                                     part[rows, 0:CELLS].rearrange("m (y x) -> m y x", x=PITCH)[
                                         :, k // 3:k // 3 + H, k % 3:k % 3 + W]).then_inc(s_aln, 16)
                    for bt in range(8):
                        sp.wait_ge(s_tev, 16 * n + 2 * bt + 2)
                        for hp in range(2):
                            y = 8 * bt + hp
                            for r in range(2):
                                for c in range(2):
                                    sp.dma_start(
                                        t[y + 1 - r:y + 1 - r + 7:2, 1 - c:1 - c + W,
                                          (2 * r + c) * C:(2 * r + c + 1) * C].rearrange("y x n -> x y n"),
                                        turned[64 * hp:64 * hp + 64, bt % 2, :, :]).then_inc(s_tab[bt % 2], 16)
                if kind == "G":
                    n = ordinal[ph]
                    if b == 0:
                        if l:
                            sp.wait_ge(s_cv, 2 * NGROUP * n)
                        sp.dma_start(wdc_sb[:, :, :, :].rearrange("p h k o -> p h (k o)"),
                                     wdc[l].rearrange("(h p) m -> p h m", p=P)).then_inc(s_w, 16)
                    nxt = ("F", 1, b)
                    if l:
                        load_x(nxt)
                if kind == "F":
                    for q in range(4):
                        sp.wait_ge(s_norm, 4 * before(ph, "G") - 4 + q + 1)
                        h, at = q // 2, (q % 2) * (PIX // 2)
                        sp.dma_start(x1[b, h * P:(h + 1) * P, at:at + PIX // 2],
                                     img[:, h, at:at + PIX // 2]).then_inc(s_out, 16)
            sp.wait_ge(s_out, 16 * 4 * B)

        @block.gpsimd
        def _(pool):
            pool.wait_ge(s_border, 16 * 44)

            def tile(ph, t, tt, skip):
                q, b = ordinal[ph], ph[2]
                nc.gpsimd.tensor_copy(idx_now[:, tt, :], idx[:, b, t, :] if isinstance(t, int) else
                                      idx[:, b, bass.ds(t, 1), :].rearrange("p a k -> p (a k)")).then_inc(s_ic, 1)
                pool.wait_ge(s_ic, NTILE * q + t + 1)
                pool.nop(nofuse=True)
                for k in range(TAPS):
                    if not skip:
                        pool.wait_ge(s_blend, NS * q + 9 * t + k - 8)
                        pool.nop(nofuse=True)
                    nc.gpsimd.indirect_dma_start(
                        out=patch[:, k, :], out_offset=None, in_=table[ph[2]],
                        in_offset=bass.IndirectOffsetOnAxis(ap=idx_now[:, tt, k:k + 1], axis=0),
                    ).then_inc(s_gat[k], 16)

            for ph in seq:
                if ph[0] != "G":
                    continue
                q = ordinal[ph]
                p = ordinal[("P",) + ph[1:]]
                pool.wait_ge(s_idx, p + 1)
                for i in range(2):
                    pool.wait_ge(s_tab[i], 16 * 8 * 4 * (p + 1))
                tile(ph, 0, 0, q == 0)
                tile(ph, 1, 1, False)
                with pool.Fori(1, NTILE // 2) as i:
                    for tt in range(2):
                        tile(ph, 2 * i + tt, tt, False)

        @block.scalar
        def _(act):
            act.wait_ge(s_const, 16 * NCONST)

            def weigh(ph, it, j):
                q = ordinal[ph]
                tt, k = (j // TAPS) % 2, j % TAPS
                if k == 0:
                    act.wait_ge(s_wc, NTILE * q + 4 * it + j // TAPS + 1)
                act.wait_ge(s_gat[k], 16 * (NTILE * q + 4 * it + j // TAPS + 1))
                if not (q == 0 and isinstance(it, int) and it == 0 and j < SRING):
                    act.wait_ge(s_tr, NS * q + 36 * it + j + 1 - SRING)
                nc.scalar.activation(blend[:, j % SRING, :], patch[:, k, 0:C], ACT.Copy,
                                     scale=wgt_now[:, tt, k, 0:1]).then_inc(s_mul, 1)

            def empty(ph, it, j):
                q = ordinal[ph]
                act.wait_ge(s_tr, NS * q + 36 * it + j + 1)
                e, tt, k = j // GS, (j // TAPS) % 2, j % TAPS
                if j % GS == 0:
                    if not (isinstance(it, int) and it == 0):
                        act.wait_ge(s_cv, 2 * (NGROUP * q + 2 * it + e - 1))
                nc.scalar.activation(cols[:, e, :, k, tt * P:(tt + 1) * P],
                                     tbank[j % TRING][:, 0:C].rearrange("p (h n) -> p h n", h=CH),
                                     ACT.Copy).then_inc(s_cols, 1)

            def keep(ph, g, oh):
                q = ordinal[ph]
                act.wait_ge(s_cv, 2 * (NGROUP * q + g) + oh + 1)
                nc.scalar.activation(img[:, oh, bass.ds(GROUP * g, GROUP)], obank[oh][:, 0:GROUP],
                                     ACT.Copy).then_inc(s_oev, 1)

            def iteration(ph, it, first):
                for j in range(2 * GS):
                    e, jj = j // GS, j % GS
                    weigh(ph, it, j)
                    if j >= LAG:
                        empty(ph, it, j - LAG)
                    elif not first:
                        empty(ph, it - 1, 2 * GS + j - LAG)
                    if jj == 3 and not first:
                        keep(ph, 2 * it + e - 2, 1)
                    if jj == 16 and not (first and e == 0):
                        if first and ph[1] and ph[2]:
                            act.wait_ge(s_out, 16 * 4 * ph[2])
                        keep(ph, 2 * it + e - 1, 0)

            for ph in seq:
                kind, l, b = ph
                if kind == "P":
                    n = ordinal[ph]
                    act.wait_ge(s_zero, 5 + 3 * n)
                    if l == 1:
                        q = before(ph, "G") - 1
                        act.wait_ge(s_sc, q + 1)
                        for c in range(4):
                            h, at = c // 2, (c % 2) * (PIX // 2)
                            nc.scalar.activation(img[:, h, at:at + PIX // 2], img[:, h, at:at + PIX // 2], ACT.Relu,
                                                 scale=scale[:, h:h + 1], bias=shift[:, h:h + 1]).then_inc(s_norm, 1)
                    rows = part[0:NPART, 0:CELLS].rearrange("m (y x) -> m y x", x=PITCH)
                    for c in range(8):
                        act.wait_ge(s_pmm, 8 * n + c + 1)
                        nc.scalar.activation(rows[:, 8 * c + 1:8 * c + 9, 1:W + 1],
                                             partbank[c % 2][0:NPART, :].rearrange("m (y x) -> m y x", x=W),
                                             ACT.Identity, bias=boff_sb[:, l:l + 1]).then_inc(s_pev, 1)
                if kind == "G":
                    q = ordinal[ph]
                    act.wait_ge(s_aln, 16 * TAPS * before(ph, "P"))
                    act.wait_ge(s_posmm, 2 * before(ph, "P"))
                    iteration(ph, 0, True)
                    with act.Fori(1, NGROUP // 2) as it:
                        iteration(ph, it, False)
                    last = NGROUP // 2 - 1
                    for j in range(2 * GS - LAG, 2 * GS):
                        empty(ph, last, j)
                    keep(ph, NGROUP - 2, 1)
                    keep(ph, NGROUP - 1, 0)
                    keep(ph, NGROUP - 1, 1)
                    act.wait_ge(s_var, q + 1)
                    nc.scalar.activation(small[:, 1, :], small[:, 0, :], ACT.Sqrt,
                                         bias=eps_sb[:, 0:1]).then_inc(s_std, 1)
                if kind == "F":
                    for c in range(4):
                        h, at = c // 2, (c % 2) * (PIX // 2)
                        act.wait_ge(s_res, 4 * ordinal[ph] + c + 1)
                        nc.scalar.activation(img[:, h, at:at + PIX // 2], img[:, h, at:at + PIX // 2], ACT.Relu,
                                             bias=shift[:, h:h + 1]).then_inc(s_norm, 1)

        @block.tensor
        def _(pe):
            pe.wait_ge(s_const, 16 * NCONST)

            def turn(ph, it, j):
                q = ordinal[ph]
                pe.wait_ge(s_blend, NS * q + 36 * it + j + 1)
                if not (q == 0 and isinstance(it, int) and it == 0 and j < TRING):
                    pe.wait_ge(s_cols, NS * q + 36 * it + j + 1 - TRING)
                for h in range(CH):
                    mm = nc.tensor.transpose(tbank[j % TRING][:, h * P:(h + 1) * P],
                                             blend[:, j % SRING, h * P:(h + 1) * P], ident[:, :])
                mm.then_inc(s_tr, 1)

            def conv(ph, g, e, oh, steps):
                q = ordinal[ph]
                for s in steps:
                    k, h = s // CH, s % CH
                    if s == 0:
                        if oh == 0:
                            pe.wait_ge(s_cols, NS * q + GS * (g + 1))
                        if not (q == 0 and isinstance(g, int) and g == 0):
                            pe.wait_ge(s_oev, 2 * (NGROUP * q + g - 1) + oh + 1)
                    mm = nc.tensor.matmul(obank[oh][:, 0:GROUP], wdc_sb[:, h, k, oh * P:(oh + 1) * P],
                                          cols[:, e, h, k, :], start=(s == 0), stop=(s == GS - 1))
                    if s == GS - 1:
                        mm.then_inc(s_cv, 1)

            def iteration(ph, it, first):
                for j in range(2 * GS):
                    e, jj = j // GS, j % GS
                    turn(ph, it, j)
                    if 5 <= jj < 17 and not (first and e == 0):
                        oh = (jj - 5) // 6
                        s0 = 3 * ((jj - 5) % 6)
                        conv(ph, 2 * it + e - 1, 1 - e, oh, range(s0, s0 + 3))

            for ph in seq:
                kind, l, b = ph
                if kind == "P":
                    n = ordinal[ph]
                    src = img if l else xin
                    if l:
                        pe.wait_ge(s_norm, 4 * before(ph, "G"))
                    else:
                        pe.wait_ge(s_x, 16 * (loads[ph] + 1))
                    if before(ph, "G"):
                        pe.wait_ge(s_oev, 2 * NGROUP * before(ph, "G"))
                    for c in range(8):
                        if n or c >= 2:
                            pe.wait_ge(s_pev, 8 * n + c - 1)
                        for h in range(CH):
                            mm = nc.tensor.matmul(partbank[c % 2][0:NPART, :], woff_sb[:, l, h, :],
                                                  src[:, h, 512 * c:512 * c + 512], start=(h == 0), stop=(h == CH - 1))
                        mm.then_inc(s_pmm, 1)
                    for c in range(16):
                        if n or c >= 2:
                            pe.wait_ge(s_tev, 16 * n + c - 1)
                        for i in range(4):
                            t, h = 2 * c + i // 2, i % 2
                            mm = nc.tensor.transpose(turnbank[c % 2][:, P * i:P * i + P],
                                                     src[:, h, P * t:P * t + P], ident[:, :])
                        mm.then_inc(s_tmm, 1)
                    pe.wait_ge(s_aln, 16 * TAPS * (n + 1))
                    if n:
                        pe.wait_ge(s_idx, n)
                    for t in range(NTILE):
                        mm = nc.tensor.matmul(posbank[t // 16][:, (t % 16) * NPOS:(t % 16 + 1) * NPOS],
                                              aligned[0:NPART, P * t:P * t + P], sel[0:NPART, :], start=True, stop=True)
                        if t % 16 == 15:
                            mm.then_inc(s_posmm, 1)
                if kind == "G":
                    q = ordinal[ph]
                    if b == 0:
                        pe.wait_ge(s_w, 16 * (l + 1))
                    pe.wait_ge(s_idx, before(ph, "P"))
                    pe.wait_ge(s_tev, 16 * before(ph, "P"))
                    iteration(ph, 0, True)
                    with pe.Fori(1, NGROUP // 2) as it:
                        iteration(ph, it, False)
                    for oh in range(2):
                        conv(ph, NGROUP - 1, 1, oh, range(GS))
                    pe.wait_ge(s_agg, q + 1)
                    pe.wait_ge(s_cols, NS * (q + 1))
                    nc.tensor.matmul(gnbank[:, 0:4], gavg[:, :], mom[:, :, :].rearrange("p a h -> p (a h)"),
                                     start=True, stop=True).then_inc(s_gn, 1)

        @block.vector
        def _(dve):
            steps = [0]

            def link(ins):
                steps[0] += 1
                ins.then_inc(s_dv, 1)
                dve.wait_ge(s_dv, steps[0])

            nc.vector.memset(cols_flat[:, 0, 0:4 * PATCH], 0.0).then_inc(s_zero, 1)
            nc.vector.memset(boff_sb[:, :], 0.0).then_inc(s_zero, 1)
            link(nc.vector.memset(eps_sb[:, :], EPS))
            dve.wait_ge(s_const, 16 * NCONST)
            dve.wait_ge(s_border, 16 * 44)

            def iteration(ph, it, first):
                q = ordinal[ph]
                base = 2 * NS * q
                for j in range(0, 2 * GS, 2):
                    for i in (j, j + 1):
                        if i % TAPS == 0:
                            tl = i // TAPS
                            t = 4 * it + tl
                            w = wgt[:, ph[2], t, :, :] if isinstance(t, int) else wgt[:, ph[2], bass.ds(t, 1), :, :].rearrange(
                                "p a k c -> p (a k) c")
                            nc.vector.tensor_copy(wgt_now[:, tl % 2, :, :], w).then_inc(s_wc, 1)
                            dve.wait_ge(s_wc, NTILE * q + t + 1)
                    for corner in (1, 2, 3):
                        for i in (j, j + 1):
                            k, tt = i % TAPS, (i // TAPS) % 2
                            if corner == 1:
                                dve.wait_ge(s_mul, NS * q + 36 * it + i + 1)
                            else:
                                dve.wait_ge(s_st, base + 72 * it + 2 * j + (i - j) + 1 + 2 * (corner - 2))
                            nc.vector.scalar_tensor_tensor(
                                out=blend[:, i % SRING, :], in0=patch[:, k, corner * C:(corner + 1) * C],
                                scalar=wgt_now[:, tt, k, corner:corner + 1], in1=blend[:, i % SRING, :],
                                op0=ALU.mult, op1=ALU.add).then_inc(s_blend if corner == 3 else s_st, 1)
                    e, jj = j // GS, j % GS
                    if jj == 6 and not first:
                        moments(ph, 2 * it + e - 2, 1)
                    if jj == 16 and not (first and e == 0):
                        moments(ph, 2 * it + e - 1, 0)

            def moments(ph, g, oh):
                dve.wait_ge(s_oev, 2 * (NGROUP * ordinal[ph] + g) + oh + 1)
                out = stats[:, oh, g, :] if isinstance(g, int) else stats[:, oh, bass.ds(g, 1), :].rearrange("p a s -> p (a s)")
                nc.vector.bn_stats(out, img[:, oh, bass.ds(GROUP * g, GROUP)])

            for ph in seq:
                kind, l, b = ph
                if kind == "P":
                    n = ordinal[ph]
                    if before(ph, "G"):
                        dve.wait_ge(s_cv, 2 * NGROUP * before(ph, "G"))
                    if n:
                        dve.wait_ge(s_aln, 16 * TAPS * n)
                    nc.vector.memset(part[0:NPART, 0:PITCH + 1], 0.0).then_inc(s_zero, 1)
                    pairs = part[0:NPART, PITCH + W + 1:PITCH + W + 1 + H * PITCH].rearrange("m (y x) -> m y x", x=PITCH)
                    nc.vector.memset(pairs[:, :, 0:2], 0.0).then_inc(s_zero, 1)
                    nc.vector.memset(part[0:NPART, CELLS - PITCH + 1:CELLS], 0.0).then_inc(s_zero, 1)
                    for c in range(16):
                        dve.wait_ge(s_tmm, 16 * n + c + 1)
                        bt = c // 2
                        if n or bt >= 2:
                            dve.wait_ge(s_tab[bt % 2], 16 * 8 * (4 * n + bt // 2))
                        nc.vector.tensor_copy(
                            turned[:, bt % 2, 2 * (c % 2):2 * (c % 2) + 2, :].rearrange("p a n -> p (a n)"),
                            turnbank[c % 2][:, :]).then_inc(s_tev, 1)
                    half = NTILE // 2
                    for i in range(2):
                        dve.wait_ge(s_posmm, 2 * n + i + 1)
                        ins = nc.vector.tensor_tensor(
                            pos[:, half * i:half * i + half, :].rearrange("p t n -> p (t n)"),
                            posbank[i][:, 0:half * NPOS],
                            posbase[:, half * i:half * i + half, :].rearrange("p t n -> p (t n)"), ALU.add)
                    link(ins)
                    flat = lambda a: a[:, :, :].rearrange("p t n -> p (t n)")
                    link(nc.vector.tensor_scalar(flat(pos), flat(pos), -1.0, float(H), ALU.max, ALU.min))
                    link(nc.vector.tensor_copy(flat(posi), flat(pos)))
                    link(nc.vector.tensor_copy(flat(low), flat(posi)))
                    link(nc.vector.tensor_tensor(flat(over), flat(low), flat(pos), ALU.is_gt))
                    link(nc.vector.tensor_tensor(flat(low), flat(low), flat(over), ALU.subtract))
                    link(nc.vector.tensor_tensor(flat(pos), flat(pos), flat(low), ALU.subtract))
                    link(nc.vector.tensor_scalar(flat(over), flat(pos), -1.0, 1.0, ALU.mult, ALU.add))
                    for r, wy in enumerate((over, pos)):
                        for c, wx in enumerate((over, pos)):
                            nc.vector.tensor_tensor(wgt[:, b, :, :, 2 * r + c], wy[:, :, 0:TAPS],
                                                    wx[:, :, TAPS:NPOS], ALU.mult)
                    link(nc.vector.scalar_tensor_tensor(out=idxf[:, :, :], in0=low[:, :, 0:TAPS], scalar=float(PITCH),
                                                        in1=low[:, :, TAPS:NPOS], op0=ALU.mult, op1=ALU.add))
                    nc.vector.tensor_scalar(idx[:, b, :, :], idxf[:, :, :], float(PITCH + 1), None,
                                            ALU.add).then_inc(s_idx, 1)
                    dve.wait_ge(s_idx, n + 1)
                if kind == "G":
                    q = ordinal[ph]
                    iteration(ph, 0, True)
                    with dve.Fori(1, NGROUP // 2) as it:
                        iteration(ph, it, False)
                    moments(ph, NGROUP - 2, 1)
                    moments(ph, NGROUP - 1, 0)
                    moments(ph, NGROUP - 1, 1)
                    link(nc.vector.memset(small[:, 3, :], 0.0))
                    for h in range(CH):
                        ins = nc.vector.bn_aggr(mv[:, h, :], stats[:, h, :, :].rearrange("p g s -> p (g s)"))
                    link(ins)
                    nc.vector.tensor_copy(mom[:, 0, :], mv[:, :, 0])
                    link(nc.vector.tensor_tensor(small[:, 2, :], mv[:, :, 0], mv[:, :, 0], ALU.mult))
                    nc.vector.tensor_tensor(mom[:, 1, :], small[:, 2, :], mv[:, :, 1], ALU.add).then_inc(s_agg, 1)
                    dve.wait_ge(s_gn, q + 1)
                    link(nc.vector.tensor_copy(gstat[:, :, :].rearrange("p a h -> p (a h)"), gnbank[:, 0:4]))
                    link(nc.vector.tensor_tensor(small[:, 2, :], gstat[:, 0, :], gstat[:, 0, :], ALU.mult))
                    nc.vector.tensor_tensor(small[:, 0, :], gstat[:, 1, :], small[:, 2, :],
                                            ALU.subtract).then_inc(s_var, 1)
                    dve.wait_ge(s_std, q + 1)
                    link(nc.vector.reciprocal(small[:, 2, :], small[:, 1, :]))
                    link(nc.vector.tensor_tensor(scale[:, :], small[:, 2, :], gb_sb[:, l, 0, :], ALU.mult))
                    link(nc.vector.tensor_tensor(small[:, 3, :], gstat[:, 0, :], scale[:, :], ALU.mult))
                    nc.vector.tensor_tensor(shift[:, :], gb_sb[:, l, 1, :], small[:, 3, :],
                                            ALU.subtract).then_inc(s_sc, 1)
                if kind == "F":
                    dve.wait_ge(s_x, 16 * (loads[ph] + 1))
                    dve.wait_ge(s_sc, before(ph, "G"))
                    for c in range(4):
                        h, at = c // 2, (c % 2) * (PIX // 2)
                        nc.vector.scalar_tensor_tensor(
                            out=img[:, h, at:at + PIX // 2], in0=img[:, h, at:at + PIX // 2], scalar=scale[:, h:h + 1],
                            in1=xin[:, h, at:at + PIX // 2], op0=ALU.mult, op1=ALU.add).then_inc(s_res, 1)
IC = C // 2
NKEY = PIX // 2
JT = NKEY // P
BLK = 4
NBLK = JT // BLK
CHUNK = 512
NCH = PIX // CHUNK
NIC = NKEY // CHUNK
AX_X = mybir.AxisListType.X


def attention_block(nc, x1, wproj, wmask, x2):
    with ExitStack() as ctx:
        def sb(name, shape, dt=F32):
            return ctx.enter_context(nc.sbuf_tensor(name, shape, dt))

        def sem(name):
            return ctx.enter_context(nc.semaphore(name))

        proj_sb = sb("proj_sb", [P, CH, 3 * IC])
        mask_sb = sb("mask_sb", [P, C])
        xa = sb("xa", [P, 2, CH, PIX])
        theta = sb("theta", [P, PIX])
        phi = sb("phi", [P, PIX])
        gt = sb("gt", [P, 2, JT, IC])
        gs = sb("gs", [P, 2, BLK, 2, IC])
        ex = sb("ex", [P, 2, BLK, NKEY])
        att = sb("att", [P, PIX])
        mx = sb("mx", [P, 2, NIC])
        nmx = sb("nmx", [P, 2])
        rs = sb("rs", [P, 2])
        rr = sb("rr", [P, 2])

        lbank = ctx.enter_context(nc.psum_tensor("lbank", [P, NKEY], F32))
        vbank = [ctx.enter_context(nc.psum_tensor(f"vbank{i}", [P, CHUNK], F32)) for i in range(2)]
        mbank = [ctx.enter_context(nc.psum_tensor(f"mbank{i}", [P, CHUNK], F32)) for i in range(2)]

        s_w = sem("a_weights_loaded")
        s_x = [sem(f"a_x_loaded{i}") for i in range(2)]
        s_st = [sem(f"a_stored{i}") for i in range(2)]
        s_mm = sem("a_product")
        s_ma = sem("a_projection_kept")
        s_md = sem("a_gt_kept")
        s_mo = sem("a_mask_added")
        s_lg = sem("a_logits")
        s_bm = sem("a_bank_max")
        s_mx = sem("a_max_ready")
        s_ex = sem("a_exp_ready")
        s_rr = sem("a_reciprocal")
        s_gs = sem("a_gt_scaled")
        s_pv = sem("a_pv_product")
        s_pa = sem("a_pv_added")
        FILLS = 2 * NCH + 2 * JT // 4 + 2 * NCH
        block = ctx.enter_context(nc.Block())

        @block.sync
        def _(sp):
            sp.dma_start(proj_sb[:, :, :], wproj.rearrange("(h p) m -> p h m", p=P)).then_inc(s_w, 16)
            sp.dma_start(mask_sb[:, :], wmask).then_inc(s_w, 16)

            def load(b):
                if b >= 2:
                    sp.wait_ge(s_st[b % 2], 32 * (b // 2))
                sp.dma_start(xa[:, b % 2, :, :], x1[b].rearrange("(h p) n -> p h n", p=P)).then_inc(s_x[b % 2], 16)

            load(0)
            load(1)
            for b in range(B):
                for h in range(CH):
                    sp.wait_ge(s_mo, 2 * NCH * b + NCH * (h + 1))
                    sp.dma_start(x2[h * P:(h + 1) * P, PIX * b:PIX * b + PIX], xa[:, b % 2, h, :]).then_inc(s_st[b % 2], 16)
                if b + 2 < B:
                    load(b + 2)
            for i in range(2):
                sp.wait_ge(s_st[i], 16 * B)

        @block.tensor
        def _(pe):
            pe.wait_ge(s_w, 32)

            def bank(b, n):
                m = n - 2 if n >= 2 else n - 2 + FILLS
                bb = b if n >= 2 else b - 1
                if bb < 0:
                    return
                if m < 2 * NCH:
                    pe.wait_ge(s_ma, 2 * NCH * bb + m + 1)
                elif m < FILLS - 2 * NCH:
                    pe.wait_ge(s_md, JT // 2 * bb + m - 2 * NCH + 1)
                else:
                    pe.wait_ge(s_mo, 2 * NCH * bb + m - (FILLS - 2 * NCH) + 1)

            def project(b):
                x = xa[:, b % 2, :, :]
                pe.wait_ge(s_x[b % 2], 16 * (b // 2 + 1))
                n = 0
                for w in range(2):
                    for c in range(NCH):
                        bank(b, n)
                        for h in range(CH):
                            mm = nc.tensor.matmul(mbank[n % 2][:, :], proj_sb[:, h, w * IC:(w + 1) * IC],
                                                  x[:, h, CHUNK * c:CHUNK * c + CHUNK], start=(h == 0), stop=(h == 1))
                        mm.then_inc(s_mm, 1)
                        n += 1
                for t in range(0, 2 * JT, 4):
                    bank(b, n)
                    for i in range(4):
                        for h in range(CH):
                            mm = nc.tensor.matmul(mbank[n % 2][:, IC * i:IC * i + IC], x[:, h, P * (t + i):P * (t + i) + P],
                                                  proj_sb[:, h, 2 * IC:3 * IC], start=(h == 0), stop=(h == 1))
                    mm.then_inc(s_mm, 1)
                    n += 1

            def logits(b, j):
                for c in range(NIC):
                    if b or j:
                        pe.wait_ge(s_ex, JT * b + j)
                    for h in range(2):
                        mm = nc.tensor.matmul(lbank[:, CHUNK * c:CHUNK * c + CHUNK],
                                              phi[:, NKEY * h + P * j:NKEY * h + P * j + P],
                                              theta[:, NKEY * h + CHUNK * c:NKEY * h + CHUNK * c + CHUNK],
                                              start=(h == 0), stop=(h == 1))
                    mm.then_inc(s_lg, 1)

            def pv(b, k, u):
                h, c = u // NIC, u % NIC
                n = 8 * (NBLK * b + k) + u
                pe.wait_ge(s_gs, JT * b + BLK * (k + 1))
                if n >= 2:
                    pe.wait_ge(s_pa, n - 1)
                for i in range(BLK):
                    mm = nc.tensor.matmul(vbank[n % 2][:, :], gs[:, k % 2, i, h, :], ex[:, k % 2, i, CHUNK * c:CHUNK * c + CHUNK],
                                          start=(i == 0), stop=(i == BLK - 1))
                mm.then_inc(s_pv, 1)

            for b in range(B):
                project(b)
                pe.wait_ge(s_ma, 2 * NCH * (b + 1))
                for j in range(JT):
                    logits(b, j)
                    if j >= BLK:
                        pv(b, j // BLK - 1, 2 * (j % BLK))
                        pv(b, j // BLK - 1, 2 * (j % BLK) + 1)
                for u in range(8):
                    pv(b, NBLK - 1, u)
                pe.wait_ge(s_pa, 8 * NBLK * (b + 1))
                for oh in range(CH):
                    for c in range(NCH):
                        n = FILLS - 2 * NCH + oh * NCH + c
                        bank(b, n)
                        nc.tensor.matmul(mbank[n % 2][:, :], mask_sb[:, oh * P:(oh + 1) * P], att[:, CHUNK * c:CHUNK * c + CHUNK],
                                         start=True, stop=True).then_inc(s_mm, 1)

        @block.scalar
        def _(act):
            for b in range(B):
                for n in range(2 * NCH):
                    act.wait_ge(s_mm, FILLS * b + n + 1)
                    if b and n == 0:
                        act.wait_ge(s_lg, NIC * JT * b)
                    dst = (theta, phi)[n // NCH]
                    nc.scalar.activation(dst[:, CHUNK * (n % NCH):CHUNK * (n % NCH) + CHUNK], mbank[n % 2][:, :],
                                         ACT.Copy).then_inc(s_ma, 1)
                for j in range(JT):
                    k = NBLK * b + j // BLK
                    act.wait_ge(s_mx, JT * b + j + 1)
                    if k >= 2:
                        act.wait_ge(s_pv, 8 * (k - 1))
                    if JT * b + j >= 2:
                        act.wait_ge(s_rr, JT * b + j - 1)
                    nc.scalar.activation(ex[:, k % 2, j % BLK, :], lbank[:, :], ACT.Exp, bias=nmx[:, j % 2:j % 2 + 1],
                                         accum_out=rs[:, j % 2:j % 2 + 1]).then_inc(s_ex, 1)

        @block.vector
        def _(dve):
            def scaled(b, j):
                dve.wait_ge(s_ex, JT * b + j + 1)
                nc.vector.reciprocal(rr[:, j % 2:j % 2 + 1], rs[:, j % 2:j % 2 + 1]).then_inc(s_rr, 1)
                dve.wait_ge(s_rr, JT * b + j + 1)
                k = NBLK * b + j // BLK
                if k >= 2:
                    dve.wait_ge(s_pv, 8 * (k - 1))
                nc.vector.tensor_scalar(gs[:, k % 2, j % BLK, :, :], gt[:, :, j, :], rr[:, j % 2:j % 2 + 1], None,
                                        ALU.mult).then_inc(s_gs, 1)

            def add(b, k, u):
                n = 8 * (NBLK * b + k) + u
                dve.wait_ge(s_pv, n + 1)
                dst = att[:, CHUNK * u:CHUNK * u + CHUNK]
                if k == 0:
                    if b:
                        dve.wait_ge(s_mm, FILLS * b)
                    nc.vector.tensor_copy(dst, vbank[n % 2][:, :]).then_inc(s_pa, 1)
                else:
                    dve.wait_ge(s_pa, n - 7)
                    nc.vector.tensor_tensor(dst, vbank[n % 2][:, :], dst, ALU.add).then_inc(s_pa, 1)

            for b in range(B):
                for n in range(2 * NCH, 2 * NCH + JT // 2):
                    dve.wait_ge(s_mm, FILLS * b + n + 1)
                    t = 4 * (n - 2 * NCH)
                    nc.vector.tensor_copy(gt[:, t // JT, t % JT:t % JT + 4, :].rearrange("p t n -> p (t n)"),
                                          mbank[n % 2][:, :]).then_inc(s_md, 1)
                for j in range(JT):
                    if JT * b + j >= 2:
                        dve.wait_ge(s_ex, JT * b + j - 1)
                    for c in range(NIC):
                        dve.wait_ge(s_lg, NIC * (JT * b + j) + c + 1)
                        nc.vector.reduce_max(mx[:, j % 2, c:c + 1], lbank[:, CHUNK * c:CHUNK * c + CHUNK], AX_X).then_inc(s_bm, 1)
                    dve.wait_ge(s_bm, NIC * (JT * b + j + 1))
                    nc.vector.tensor_reduce(nmx[:, j % 2:j % 2 + 1], mx[:, j % 2, :], AX_X, ALU.max, negate=True).then_inc(s_mx, 1)
                    if j:
                        scaled(b, j - 1)
                    if j >= BLK:
                        add(b, j // BLK - 1, 2 * (j % BLK))
                        add(b, j // BLK - 1, 2 * (j % BLK) + 1)
                scaled(b, JT - 1)
                for u in range(8):
                    add(b, NBLK - 1, u)
                for m in range(2 * NCH):
                    n = FILLS - 2 * NCH + m
                    dve.wait_ge(s_mm, FILLS * b + n + 1)
                    dst = xa[:, b % 2, m // NCH, CHUNK * (m % NCH):CHUNK * (m % NCH) + CHUNK]
                    nc.vector.tensor_tensor(dst, mbank[n % 2][:, :], dst, ALU.add).then_inc(s_mo, 1)


PATHS, HD = 32, 4
ALL = B * PIX
LOADW = 2048
NLOAD = ALL // LOADW
NFILL = ALL // CHUNK
PART3 = ((0, 0), (0, 1), (1, 0), (0, 2), (1, 1), (2, 0))
NCOPY = len(PART3)
KROWS = NCOPY * HD
KBIAS = 3


def squeeze_block(nc, x2, w1t, w2bd, vec128, w3r, bc3, masks, parts, wparts):
    with ExitStack() as ctx:
        def sb(name, shape, dt=F32):
            return ctx.enter_context(nc.sbuf_tensor(name, shape, dt))

        def sem(name):
            return ctx.enter_context(nc.semaphore(name))

        w1_sb = sb("w1_sb", [P, CH, P])
        w2_sb = sb("w2_sb", [P, TAPS, P])
        vec = sb("vec", [P, 6])
        w3_sb = sb("w3_sb", [P, C])
        g3_sb = sb("g3_sb", [P, 3, C])
        mk = sb("mk", [P, 2 * P])
        xc = sb("xc", [P, 2, CH, LOADW])
        y1 = sb("y1", [P, B, CELLS])
        y2 = sb("y2", [P, ALL])
        st1 = sb("st1", [P, NFILL, 6])
        st2 = sb("st2", [P, NFILL, 6])
        mv1 = sb("mv1", [P, 2])
        mv2 = sb("mv2", [P, 2])
        tiny = sb("tiny", [P, 12])
        sums = sb("sums", [P, NLOAD])
        xflat = xc[:, :, :, :].rearrange("p a h n -> p (a h n)")
        cen = xflat[:, 0:2 * CHUNK].rearrange("p (a n) -> p a n", a=2)
        yt = xflat[:, 2 * CHUNK:4 * CHUNK].rearrange("p (a n) -> p a n", a=2)
        rest = xflat[:, 4 * CHUNK:4 * CHUNK + LOADW]
        yflat = y1[:, :, :].rearrange("p b n -> p (b n)")
        yp = yflat[:, 0:3 * LOADW].bitcast(BF16).rearrange("p (a i n) -> p a i n", a=2, i=3)
        o = 3 * LOADW
        covm = yflat[:, o:o + P]
        tcov = yflat[:, o + P:o + P + C]
        tmean = yflat[:, o + P + C:o + P + 2 * C]
        s3 = yflat[:, o + P + 2 * C:o + P + 3 * C]
        a3 = yflat[:, o + P + 3 * C:o + P + 4 * C]
        b3 = yflat[:, o + P + 4 * C:o + P + 5 * C]
        o += P + 5 * C
        ap = yflat[:, o:o + 3 * C].bitcast(BF16).rearrange("p (k i n) -> p k i n", k=2, i=3)

        bank = [ctx.enter_context(nc.psum_tensor(f"qbank{i}", [P, CHUNK], F32)) for i in range(8)]

        s_w = sem("q_weights_loaded")
        s_x = [sem(f"q_x_loaded{i}") for i in range(2)]
        s_zero = sem("q_border_zeroed")
        s_c1 = sem("q_conv1_product")
        s_k1 = sem("q_conv1_kept")
        s_c2 = sem("q_conv2_product")
        s_k2 = sem("q_conv2_kept")
        s_var = sem("q_variance_ready")
        s_std = sem("q_deviation_ready")
        s_sc = sem("q_scale_ready")
        s_n1 = sem("q_y1_normalised")
        s_n2 = sem("q_y2_normalised")
        s_dv = sem("q_vector_step")
        s_mean = sem("q_mean_ready")
        s_cen = sem("q_centred")
        s_tp = sem("q_turned")
        s_tk = sem("q_turned_kept")
        s_cov = sem("q_covariance_product")
        s_p = [sem(f"q_part{i}") for i in range(3)]
        s_rest = sem("q_rest")
        s_pst = [sem(f"q_parts_stored{i}") for i in range(2)]
        s_cm = sem("q_covariance_masked")
        s_t = sem("q_cov_times_w")
        s_u = sem("q_w_cov_w")
        s_m3 = sem("q_moments3")
        s_v3 = sem("q_variance3")
        s_d3 = sem("q_deviation3")
        s_wp = sem("q_weight_parts")
        s_wst = sem("q_weight_parts_stored")
        block = ctx.enter_context(nc.Block())
        NW = 6

        @block.sync
        def _(sp):
            sp.dma_start(w1_sb[:, :, :], w1t.rearrange("(h p) m -> p h m", p=P)).then_inc(s_w, 16)
            sp.dma_start(w2_sb[:, :, :].rearrange("p k m -> p (k m)"), w2bd).then_inc(s_w, 16)
            sp.dma_start(vec[:, :], vec128).then_inc(s_w, 16)
            sp.dma_start(w3_sb[:, :], w3r).then_inc(s_w, 16)
            sp.dma_start(g3_sb[:, :, :].rearrange("p a c -> p (a c)"), bc3).then_inc(s_w, 16)
            sp.dma_start(mk[:, :], masks).then_inc(s_w, 16)
            for n in range(NLOAD):
                if n >= 2:
                    sp.wait_ge(s_c1, 4 * (n - 1))
                sp.dma_start(xc[:, n % 2, :, :], x2[:, LOADW * n:LOADW * n + LOADW].rearrange("(h p) n -> p h n", p=P)
                             ).then_inc(s_x[n % 2], 16)
            for n in range(NLOAD):
                for i in (0, 1, 2):
                    sp.wait_ge(s_p[i], n + 1)
                    for cp, (_, yi) in enumerate(PART3):
                        if yi != i:
                            continue
                        for h in range(HD):
                            sp.dma_start(parts[:, HD * cp + h, LOADW * n:LOADW * n + LOADW],
                                         yp[32 * h:32 * h + 32, n % 2, i, :]).then_inc(s_pst[n % 2], 16)
            sp.wait_ge(s_wp, 1)
            for cp, (wi, _) in enumerate(PART3):
                for h in range(HD):
                    sp.dma_start(wparts[:, HD * cp + h, :], ap[32 * h:32 * h + 32, 0, wi, :]).then_inc(s_wst, 16)
            for i in range(KBIAS):
                sp.dma_start(wparts[:, KROWS + i, :], ap[0:32, 1, i, :]).then_inc(s_wst, 16)
            sp.wait_ge(s_wst, 16 * (NCOPY * HD + KBIAS))
            for i in range(2):
                sp.wait_ge(s_pst[i], 16 * NCOPY * HD * NLOAD // 2)

        @block.gpsimd
        def _(pool):
            nc.gpsimd.memset(yflat[:, :], 0.0).then_inc(s_zero, 1)
            for n in range(NLOAD):
                src = y2[:, LOADW * n:LOADW * n + LOADW]
                if n == 0:
                    pool.wait_ge(s_c2, NFILL)
                pool.wait_ge(s_p[0], n + 1)
                if n:
                    pool.wait_ge(s_p[2], n)
                    pool.wait_ge(s_p[1], n)
                nc.gpsimd.tensor_tensor(rest, src, yp[:, n % 2, 0, :], ALU.subtract).then_inc(s_rest, 1)
                pool.wait_ge(s_p[1], n + 1)
                nc.gpsimd.tensor_tensor(yp[:, n % 2, 2, :], rest, yp[:, n % 2, 1, :], ALU.subtract).then_inc(s_p[2], 1)

        @block.tensor
        def _(pe):
            pe.wait_ge(s_w, 16 * NW)
            for n in range(NFILL):
                if n % 4 == 0:
                    pe.wait_ge(s_x[(n // 4) % 2], 16 * (n // 8 + 1))
                if n >= 4:
                    pe.wait_ge(s_k1, n - 3)
                for h in range(CH):
                    mm = nc.tensor.matmul(bank[n % 4][:, :], w1_sb[:, h, :],
                                          xc[:, (n // 4) % 2, h, CHUNK * (n % 4):CHUNK * (n % 4) + CHUNK],
                                          start=(h == 0), stop=(h == 1))
                mm.then_inc(s_c1, 1)
            for n in range(NFILL):
                b, y = n // 8, 8 * (n % 8)
                if n % 8 == 0:
                    pe.wait_ge(s_n1, b + 1)
                if n >= 4:
                    pe.wait_ge(s_k2, n - 3)
                rows = y1[:, b, :].rearrange("p (y x) -> p y x", x=PITCH)
                for k in range(TAPS):
                    mm = nc.tensor.matmul(bank[4 + n % 4][:, :], w2_sb[:, k, :],
                                          rows[:, y + k // 3:y + k // 3 + 8, k % 3:k % 3 + W],
                                          start=(k == 0), stop=(k == TAPS - 1))
                mm.then_inc(s_c2, 1)
            pe.wait_ge(s_k2, NFILL)

            def covary(n):
                pe.wait_ge(s_tk, n + 1)
                for i in range(4):
                    t = yt[:, n % 2, P * i:P * i + P]
                    mm = nc.tensor.matmul(bank[7][:, 0:P], t, t, start=(n == 0 and i == 0),
                                          stop=(n == NFILL - 1 and i == 3))
                mm.then_inc(s_cov, 1)

            for n in range(NFILL):
                pe.wait_ge(s_cen, n + 1)
                if n >= 2:
                    pe.wait_ge(s_tk, n - 1)
                for i in range(4):
                    mm = nc.tensor.transpose(bank[n % 2][:, P * i:P * i + P], cen[:, n % 2, P * i:P * i + P], mk[:, 0:P])
                mm.then_inc(s_tp, 1)
                if n:
                    covary(n - 1)
            covary(NFILL - 1)
            pe.wait_ge(s_cm, 1)
            nc.tensor.matmul(bank[2][:, 0:C], covm, w3_sb[:, :], start=True, stop=True).then_inc(s_t, 1)
            pe.wait_ge(s_u, 1)
            nc.tensor.matmul(bank[3][:, 0:C], mk[:, P:2 * P], tcov, start=True, stop=True)
            nc.tensor.matmul(bank[4][:, 0:C], mk[:, P:2 * P], tmean, start=True, stop=True).then_inc(s_m3, 1)

        @block.scalar
        def _(act):
            act.wait_ge(s_w, 16 * NW)
            act.wait_ge(s_zero, 1)
            for n in range(NFILL):
                act.wait_ge(s_c1, n + 1)
                rows = y1[:, n // 8, :].rearrange("p (y x) -> p y x", x=PITCH)
                y = 8 * (n % 8)
                nc.scalar.activation(rows[:, y + 1:y + 9, 1:W + 1], bank[n % 4][:, :].rearrange("p (y x) -> p y x", x=W),
                                     ACT.Identity, bias=vec[:, 0:1]).then_inc(s_k1, 1)
            act.wait_ge(s_var, 1)
            nc.scalar.activation(tiny[:, 1:2], tiny[:, 0:1], ACT.Sqrt).then_inc(s_std, 1)
            act.wait_ge(s_sc, 1)
            for b in range(B):
                rows = y1[:, b, :].rearrange("p (y x) -> p y x", x=PITCH)[:, 1:H + 1, 1:W + 1]
                nc.scalar.activation(rows, rows, ACT.Relu, scale=tiny[:, 2:3], bias=tiny[:, 3:4]).then_inc(s_n1, 1)
            for n in range(NFILL):
                act.wait_ge(s_c2, n + 1)
                nc.scalar.activation(y2[:, CHUNK * n:CHUNK * n + CHUNK], bank[4 + n % 4][:, :], ACT.Identity,
                                     bias=vec[:, 3:4]).then_inc(s_k2, 1)
            act.wait_ge(s_var, 2)
            nc.scalar.activation(tiny[:, 5:6], tiny[:, 4:5], ACT.Sqrt).then_inc(s_std, 1)
            act.wait_ge(s_sc, 2)
            for n in range(NLOAD):
                part = y2[:, LOADW * n:LOADW * n + LOADW]
                nc.scalar.activation(part, part, ACT.Relu, scale=tiny[:, 6:7], bias=tiny[:, 7:8],
                                     accum_out=sums[:, n:n + 1]).then_inc(s_n2, 1)

            def keep_turned(n):
                act.wait_ge(s_tp, n + 1)
                if n >= 2:
                    act.wait_ge(s_cov, n - 1)
                nc.scalar.activation(yt[:, n % 2, :], bank[n % 2][:, :], ACT.Copy).then_inc(s_tk, 1)

            for n in range(NLOAD):
                if n >= 2:
                    act.wait_ge(s_pst[n % 2], 16 * NCOPY * HD * (n // 2))
                act.wait_ge(s_n2, n + 1)
                nc.scalar.activation(yp[:, n % 2, 0, :], y2[:, LOADW * n:LOADW * n + LOADW], ACT.Copy).then_inc(s_p[0], 1)
                for i in range(4):
                    keep_turned(4 * n + i)
                act.wait_ge(s_rest, n + 1)
                nc.scalar.activation(yp[:, n % 2, 1, :], rest, ACT.Copy).then_inc(s_p[1], 1)
            act.wait_ge(s_v3, 1)
            nc.scalar.activation(s3, tcov, ACT.Sqrt).then_inc(s_d3, 1)

        @block.vector
        def _(dve):
            steps = [0]

            def link(ins):
                steps[0] += 1
                ins.then_inc(s_dv, 1)
                dve.wait_ge(s_dv, steps[0])

            def norm(n, st, mv, g, be):
                o = 4 * n
                link(nc.vector.memset(tiny[:, o:o + 1], 0.0))
                link(nc.vector.bn_aggr(mv[:, :], st[:, :, :].rearrange("p g s -> p (g s)")))
                nc.vector.tensor_scalar(tiny[:, o:o + 1], mv[:, 1:2], EPS, None, ALU.add).then_inc(s_var, 1)
                dve.wait_ge(s_std, n + 1)
                link(nc.vector.reciprocal(tiny[:, 8:9], tiny[:, o + 1:o + 2]))
                link(nc.vector.tensor_tensor(tiny[:, o + 2:o + 3], tiny[:, 8:9], vec[:, g:g + 1], ALU.mult))
                link(nc.vector.tensor_tensor(tiny[:, 9:10], mv[:, 0:1], tiny[:, o + 2:o + 3], ALU.mult))
                nc.vector.tensor_tensor(tiny[:, o + 3:o + 4], vec[:, be:be + 1], tiny[:, 9:10], ALU.subtract).then_inc(s_sc, 1)

            dve.wait_ge(s_w, 16 * NW)
            for n in range(NFILL):
                dve.wait_ge(s_k1, n + 1)
                rows = y1[:, n // 8, :].rearrange("p (y x) -> p y x", x=PITCH)
                y = 8 * (n % 8)
                nc.vector.bn_stats(st1[:, n, :], rows[:, y + 1:y + 9, 1:W + 1])
            norm(0, st1, mv1, 1, 2)
            for n in range(NFILL):
                dve.wait_ge(s_k2, n + 1)
                nc.vector.bn_stats(st2[:, n, :], y2[:, CHUNK * n:CHUNK * n + CHUNK])
            norm(1, st2, mv2, 4, 5)
            dve.wait_ge(s_n2, NLOAD)
            link(nc.vector.reduce_sum(tiny[:, 10:11], sums[:, :], AX_X))
            link(nc.vector.tensor_scalar(tiny[:, 11:12], tiny[:, 10:11], 1.0 / ALL, None, ALU.mult))
            for n in range(NFILL):
                if n >= 2:
                    dve.wait_ge(s_tp, n - 1)
                nc.vector.tensor_scalar(cen[:, n % 2, :], y2[:, CHUNK * n:CHUNK * n + CHUNK], tiny[:, 11:12], None,
                                        ALU.subtract).then_inc(s_cen, 1)
            dve.wait_ge(s_cov, NFILL)
            nc.vector.scalar_tensor_tensor(out=covm, in0=bank[7][:, 0:P], scalar=1.0 / ALL, in1=mk[:, P:2 * P],
                                           op0=ALU.mult, op1=ALU.mult).then_inc(s_cm, 1)
            nc.vector.tensor_scalar(tmean, w3_sb[:, :], tiny[:, 11:12], None, ALU.mult)
            dve.wait_ge(s_t, 1)
            nc.vector.tensor_tensor(tcov, bank[2][:, 0:C], w3_sb[:, :], ALU.mult).then_inc(s_u, 1)
            dve.wait_ge(s_m3, 1)
            nc.vector.tensor_scalar(tcov, bank[3][:, 0:C], EPS, None, ALU.add).then_inc(s_v3, 1)
            link(nc.vector.tensor_tensor(tmean, bank[4][:, 0:C], g3_sb[:, 2, :], ALU.add))
            link(nc.vector.tensor_tensor(b3, g3_sb[:, 2, :], tmean, ALU.subtract))
            dve.wait_ge(s_d3, 1)
            link(nc.vector.reciprocal(a3, s3))
            link(nc.vector.tensor_tensor(s3, a3, g3_sb[:, 0, :], ALU.mult))
            link(nc.vector.tensor_tensor(a3, w3_sb[:, :], s3, ALU.mult))
            link(nc.vector.tensor_tensor(tmean, b3, s3, ALU.mult))
            link(nc.vector.tensor_tensor(b3, tmean, g3_sb[:, 1, :], ALU.add))
            for k, v in enumerate((a3, b3)):
                link(nc.vector.tensor_copy(ap[:, k, 0, :], v))
                link(nc.vector.tensor_tensor(s3, v, ap[:, k, 0, :], ALU.subtract))
                link(nc.vector.tensor_copy(ap[:, k, 1, :], s3))
                ins = nc.vector.tensor_tensor(ap[:, k, 2, :], s3, ap[:, k, 1, :], ALU.subtract)
                if k == 0:
                    link(ins)
            ins.then_inc(s_wp, 1)


TILE = 1024
NT = ALL // TILE
UNITS = 2 * PATHS
SLOTS = 4
TMPS = 4


def by_pool(path):
    return path % 3 == 1


def expand_block(nc, x2, parts, wparts, total, st4):
    with ExitStack() as ctx:
        def sb(name, shape, dt=F32):
            return ctx.enter_context(nc.sbuf_tensor(name, shape, dt))

        def sem(name):
            return ctx.enter_context(nc.semaphore(name))

        wl = sb("wl", [P, PATHS // 4, C], BF16)
        yv = sb("yv", [P, 2, PATHS // 4, TILE], BF16)
        acc = sb("acc", [P, 2, CH, TILE])
        tmp = sb("tmp", [P, TMPS, TILE])
        slot = [ctx.enter_context(nc.psum_tensor(f"slot{i}", [P, TILE], F32)) for i in range(SLOTS)]

        s_w = sem("e_weights_loaded")
        s_one = sem("e_ones_set")
        s_y = [sem(f"e_parts_loaded{i}") for i in range(2)]
        s_x = [sem(f"e_x_loaded{i}") for i in range(2)]
        s_z = sem("e_product")
        s_vec = sem("e_added_by_vector")
        s_rel = sem("e_rectified")
        s_pool = sem("e_added_by_pool")
        s_mrg = sem("e_merged")
        block = ctx.enter_context(nc.Block())

        NV = 2 * sum(not by_pool(p) for p in range(PATHS))
        NP = 2 * sum(by_pool(p) for p in range(PATHS))
        first = [p for p in range(PATHS) if not by_pool(p)][0]
        MERGE = 6
        vec_before = [2 * sum(not by_pool(q) for q in range(p)) for p in range(PATHS)]
        pool_before = [2 * sum(by_pool(q) for q in range(p)) for p in range(PATHS)]

        @block.sync
        def _(sp):
            for pq in range(4):
                sp.dma_start(wl[32 * pq:32 * pq + KROWS + KBIAS, :, :],
                             wparts.rearrange("(q r) k c -> r k q c", r=4)[pq]).then_inc(s_w, 16)
            sp.wait_ge(s_one, 1)

            def load(t, a):
                src = parts.rearrange("(q r) k n -> r k q n", r=4)
                for pq in range(4):
                    sp.dma_start(yv[32 * pq:32 * pq + KROWS, a, :, :],
                                 src[pq, :, :, bass.ds(TILE * t, TILE)]).then_inc(s_y[a], 16)
                sp.dma_start(acc[:, a, :, :], x2.rearrange("(h p) n -> p h n", p=P)[:, :, bass.ds(TILE * t, TILE)]).then_inc(s_x[a], 16)

            load(0, 0)
            load(1, 1)
            with sp.Fori(1, NT // 2) as it:
                for a in range(2):
                    sp.wait_ge(s_z, UNITS * (2 * it + a - 1))
                    sp.nop(nofuse=True)
                    sp.wait_ge(s_mrg, 2 * (2 * it + a - 1))
                    sp.nop(nofuse=True)
                    load(2 * it + a, a)

        @block.tensor
        def _(pe):
            pe.wait_ge(s_w, 64)

            def tile(t, a, start):
                pe.wait_ge(s_y[a], 64 * ((t - a) // 2 + 1) if isinstance(t, int) else 32 * (t - a) + 64)
                for p in range(PATHS):
                    for h in range(CH):
                        u = 2 * p + h
                        v = (u - SLOTS) % UNITS
                        vp, tt = v // 2, (t if u >= SLOTS else t - 1)
                        if not (start and u < SLOTS):
                            if by_pool(vp):
                                pe.wait_ge(s_rel, NP * tt + pool_before[vp] + v % 2 + 1)
                            else:
                                pe.wait_ge(s_vec, NV * tt + vec_before[vp] + v % 2 + 1)
                        r = slice(32 * (p % 4), 32 * (p % 4) + KROWS + KBIAS)
                        for c in range(TILE // CHUNK):
                            mm = nc.tensor.matmul(slot[u % SLOTS][:, CHUNK * c:CHUNK * c + CHUNK],
                                                  wl[r, p // 4, h * P:(h + 1) * P],
                                                  yv[r, a, p // 4, CHUNK * c:CHUNK * c + CHUNK], start=True, stop=True)
                        mm.then_inc(s_z, 1)

            tile(0, 0, True)
            tile(1, 1, False)
            with pe.Fori(1, NT // 2) as it:
                for a in range(2):
                    tile(2 * it + a, a, False)

        @block.scalar
        def _(act):
            def tile(t, a, start):
                for p in range(PATHS):
                    if not by_pool(p):
                        continue
                    for h in range(CH):
                        n = pool_before[p] + h
                        act.wait_ge(s_z, UNITS * t + 2 * p + h + 1)
                        if not (start and n < TMPS):
                            act.wait_ge(s_pool, NP * t + n + 1 - TMPS)
                        nc.scalar.activation(tmp[:, (NP * a + n) % TMPS, :], slot[(2 * p + h) % SLOTS][:, :],
                                             ACT.Relu).then_inc(s_rel, 1)

            tile(0, 0, True)
            tile(1, 1, False)
            with act.Fori(1, NT // 2) as it:
                for a in range(2):
                    tile(2 * it + a, a, False)

        @block.gpsimd
        def _(pool):
            nc.gpsimd.memset(yv[:, :, :, :].rearrange("p a q n -> p (a q n)"), 1.0).then_inc(s_one, 1)

            def tile(t, a, start):
                pool.wait_ge(s_x[a], 16 * ((t - a) // 2 + 1) if isinstance(t, int) else 8 * (t - a) + 16)
                for n in range(NP):
                    pool.wait_ge(s_rel, NP * t + n + 1)
                    if n >= 2:
                        pool.wait_ge(s_pool, NP * t + n - 1)
                    nc.gpsimd.tensor_tensor(acc[:, a, n % 2, :], tmp[:, (NP * a + n) % TMPS, :], acc[:, a, n % 2, :],
                                            ALU.add).then_inc(s_pool, 1)

            tile(0, 0, True)
            tile(1, 1, False)
            with pool.Fori(1, NT // 2) as it:
                for a in range(2):
                    tile(2 * it + a, a, False)

        @block.vector
        def _(dve):
            def here(t, h, c0=0, n=TILE):
                return total[:, h, bass.ds(TILE * t + c0, n)]

            def merge(t, a):
                dve.wait_ge(s_pool, NP * (t + 1))
                dve.wait_ge(s_vec, NV * (t + 1))
                for h in range(CH):
                    nc.vector.tensor_tensor(here(t, h), here(t, h), acc[:, a, h, :], ALU.add).then_inc(s_mrg, 1)
                dve.wait_ge(s_mrg, 2 * (t + 1))
                for h in range(CH):
                    for c in range(TILE // CHUNK):
                        at = TILE // CHUNK * t + c
                        out = st4[:, h, at, :] if isinstance(at, int) else st4[:, h, bass.ds(at, 1), :].rearrange(
                            "p a s -> p (a s)")
                        nc.vector.bn_stats(out, here(t, h, CHUNK * c, CHUNK))

            def tile(t, a, start):
                i = 0
                for p in range(PATHS):
                    if by_pool(p):
                        continue
                    for h in range(CH):
                        if i == MERGE and not start:
                            merge(t - 1, 1 - a)
                        u = 2 * p + h
                        dve.wait_ge(s_z, UNITS * t + u + 1)
                        z = slot[u % SLOTS][:, :]
                        if p == first:
                            ins = nc.vector.tensor_scalar(here(t, h), z, 0.0, None, ALU.max)
                        else:
                            dve.wait_ge(s_vec, NV * t + i - 1)
                            ins = nc.vector.scalar_tensor_tensor(out=here(t, h), in0=z, scalar=0.0, in1=here(t, h),
                                                                 op0=ALU.max, op1=ALU.add)
                        ins.then_inc(s_vec, 1)
                        i += 1

            tile(0, 0, True)
            tile(1, 1, False)
            with dve.Fori(1, NT // 2) as it:
                for a in range(2):
                    tile(2 * it + a, a, False)
            merge(NT - 1, 1)


SC = 1024


def sequence_block(nc, total, st4, vec256, out):
    with ExitStack() as ctx:
        def sb(name, shape, dt=F32):
            return ctx.enter_context(nc.sbuf_tensor(name, shape, dt))

        def sem(name):
            return ctx.enter_context(nc.semaphore(name))

        vec = sb("seq_vec", [P, 6, CH])
        mv = sb("seq_mv", [P, CH, 2])
        sm = sb("seq_sm", [P, 10, CH])
        v = sb("seq_v", [P, 2, PIX + 2])
        u = sb("seq_u", [P, 2, PIX])
        keep = sb("seq_keep", [P, SC])
        s_w = sem("r_vectors_loaded")
        s_dv = sem("r_vector_step")
        s_var = sem("r_variance")
        s_std = sem("r_deviation")
        s_sc = sem("r_scales")
        s_edge = sem("r_edges_zeroed")
        s_v = sem("r_normalised")
        s_u = sem("r_tenth")
        s_c = sem("r_middle")
        s_e = sem("r_average_part")
        s_t = sem("r_taps")
        s_sum = sem("r_summed")
        s_out = sem("r_stored")
        block = ctx.enter_context(nc.Block())
        rows = [(h, b) for b in range(B) for h in range(CH)]
        NSC = PIX // SC

        @block.sync
        def _(sp):
            sp.dma_start(vec[:, :, :].rearrange("p a h -> p (a h)"), vec256).then_inc(s_w, 16)
            for r, (h, b) in enumerate(rows):
                sp.wait_ge(s_sum, r + 1)
                sp.dma_start(out[b, h * P:(h + 1) * P, :], total[:, h, PIX * b:PIX * b + PIX]).then_inc(s_out, 16)
            sp.wait_ge(s_out, 16 * len(rows))

        @block.gpsimd
        def _(pool):
            nc.gpsimd.memset(v[:, :, 0:1], 0.0).then_inc(s_edge, 1)
            nc.gpsimd.memset(v[:, :, PIX + 1:PIX + 2], 0.0).then_inc(s_edge, 1)
            nc.gpsimd.memset(keep[:, :], 0.9).then_inc(s_edge, 1)
            for r, (h, b) in enumerate(rows):
                pool.wait_ge(s_e, NSC * (r + 1))
                pool.wait_ge(s_t, 2 * (r + 1))
                dst = total[:, h, PIX * b:PIX * b + PIX]
                nc.gpsimd.tensor_tensor(dst, dst, u[:, r % 2, :], ALU.add).then_inc(s_sum, 1)

        @block.scalar
        def _(act):
            act.wait_ge(s_var, 1)
            nc.scalar.activation(sm[:, 1, :], sm[:, 0, :], ACT.Sqrt).then_inc(s_std, 1)
            act.wait_ge(s_sc, 1)
            for r, (h, b) in enumerate(rows):
                src = total[:, h, PIX * b:PIX * b + PIX]
                if r >= 2:
                    act.wait_ge(s_t, 2 * (r - 1))
                nc.scalar.activation(v[:, r % 2, 1:PIX + 1], src, ACT.Identity, scale=sm[:, 2, h:h + 1],
                                     bias=sm[:, 3, h:h + 1]).then_inc(s_v, 1)
                if r >= 2:
                    act.wait_ge(s_sum, r - 1)
                nc.scalar.activation(u[:, r % 2, :], src, ACT.Identity, scale=sm[:, 4, h:h + 1],
                                     bias=sm[:, 5, h:h + 1]).then_inc(s_u, 1)
                nc.scalar.activation(src, src, ACT.Identity, scale=sm[:, 6, h:h + 1],
                                     bias=sm[:, 7, h:h + 1]).then_inc(s_c, 1)

        @block.vector
        def _(dve):
            steps = [0]

            def link(ins):
                steps[0] += 1
                ins.then_inc(s_dv, 1)
                dve.wait_ge(s_dv, steps[0])

            dve.wait_ge(s_w, 16)
            link(nc.vector.memset(sm[:, :, :].rearrange("p a h -> p (a h)"), 0.0))
            for h in range(CH):
                ins = nc.vector.bn_aggr(mv[:, h, :], st4[:, h, :, :].rearrange("p g s -> p (g s)"))
            link(ins)
            nc.vector.tensor_scalar(sm[:, 0, :], mv[:, :, 1], EPS, None, ALU.add).then_inc(s_var, 1)
            dve.wait_ge(s_std, 1)
            link(nc.vector.reciprocal(sm[:, 8, :], sm[:, 1, :]))
            link(nc.vector.tensor_tensor(sm[:, 2, :], sm[:, 8, :], vec[:, 0, :], ALU.mult))
            link(nc.vector.tensor_tensor(sm[:, 9, :], mv[:, :, 0], sm[:, 2, :], ALU.mult))
            link(nc.vector.tensor_tensor(sm[:, 3, :], vec[:, 1, :], sm[:, 9, :], ALU.subtract))
            link(nc.vector.tensor_scalar(sm[:, 4:6, :], sm[:, 2:4, :], 0.1, None, ALU.mult))
            link(nc.vector.tensor_scalar(sm[:, 8, :], vec[:, 3, :], 1.0, None, ALU.add))
            link(nc.vector.tensor_tensor(sm[:, 6, :], sm[:, 2, :], sm[:, 8, :], ALU.mult))
            link(nc.vector.tensor_tensor(sm[:, 9, :], sm[:, 3, :], sm[:, 8, :], ALU.mult))
            nc.vector.tensor_tensor(sm[:, 7, :], sm[:, 9, :], vec[:, 5, :], ALU.add).then_inc(s_sc, 1)
            dve.wait_ge(s_edge, 3)
            for r, (h, b) in enumerate(rows):
                dst = total[:, h, PIX * b:PIX * b + PIX]
                a = r % 2
                dve.wait_ge(s_u, r + 1)
                for c in range(NSC):
                    part = u[:, a, SC * c:SC * c + SC]
                    if c:
                        dve.wait_ge(s_e, NSC * r + c)
                    start = u[:, a, SC * c - 1:SC * c] if c else v[:, a, 1:2]
                    nc.vector.tensor_tensor_scan(part, keep[:, :], part, start, ALU.mult, ALU.add).then_inc(s_e, 1)
                dve.wait_ge(s_c, r + 1)
                for i, (tap, at) in enumerate(((2, 0), (4, 2))):
                    if i:
                        dve.wait_ge(s_t, 2 * r + 1)
                    nc.vector.scalar_tensor_tensor(out=dst, in0=v[:, a, at:at + PIX], scalar=vec[:, tap, h:h + 1], in1=dst,
                                                   op0=ALU.mult, op1=ALU.add).then_inc(s_t, 1)


def layer23(nc, x2, a, parts, wparts, out):
    squeeze_block(nc, x2, a["w1t"], a["w2bd"], a["vec128"], a["w3r"], a["bc3"], a["masks"], parts, wparts)
    with ExitStack() as ctx:
        total = ctx.enter_context(nc.sbuf_tensor("total", [P, CH, ALL], F32))
        st4 = ctx.enter_context(nc.sbuf_tensor("st4", [P, CH, NFILL, 6], F32))
        expand_block(nc, x2, parts, wparts, total, st4)
        sequence_block(nc, total, st4, a["vec256"], out)


def host0(inputs):
    f = np.float32
    out = {"x": inputs["x"].reshape(B, C, PIX)}
    for l in range(2):
        n = str(l + 1)
        out[f"wdc{l}"] = np.ascontiguousarray(
            inputs["L0_conv_w_dc" + n].reshape(C, C, TAPS).transpose(1, 2, 0)).reshape(C, TAPS * C)
        w = np.concatenate([inputs["L0_conv_w_tm" + n], inputs["L0_conv_w_tr" + n]]).reshape(NOFF, C, TAPS)
        out[f"woff{l}"] = np.ascontiguousarray(w.transpose(1, 2, 0)).reshape(C, NPART)
        out[f"boff{l}"] = np.concatenate([inputs["L0_conv_b_tm" + n], inputs["L0_conv_b_tr" + n]]).reshape(NOFF, 1)
    gb = np.stack([np.stack([inputs[f"L0_conv_g{n}"], inputs[f"L0_conv_be{n}"]]) for n in (1, 2)])
    out["gb"] = np.ascontiguousarray(gb.reshape(2, 2, CH, P).transpose(3, 0, 1, 2)).reshape(P, 4 * CH)
    c = np.zeros((P, 2 * P + NPOS + NTILE * NPOS), f)
    c[:, 0:P] = np.eye(P, dtype=f)
    c[:, P:2 * P] = np.kron(np.eye(P // GN_GROUP, dtype=f), np.full((GN_GROUP, GN_GROUP), 1 / GN_GROUP, f))
    for k in range(TAPS):
        ry, rx = k // 3 - 1, k % 3 - 1
        for tap in range(TAPS):
            for o, col, v in ((0, k, ry), (1, k, rx), (4, k, 1), (2, TAPS + k, ry), (3, TAPS + k, rx), (5, TAPS + k, 1)):
                c[NOFF * tap + o, 2 * P + col] = v
    at = c[:, 2 * P + NPOS:].reshape(P, NTILE, 2, TAPS)
    at[:, :, 0, :] = (2 * np.arange(NTILE)[None, :, None] + (np.arange(P) // W)[:, None, None])
    at[:, :, 1, :] = (np.arange(P) % W)[:, None, None]
    out["consts"] = c
    return out


def host1(inputs):
    w = np.concatenate([inputs["L1_conv_w_theta"], inputs["L1_conv_w_phi"], inputs["L1_conv_w_g"]])
    return {"wproj": np.ascontiguousarray(w.T), "wmask": np.ascontiguousarray(inputs["L1_conv_w_mask"].T)}


def host2(inputs):
    f = np.float32
    hp = lambda a: np.ascontiguousarray(a.reshape(PATHS, HD, *a.shape[1:]).swapaxes(0, 1)).reshape(a.shape)
    g = lambda n: inputs["L2_conv_" + n]
    out = {"w1t": np.ascontiguousarray(g("w1").T)}
    w2 = g("w2").reshape(PATHS, HD, HD, TAPS)
    bd = np.zeros((PATHS, HD, TAPS, HD, PATHS), f)
    for p in range(PATHS):
        bd[p, :, :, :, p] = w2[p].transpose(1, 2, 0)
    out["w2bd"] = bd.reshape(P, TAPS * P)
    out["vec128"] = np.ascontiguousarray(np.stack(
        [g("b1"), g("g1"), g("be1"), hp(g("b2")), hp(g("g2")), hp(g("be2"))], axis=1))
    out["w3r"] = np.ascontiguousarray(g("w3").transpose(2, 0, 1)).reshape(P, C)
    bc = np.stack([g("g3"), g("be3"), g("b3")], axis=1)
    out["bc3"] = np.ascontiguousarray(np.broadcast_to(bc[None], (HD, PATHS, 3, C))).reshape(P, 3 * C)
    out["masks"] = np.concatenate([np.eye(P, dtype=f), np.kron(np.ones((HD, HD), f), np.eye(PATHS, dtype=f))], axis=1)
    k = inputs["L3_conv_conv_w"].reshape(C, 3)
    v = np.stack([g("g4"), g("be4"), k[:, 0], k[:, 1], k[:, 2], inputs["L3_conv_conv_b"]])
    out["vec256"] = np.ascontiguousarray(v.reshape(6, CH, P).transpose(2, 0, 1)).reshape(P, 6 * CH)
    return out


def build(nc, a, out):
    table = [nc.dram_tensor(f"table{b}", (CELLS, PATCH), F32).ap() for b in range(B)]
    x1 = nc.dram_tensor("x1", (B, C, PIX), F32).ap()
    x2 = nc.dram_tensor("x2", (C, ALL), F32).ap()
    parts = nc.dram_tensor("parts", (PATHS, KROWS, ALL), BF16).ap()
    wparts = nc.dram_tensor("wparts", (PATHS, KROWS + KBIAS, C), BF16).ap()
    deformable_block(nc, a["x"], [a["wdc0"], a["wdc1"]], [a["woff0"], a["woff1"]], [a["boff0"], a["boff1"]],
                     a["gb"], table, x1, a["consts"])
    attention_block(nc, x1, a["wproj"], a["wmask"], x2)
    layer23(nc, x2, a, parts, wparts, out)


def kernel(**inputs):
    import concourse.bacc as bacc
    from concourse.bass_utils import run_bass_kernel_spmd

    inputs = {k: np.asarray(v) for k, v in inputs.items()}
    arrays = {**host0(inputs), **host1(inputs), **host2(inputs)}
    nc = bacc.Bacc("TRN2", target_bir_lowering=False, num_devices=1)
    args = {n: nc.dram_tensor(n, v.shape, mybir.dt.from_np(v.dtype), kind="ExternalInput").ap() for n, v in arrays.items()}
    out = nc.dram_tensor("out", (B, C, PIX), F32, kind="ExternalOutput").ap()
    build(nc, args, out)
    r = run_bass_kernel_spmd(nc, [arrays], core_ids=[0])
    return r.results[0]["out"].reshape(B, C, H, W)
```

```python
from contextlib import ExitStack

import numpy as np

import concourse.bass as bass
from concourse import mybir

ALU = mybir.AluOpType
ACT = mybir.ActivationFunctionType
F32 = mybir.dt.float32
I32 = mybir.dt.int32
BF16 = mybir.dt.bfloat16

B, C, H, W = 4, 256, 64, 64
P = 128
CH = C // P
PIX = H * W
TAPS = 9
PITCH = W + 2
CELLS = PITCH * (H + 2)
PATCH = 4 * C
NTILE = PIX // P
GN_GROUP = 8
EPS = 1e-5
NOFF = 6
NPART = TAPS * NOFF
NPOS = 2 * TAPS

GROUP_TILES = 2
GROUP = GROUP_TILES * P
NGROUP = PIX // GROUP
GS = GROUP_TILES * TAPS
NS = NTILE * TAPS
SRING = 6
TRING = 3
IDX_AFTER = 4
LAG = 3


def order_of_phases():
    seq = [("P", 0, b) for b in range(B)]
    for b in range(B):
        seq.append(("G", 0, b))
        if b:
            seq.append(("P", 1, b - 1))
    seq.append(("P", 1, B - 1))
    return seq + [("G", 1, b) for b in range(B)]


def deformable_block(nc, x, wdc, woff, boff, gamma_beta, table, x1, consts):
    seq = order_of_phases()
    ordinal = {}
    for kind in "PG":
        for n, ph in enumerate([ph for ph in seq if ph[0] == kind]):
            ordinal[ph] = n
    loads = {ph: n for n, ph in enumerate([ph for ph in seq if ph[:2] in (("P", 0), ("G", 1))])}

    def previous(ph):
        n = seq.index(ph)
        return seq[n - 1] if n else None

    def following(ph):
        n = seq.index(ph) + 1
        return seq[n] if n < len(seq) else None

    def ended_by(ph):
        prev = previous(ph)
        return prev if prev and prev[0] == "G" else None

    def before(ph, kind):
        return sum(q[0] == kind for q in seq[:seq.index(ph)])

    with ExitStack() as ctx:
        def sb(name, shape, dt=F32):
            return ctx.enter_context(nc.sbuf_tensor(name, shape, dt))

        def sem(name):
            return ctx.enter_context(nc.semaphore(name))

        ident = sb("ident", [P, P])
        gavg = sb("gavg", [P, P])
        sel = sb("sel", [P, NPOS])
        posbase = sb("posbase", [P, NTILE, NPOS])
        wdc_sb = sb("wdc_sb", [P, CH, TAPS, C])
        woff_sb = sb("woff_sb", [P, 2, CH, NPART])
        boff_sb = sb("boff_sb", [NPART, 2])
        gb_sb = sb("gb_sb", [P, 2, 2, CH])
        eps_sb = sb("eps_sb", [P, 1])
        image = [sb(f"image{i}", [P, CH, PIX]) for i in range(2)]
        turned = sb("turned", [P, 2, 4, C])
        pos = sb("pos", [P, NTILE, NPOS])
        posi = sb("posi", [P, NTILE, NPOS], I32)
        low = sb("low", [P, NTILE, NPOS])
        over = sb("over", [P, NTILE, NPOS])
        idxf = sb("idxf", [P, NTILE, TAPS])
        idx = sb("idx", [P, B, NTILE, TAPS], I32)
        wgt = sb("wgt", [P, B, NTILE, TAPS, 4])
        patch = sb("patch", [P, TAPS, PATCH])
        idx_now = sb("idx_now", [P, 2, TAPS], I32)
        wgt_now = sb("wgt_now", [P, 2, TAPS, 4])
        blend = sb("blend", [P, SRING, C])
        cols = sb("cols", [P, 2, CH, TAPS, GROUP])
        cols_flat = cols[:, :, :, :, :].rearrange("p a h k q -> p a (h k q)")
        part = cols_flat[:, 0, :]
        aligned = cols_flat[:, 1, :]
        stats = sb("stats", [P, CH, NGROUP, 6])
        mv = sb("mv", [P, CH, 2])
        mom = sb("mom", [P, 2, CH])
        gstat = sb("gstat", [P, 2, CH])
        small = sb("small", [P, 4, CH])
        scale = sb("scale", [P, CH])
        shift = sb("shift", [P, CH])

        bank = [ctx.enter_context(nc.psum_tensor(f"bank{i}", [P, 512], F32)) for i in range(8)]
        tbank = bank[0:TRING]
        obank = bank[3:5]
        partbank = bank[5:7]
        turnbank = [bank[7], bank[2]]
        posbank = bank[5:7]
        gnbank = bank[6]

        def buffer_of(ph):
            return image[0] if ph[:2] == ("G", 1) else image[ph[2] % 2]

        quarters = [(h, at) for at in (0, PIX // 2) for h in range(CH)]

        s_const = sem("const_loaded")
        s_w = sem("wdc_loaded")
        s_border = sem("table_border_written")
        s_x = [sem(f"x_loaded{i}") for i in range(2)]
        s_tab = [sem(f"table_written{i}") for i in range(2)]
        s_aln = sem("partials_aligned")
        s_gat = [sem(f"patch_gathered{k}") for k in range(TAPS)]
        s_out = sem("x1_stored")
        s_zero = sem("part_border_zeroed")
        s_pmm = sem("part_product")
        s_pev = sem("part_emptied")
        s_tmm = sem("turned_product")
        s_tev = sem("turned_emptied")
        s_posmm = sem("pos_product")
        s_dv = sem("vector_step")
        s_idx = sem("indices_ready")
        s_ic = sem("idx_copied")
        s_wc = sem("wgt_copied")
        s_mul = sem("corner0_weighted")
        s_st = sem("corner_added")
        s_blend = sem("blend_ready")
        s_tr = sem("sample_transposed")
        s_cols = sem("columns_ready")
        s_cv = sem("conv_product")
        s_oev = sem("conv_emptied")
        s_agg = sem("channel_moments")
        s_gn = sem("group_moments")
        s_var = sem("variance_ready")
        s_std = sem("deviation_ready")
        s_sc = sem("scale_ready")
        s_norm = sem("image_normalised")
        s_res = sem("residual_added")

        NCONST = 9
        block = ctx.enter_context(nc.Block())

        @block.sync
        def _(sp):
            zero = cols_flat
            o = 0
            sp.dma_start(ident[:, :], consts[:, 0:P]).then_inc(s_const, 16)
            sp.dma_start(gavg[:, :], consts[:, P:2 * P]).then_inc(s_const, 16)
            sp.dma_start(sel[:, :], consts[:, 2 * P:2 * P + NPOS]).then_inc(s_const, 16)
            sp.dma_start(posbase[:, :, :], consts[:, 2 * P + NPOS:2 * P + NPOS + NTILE * NPOS].rearrange(
                "p (t n) -> p t n", t=NTILE)).then_inc(s_const, 16)
            for l in range(2):
                sp.dma_start(woff_sb[:, l, :, :], woff[l].rearrange("(h p) m -> p h m", p=P)).then_inc(s_const, 16)
            sp.dma_start(gb_sb[:, :, :, :].rearrange("p l g h -> p (l g h)"), gamma_beta).then_inc(s_const, 16)

            def load_x(ph):
                n = loads[ph]
                if ph[1]:
                    if ph[2] == 0:
                        sp.wait_ge(s_tmm, 16 * 2 * B)
                        sp.wait_ge(s_pmm, 8 * 2 * B)
                    else:
                        sp.wait_ge(s_out, 16 * 4 * ph[2])
                    dst = image[1]
                else:
                    if n >= 2:
                        sp.wait_ge(s_tmm, 16 * (n - 1))
                        sp.wait_ge(s_pmm, 8 * (n - 1))
                    dst = buffer_of(ph)
                sp.dma_start(dst[:, :, :], x[ph[2]].rearrange("(h p) n -> p h n", p=P)).then_inc(s_x[n % 2], 16)

            sp.wait_ge(s_zero, 1)
            for l in range(2):
                sp.dma_start(boff_sb[4 * NOFF:5 * NOFF, l:l + 1], boff[l]).then_inc(s_const, 16)
            load_x(seq[0])
            load_x(seq[1])
            sp.wait_ge(s_zero, 2)
            for b in range(B):
                t = table[b].rearrange("(y x) n -> y x n", y=H + 2)
                sp.dma_start(t[:, W + 1, :], zero[0:H + 2, 0, 0:PATCH]).then_inc(s_border, 16)
                for col, side in ((0, 0), (W, 1)):
                    sp.dma_start(t[:, col, :].rearrange("y (r c n) -> y r c n", r=2, c=2)[:, :, side, :],
                                 zero[0:H + 2, 0, 0:2 * C].rearrange("p (r n) -> p r n", r=2)).then_inc(s_border, 16)
                for row, r in ((0, 0), (H, 1), (H + 1, 0), (H + 1, 1)):
                    for side in range(2):
                        lo = (2 * r + side) * C
                        sp.dma_start(t[row, 1 - side:1 - side + W, lo:lo + C], zero[0:W, 0, 0:C]).then_inc(s_border, 16)

            for ph in seq:
                kind, l, b = ph
                if kind == "P":
                    n = ordinal[ph]
                    t = table[b].rearrange("(y x) n -> y x n", y=H + 2)
                    for bt in range(8):
                        sp.wait_ge(s_tev, 16 * n + 2 * bt + 2)
                        for hp in range(2):
                            y = 8 * bt + hp
                            for r in range(2):
                                for c in range(2):
                                    sp.dma_start(
                                        t[y + 1 - r:y + 1 - r + 7:2, 1 - c:1 - c + W,
                                          (2 * r + c) * C:(2 * r + c + 1) * C].rearrange("y x n -> x y n"),
                                        turned[64 * hp:64 * hp + 64, bt % 2, :, :]).then_inc(s_tab[bt % 2], 16)
                    if l == 0 and b + 2 < B:
                        load_x(("P", 0, b + 2))
                    if l == 1 and b == B - 1:
                        load_x(("G", 1, 0))
                else:
                    n = ordinal[ph]
                    if b == 0:
                        if l:
                            sp.wait_ge(s_cv, 2 * NGROUP * n)
                        sp.dma_start(wdc_sb[:, :, :, :].rearrange("p h k o -> p h (k o)"),
                                     wdc[l].rearrange("(h p) m -> p h m", p=P)).then_inc(s_w, 16)
                    if l:
                        for c, (h, at) in enumerate(quarters):
                            sp.wait_ge(s_norm, 4 * n + c + 1)
                            sp.dma_start(x1[b, h * P:(h + 1) * P, at:at + PIX // 2],
                                         image[1][:, h, at:at + PIX // 2]).then_inc(s_out, 16)
                        if b + 1 < B:
                            load_x(("G", 1, b + 1))
            sp.wait_ge(s_out, 16 * 4 * B)

        @block.gpsimd
        def _(pool):
            pool.wait_ge(s_border, 16 * 44)

            def tile(ph, t, tt, skip):
                q, b = ordinal[ph], ph[2]
                nc.gpsimd.tensor_copy(idx_now[:, tt, :], idx[:, b, t, :] if isinstance(t, int) else
                                      idx[:, b, bass.ds(t, 1), :].rearrange("p a k -> p (a k)")).then_inc(s_ic, 1)
                pool.wait_ge(s_ic, NTILE * q + t + 1)
                pool.nop(nofuse=True)
                for k in range(TAPS):
                    if not skip:
                        pool.wait_ge(s_blend, NS * q + 9 * t + k - 8)
                        pool.nop(nofuse=True)
                    nc.gpsimd.indirect_dma_start(
                        out=patch[:, k, :], out_offset=None, in_=table[ph[2]],
                        in_offset=bass.IndirectOffsetOnAxis(ap=idx_now[:, tt, k:k + 1], axis=0),
                    ).then_inc(s_gat[k], 16)

            for ph in seq:
                if ph[0] != "G":
                    continue
                q = ordinal[ph]
                p = ordinal[("P",) + ph[1:]]
                pool.wait_ge(s_idx, p + 1)
                for i in range(2):
                    pool.wait_ge(s_tab[i], 16 * 8 * 4 * (p + 1))
                tile(ph, 0, 0, q == 0)
                tile(ph, 1, 1, False)
                with pool.Fori(1, NTILE // 2) as i:
                    for tt in range(2):
                        tile(ph, 2 * i + tt, tt, False)

        @block.scalar
        def _(act):
            act.wait_ge(s_const, 16 * NCONST)

            def weigh(ph, it, j):
                q = ordinal[ph]
                tt, k = (j // TAPS) % 2, j % TAPS
                if k == 0:
                    act.wait_ge(s_wc, NTILE * q + 4 * it + j // TAPS + 1)
                act.wait_ge(s_gat[k], 16 * (NTILE * q + 4 * it + j // TAPS + 1))
                if not (q == 0 and isinstance(it, int) and it == 0 and j < SRING):
                    act.wait_ge(s_tr, NS * q + 36 * it + j + 1 - SRING)
                nc.scalar.activation(blend[:, j % SRING, :], patch[:, k, 0:C], ACT.Copy,
                                     scale=wgt_now[:, tt, k, 0:1]).then_inc(s_mul, 1)

            def empty(ph, it, j):
                q = ordinal[ph]
                act.wait_ge(s_tr, NS * q + 36 * it + j + 1)
                e, tt, k = j // GS, (j // TAPS) % 2, j % TAPS
                if isinstance(it, int) and it == 0 and j == 0 and not ended_by(ph):
                    act.wait_ge(s_aln, 16 * TAPS * before(ph, "P"))
                    act.wait_ge(s_posmm, 2 * before(ph, "P"))
                elif j % GS == 0 and not (isinstance(it, int) and it == 0 and not ended_by(ph)):
                    act.wait_ge(s_cv, 2 * (NGROUP * q + 2 * it + e - 1))
                nc.scalar.activation(cols[:, e, :, k, tt * P:(tt + 1) * P],
                                     tbank[j % TRING][:, 0:C].rearrange("p (h n) -> p h n", h=CH),
                                     ACT.Copy).then_inc(s_cols, 1)

            def keep(ph, g, oh):
                q = ordinal[ph]
                act.wait_ge(s_cv, 2 * (NGROUP * q + g) + oh + 1)
                dst, g = (buffer_of(previous(ph)), g + NGROUP) if isinstance(g, int) and g < 0 else (buffer_of(ph), g)
                nc.scalar.activation(dst[:, oh, bass.ds(GROUP * g, GROUP)], obank[oh][:, 0:GROUP],
                                     ACT.Copy).then_inc(s_oev, 1)

            def deviation(ph):
                act.wait_ge(s_var, ordinal[ph] + 1)
                nc.scalar.activation(small[:, 1, :], small[:, 0, :], ACT.Sqrt,
                                     bias=eps_sb[:, 0:1]).then_inc(s_std, 1)

            def normalise(ph, c):
                h, at = quarters[c]
                if ph[1] == 0:
                    act.wait_ge(s_sc, ordinal[ph] + 1)
                    buf = buffer_of(ph)[:, h, at:at + PIX // 2]
                    nc.scalar.activation(buf, buf, ACT.Relu, scale=scale[:, h:h + 1],
                                         bias=shift[:, h:h + 1]).then_inc(s_norm, 1)
                else:
                    act.wait_ge(s_res, 4 * ph[2] + c + 1)
                    buf = image[1][:, h, at:at + PIX // 2]
                    nc.scalar.activation(buf, buf, ACT.Relu, bias=shift[:, h:h + 1]).then_inc(s_norm, 1)

            def iteration(ph, it, first):
                ends = ended_by(ph) if isinstance(it, int) else None
                alone = first and not ends
                for j in range(2 * GS):
                    e, jj = j // GS, j % GS
                    weigh(ph, it, j)
                    if j >= LAG:
                        empty(ph, it, j - LAG)
                    elif not alone:
                        empty(ph, it - 1, 2 * GS + j - LAG)
                    if jj == 3 and not alone:
                        keep(ph, 2 * it + e - 2, 1)
                    if ends and e:
                        if jj == 10:
                            deviation(ends)
                        if jj in (15, 17):
                            normalise(ends, jj - 15)
                            normalise(ends, jj - 14)
                    if jj == 16 and not (alone and e == 0):
                        keep(ph, 2 * it + e - 1, 0)

            for ph in seq:
                kind, l, b = ph
                if kind == "P":
                    n = ordinal[ph]
                    ends = ended_by(ph)
                    if ends:
                        keep(ends, NGROUP - 1, 0)
                        keep(ends, NGROUP - 1, 1)
                        deviation(ends)
                    act.wait_ge(s_zero, 5 + 3 * n)
                    rows = part[0:NPART, 0:CELLS].rearrange("m (y x) -> m y x", x=PITCH)
                    for c in range(8):
                        act.wait_ge(s_pmm, 8 * n + c + 1)
                        nc.scalar.activation(rows[:, 8 * c + 1:8 * c + 9, 1:W + 1],
                                             partbank[c % 2][0:NPART, :].rearrange("m (y x) -> m y x", x=W),
                                             ACT.Identity, bias=boff_sb[:, l:l + 1]).then_inc(s_pev, 1)
                        if ends and c % 2:
                            normalise(ends, c // 2)
                    act.wait_ge(s_pev, 8 * (n + 1))
                    if before(ph, "G"):
                        act.wait_ge(s_cv, 2 * NGROUP * before(ph, "G"))
                    if n > 0:
                        act.wait_ge(s_posmm, 2 * n)
                    for k in range(TAPS):
                        rows_k = slice(NOFF * k, NOFF * k + NOFF)
                        act.dma_start(aligned[rows_k, 0:PIX].rearrange("m (y x) -> m y x", x=W),
                                      part[rows_k, 0:CELLS].rearrange("m (y x) -> m y x", x=PITCH)[
                                          :, k // 3:k // 3 + H, k % 3:k % 3 + W]).then_inc(s_aln, 16)
                else:
                    iteration(ph, 0, True)
                    with act.Fori(1, NGROUP // 2) as it:
                        iteration(ph, it, False)
                    nxt = following(ph)
                    if not nxt or nxt[0] == "P":
                        for j in range(2 * GS - LAG, 2 * GS):
                            empty(ph, NGROUP // 2 - 1, j)
                        keep(ph, NGROUP - 2, 1)
                    if not nxt:
                        keep(ph, NGROUP - 1, 0)
                        keep(ph, NGROUP - 1, 1)
                        deviation(ph)
                        for c in range(4):
                            normalise(ph, c)

        @block.tensor
        def _(pe):
            pe.wait_ge(s_const, 16 * NCONST)

            def turn(ph, it, j):
                q = ordinal[ph]
                pe.wait_ge(s_blend, NS * q + 36 * it + j + 1)
                if not (q == 0 and isinstance(it, int) and it == 0 and j < TRING):
                    pe.wait_ge(s_cols, NS * q + 36 * it + j + 1 - TRING)
                for h in range(CH):
                    mm = nc.tensor.transpose(tbank[j % TRING][:, h * P:(h + 1) * P],
                                             blend[:, j % SRING, h * P:(h + 1) * P], ident[:, :])
                mm.then_inc(s_tr, 1)

            def conv(ph, g, e, oh, steps):
                q = ordinal[ph]
                for s in steps:
                    k, h = s // CH, s % CH
                    if s == 0:
                        if oh == 0:
                            pe.wait_ge(s_cols, NS * q + GS * (g + 1))
                        if not (q == 0 and isinstance(g, int) and g == 0):
                            pe.wait_ge(s_oev, 2 * (NGROUP * q + g - 1) + oh + 1)
                    mm = nc.tensor.matmul(obank[oh][:, 0:GROUP], wdc_sb[:, h, k, oh * P:(oh + 1) * P],
                                          cols[:, e, h, k, :], start=(s == 0), stop=(s == GS - 1))
                    if s == GS - 1:
                        mm.then_inc(s_cv, 1)

            def group_means(ph):
                pe.wait_ge(s_agg, ordinal[ph] + 1)
                pe.wait_ge(s_idx, before(ph, "P"))
                nc.tensor.matmul(gnbank[:, 0:4], gavg[:, :], mom[:, :, :].rearrange("p a h -> p (a h)"),
                                 start=True, stop=True).then_inc(s_gn, 1)

            def iteration(ph, it, first):
                ends = ended_by(ph) if isinstance(it, int) else None
                for j in range(2 * GS):
                    e, jj = j // GS, j % GS
                    turn(ph, it, j)
                    if 5 <= jj < 17 and not (first and not ends and e == 0):
                        oh = (jj - 5) // 6
                        s0 = 3 * ((jj - 5) % 6)
                        conv(ph, 2 * it + e - 1, 1 - e, oh, range(s0, s0 + 3))
                    if ends and e and jj == 7:
                        group_means(ends)

            for ph in seq:
                kind, l, b = ph
                ends = ended_by(ph)
                if kind == "P":
                    n = ordinal[ph]
                    src = buffer_of(ph)
                    if l == 0:
                        pe.wait_ge(s_x[loads[ph] % 2], 16 * (loads[ph] // 2 + 1))
                    if ends:
                        pe.wait_ge(s_cols, NS * (ordinal[ends] + 1))

                    def part_conv(c):
                        if n or c >= 2:
                            pe.wait_ge(s_pev, 8 * n + c - 1)
                        if ends and c == 0:
                            pe.wait_ge(s_var, ordinal[ends] + 1)
                        if n and c == 0:
                            pe.wait_ge(s_idx, n)
                        for h in range(CH):
                            mm = nc.tensor.matmul(partbank[c % 2][0:NPART, :], woff_sb[:, l, h, :],
                                                  src[:, h, 512 * c:512 * c + 512], start=(h == 0), stop=(h == CH - 1))
                        mm.then_inc(s_pmm, 1)

                    def positions():
                        pe.wait_ge(s_aln, 16 * TAPS * (n + 1))
                        pe.wait_ge(s_pev, 8 * (n + 1))
                        for t in range(NTILE):
                            mm = nc.tensor.matmul(posbank[t // 16][:, (t % 16) * NPOS:(t % 16 + 1) * NPOS],
                                                  aligned[0:NPART, P * t:P * t + P], sel[0:NPART, :], start=True, stop=True)
                            if t % 16 == 15:
                                mm.then_inc(s_posmm, 1)

                    for c in range(16):
                        if l and c % 8 == 0:
                            pe.wait_ge(s_norm, 4 * b + 2 + c // 4)
                        if n or c >= 2:
                            pe.wait_ge(s_tev, 16 * n + c - 1)
                        for i in range(4):
                            t, h = 2 * c + i // 2, i % 2
                            mm = nc.tensor.transpose(turnbank[c % 2][:, P * i:P * i + P],
                                                     src[:, h, P * t:P * t + P], ident[:, :])
                        mm.then_inc(s_tmm, 1)
                        if ends:
                            if c == 3:
                                for oh in range(2):
                                    conv(ends, NGROUP - 1, 1, oh, range(GS))
                            if c == 5:
                                group_means(ends)
                            if 6 <= c < 10:
                                part_conv(2 * (c - 6))
                                part_conv(2 * (c - 6) + 1)
                        elif c < 8:
                            part_conv(c)
                    positions()
                else:
                    if b == 0:
                        pe.wait_ge(s_w, 16 * (l + 1))
                    pe.wait_ge(s_tev, 16 * before(ph, "P"))
                    iteration(ph, 0, True)
                    with pe.Fori(1, NGROUP // 2) as it:
                        iteration(ph, it, False)
                    if not following(ph):
                        for oh in range(2):
                            conv(ph, NGROUP - 1, 1, oh, range(GS))
                        group_means(ph)

        @block.vector
        def _(dve):
            steps = [0]

            def link(ins):
                steps[0] += 1
                ins.then_inc(s_dv, 1)
                dve.wait_ge(s_dv, steps[0])

            nc.vector.memset(boff_sb[:, :], 0.0).then_inc(s_zero, 1)
            nc.vector.memset(cols_flat[:, 0, 0:4 * PATCH], 0.0).then_inc(s_zero, 1)
            link(nc.vector.memset(eps_sb[:, :], EPS))
            dve.wait_ge(s_const, 16 * NCONST)
            dve.wait_ge(s_border, 16 * 44)

            def iteration(ph, it, first):
                q = ordinal[ph]
                ends = ended_by(ph) if isinstance(it, int) else None
                alone = first and not ends
                base = 2 * NS * q
                for j in range(0, 2 * GS, 2):
                    for i in (j, j + 1):
                        if i % TAPS == 0:
                            tl = i // TAPS
                            t = 4 * it + tl
                            w = wgt[:, ph[2], t, :, :] if isinstance(t, int) else wgt[:, ph[2], bass.ds(t, 1), :, :].rearrange(
                                "p a k c -> p (a k) c")
                            nc.vector.tensor_copy(wgt_now[:, tl % 2, :, :], w).then_inc(s_wc, 1)
                            dve.wait_ge(s_wc, NTILE * q + t + 1)
                    for corner in (1, 2, 3):
                        for i in (j, j + 1):
                            k, tt = i % TAPS, (i // TAPS) % 2
                            if corner == 1:
                                dve.wait_ge(s_mul, NS * q + 36 * it + i + 1)
                            else:
                                dve.wait_ge(s_st, base + 72 * it + 2 * j + (i - j) + 1 + 2 * (corner - 2))
                            nc.vector.scalar_tensor_tensor(
                                out=blend[:, i % SRING, :], in0=patch[:, k, corner * C:(corner + 1) * C],
                                scalar=wgt_now[:, tt, k, corner:corner + 1], in1=blend[:, i % SRING, :],
                                op0=ALU.mult, op1=ALU.add).then_inc(s_blend if corner == 3 else s_st, 1)
                    e, jj = j // GS, j % GS
                    if j == IDX_AFTER and first and not ends:
                        indices(previous(ph))
                    if jj == 6 and not alone:
                        moments(ph, 2 * it + e - 2, 1)
                    if jj == 16 and not (alone and e == 0):
                        moments(ph, 2 * it + e - 1, 0)
                    if ends and e:
                        if jj == 6:
                            channel_moments()
                        if jj == 8:
                            variance(ends)
                        if jj == 10:
                            affine(ends)
                        if jj in (12, 14) and ends[1]:
                            residual(ends, jj - 12)
                            residual(ends, jj - 11)

            def moments(ph, g, oh):
                dve.wait_ge(s_oev, 2 * (NGROUP * ordinal[ph] + g) + oh + 1)
                src, g = (buffer_of(previous(ph)), g + NGROUP) if isinstance(g, int) and g < 0 else (buffer_of(ph), g)
                out = stats[:, oh, g, :] if isinstance(g, int) else stats[:, oh, bass.ds(g, 1), :].rearrange("p a s -> p (a s)")
                nc.vector.bn_stats(out, src[:, oh, bass.ds(GROUP * g, GROUP)])

            def channel_moments():
                link(nc.vector.memset(small[:, 3, :], 0.0))
                for h in range(CH):
                    ins = nc.vector.bn_aggr(mv[:, h, :], stats[:, h, :, :].rearrange("p g s -> p (g s)"))
                link(ins)
                nc.vector.tensor_copy(mom[:, 0, :], mv[:, :, 0])
                link(nc.vector.tensor_tensor(small[:, 2, :], mv[:, :, 0], mv[:, :, 0], ALU.mult))
                nc.vector.tensor_tensor(mom[:, 1, :], small[:, 2, :], mv[:, :, 1], ALU.add).then_inc(s_agg, 1)

            def variance(ph):
                dve.wait_ge(s_gn, ordinal[ph] + 1)
                link(nc.vector.tensor_copy(gstat[:, :, :].rearrange("p a h -> p (a h)"), gnbank[:, 0:4]))
                link(nc.vector.tensor_tensor(small[:, 2, :], gstat[:, 0, :], gstat[:, 0, :], ALU.mult))
                nc.vector.tensor_tensor(small[:, 0, :], gstat[:, 1, :], small[:, 2, :],
                                        ALU.subtract).then_inc(s_var, 1)

            def affine(ph):
                dve.wait_ge(s_std, ordinal[ph] + 1)
                link(nc.vector.reciprocal(small[:, 2, :], small[:, 1, :]))
                link(nc.vector.tensor_tensor(scale[:, :], small[:, 2, :], gb_sb[:, ph[1], 0, :], ALU.mult))
                link(nc.vector.tensor_tensor(small[:, 3, :], gstat[:, 0, :], scale[:, :], ALU.mult))
                nc.vector.tensor_tensor(shift[:, :], gb_sb[:, ph[1], 1, :], small[:, 3, :],
                                        ALU.subtract).then_inc(s_sc, 1)

            def residual(ph, c):
                h, at = quarters[c]
                dve.wait_ge(s_x[loads[ph] % 2], 16 * (loads[ph] // 2 + 1))
                dve.wait_ge(s_sc, ordinal[ph] + 1)
                out = image[1][:, h, at:at + PIX // 2]
                nc.vector.scalar_tensor_tensor(out=out, in0=buffer_of(ph)[:, h, at:at + PIX // 2], scalar=scale[:, h:h + 1],
                                               in1=out, op0=ALU.mult, op1=ALU.add).then_inc(s_res, 1)

            def indices(ph):
                n, b = ordinal[ph], ph[2]
                half = NTILE // 2
                for i in range(2):
                    dve.wait_ge(s_posmm, 2 * n + i + 1)
                    ins = nc.vector.tensor_tensor(
                        pos[:, half * i:half * i + half, :].rearrange("p t n -> p (t n)"),
                        posbank[i][:, 0:half * NPOS],
                        posbase[:, half * i:half * i + half, :].rearrange("p t n -> p (t n)"), ALU.add)
                link(ins)
                flat = lambda a: a[:, :, :].rearrange("p t n -> p (t n)")
                link(nc.vector.tensor_scalar(flat(pos), flat(pos), -1.0, float(H), ALU.max, ALU.min))
                link(nc.vector.tensor_copy(flat(posi), flat(pos)))
                link(nc.vector.tensor_copy(flat(low), flat(posi)))
                link(nc.vector.tensor_tensor(flat(over), flat(low), flat(pos), ALU.is_gt))
                link(nc.vector.tensor_tensor(flat(low), flat(low), flat(over), ALU.subtract))
                link(nc.vector.tensor_tensor(flat(pos), flat(pos), flat(low), ALU.subtract))
                link(nc.vector.tensor_scalar(flat(over), flat(pos), -1.0, 1.0, ALU.mult, ALU.add))
                for r, wy in enumerate((over, pos)):
                    for c, wx in enumerate((over, pos)):
                        nc.vector.tensor_tensor(wgt[:, b, :, :, 2 * r + c], wy[:, :, 0:TAPS],
                                                wx[:, :, TAPS:NPOS], ALU.mult)
                link(nc.vector.scalar_tensor_tensor(out=idxf[:, :, :], in0=low[:, :, 0:TAPS], scalar=float(PITCH),
                                                    in1=low[:, :, TAPS:NPOS], op0=ALU.mult, op1=ALU.add))
                nc.vector.tensor_scalar(idx[:, b, :, :], idxf[:, :, :], float(PITCH + 1), None,
                                        ALU.add).then_inc(s_idx, 1)
                dve.wait_ge(s_idx, n + 1)

            for ph in seq:
                kind, l, b = ph
                ends = ended_by(ph)
                if kind == "P":
                    n = ordinal[ph]
                    if ends:
                        moments(ends, NGROUP - 2, 1)
                        dve.wait_ge(s_cv, 2 * NGROUP * before(ph, "G") - 2)
                    if n:
                        dve.wait_ge(s_aln, 16 * TAPS * n)
                    nc.vector.memset(part[0:NPART, 0:PITCH + 1], 0.0).then_inc(s_zero, 1)
                    pairs = part[0:NPART, PITCH + W + 1:PITCH + W + 1 + H * PITCH].rearrange("m (y x) -> m y x", x=PITCH)
                    nc.vector.memset(pairs[:, :, 0:2], 0.0).then_inc(s_zero, 1)
                    nc.vector.memset(part[0:NPART, CELLS - PITCH + 1:CELLS], 0.0).then_inc(s_zero, 1)
                    for c in range(16):
                        dve.wait_ge(s_tmm, 16 * n + c + 1)
                        bt = c // 2
                        if n or bt >= 2:
                            dve.wait_ge(s_tab[bt % 2], 16 * 8 * (4 * n + bt // 2))
                        nc.vector.tensor_copy(
                            turned[:, bt % 2, 2 * (c % 2):2 * (c % 2) + 2, :].rearrange("p a n -> p (a n)"),
                            turnbank[c % 2][:, :]).then_inc(s_tev, 1)
                        if ends and c == 3:
                            moments(ends, NGROUP - 1, 0)
                            moments(ends, NGROUP - 1, 1)
                            channel_moments()
                        if ends and c == 5:
                            variance(ends)
                        if ends and c == 6:
                            affine(ends)
                    if following(ph)[0] == "P":
                        indices(ph)
                else:
                    iteration(ph, 0, True)
                    with dve.Fori(1, NGROUP // 2) as it:
                        iteration(ph, it, False)
                    if not following(ph):
                        moments(ph, NGROUP - 2, 1)
                        moments(ph, NGROUP - 1, 0)
                        moments(ph, NGROUP - 1, 1)
                        channel_moments()
                        variance(ph)
                        affine(ph)
                        for c in range(4):
                            residual(ph, c)
IC = C // 2
NKEY = PIX // 2
JT = NKEY // P
BLK = 2
NBLK = JT // BLK
CHUNK = 512
NCH = PIX // CHUNK
NIC = NKEY // CHUNK
XR = 4
ER = 2 * BLK
AX_X = mybir.AxisListType.X
FR = mybir.dt.float32r


def attention_block(nc, x1, wproj, wmask, x2):
    with ExitStack() as ctx:
        def sb(name, shape, dt=F32):
            return ctx.enter_context(nc.sbuf_tensor(name, shape, dt))

        def sem(name):
            return ctx.enter_context(nc.semaphore(name))

        proj = [sb(f"proj_{part}", [P, CH, 3 * IC], FR) for part in ("hi", "lo")]
        mask = [sb(f"mask_{part}", [P, C], FR) for part in ("hi", "lo")]
        xr = sb("xr", [P, XR, CH, CHUNK])
        split = [sb(f"split_{part}", [P, 2, CH, CHUNK], FR) for part in ("hi", "lo")]
        theta = [sb(f"theta_{part}", [P, PIX], FR) for part in ("hi", "lo")]
        phi = sb("phi", [P, 2, NKEY])
        phij = [sb(f"phi_tile_{part}", [P, 2, 2, P], FR) for part in ("hi", "lo")]
        gt = sb("gt", [P, 2, JT, IC])
        gs = [sb(f"gs_{part}", [P, ER, 2, IC], FR) for part in ("hi", "lo")]
        expo = sb("expo", [P, NKEY])
        ex = [sb(f"ex_{part}", [P, ER, NKEY], FR) for part in ("hi", "lo")]
        att = sb("att", [P, PIX])
        mx = sb("mx", [P, 2, NIC])
        nmx = sb("nmx", [P, 2])
        rs = sb("rs", [P, 2])
        rr = sb("rr", [P, 2])
        wraw = att[:, 0:CH * 3 * IC + C]

        lbank = ctx.enter_context(nc.psum_tensor("lbank", [P, NKEY], F32))
        vbank = [ctx.enter_context(nc.psum_tensor(f"vbank{i}", [P, CHUNK], F32)) for i in range(2)]
        mbank = [ctx.enter_context(nc.psum_tensor(f"mbank{i}", [P, CHUNK], F32)) for i in range(2)]

        s_w = sem("a_weights_loaded")
        s_wh = sem("a_weights_hi")
        s_wl = sem("a_weights_lo")
        s_x = [sem(f"a_x_loaded{i}") for i in range(XR)]
        s_st = [sem(f"a_stored{i}") for i in range(XR)]
        s_hi = sem("a_split_hi")
        s_lo = sem("a_split_lo")
        s_mm = sem("a_product")
        s_th = sem("a_theta_hi")
        s_phi = sem("a_phi_kept")
        s_ed = sem("a_bank_emptied_by_vector")
        s_pjh = sem("a_phi_tile_hi")
        s_pj = sem("a_phi_tile_ready")
        s_lg = sem("a_logits")
        s_bm = sem("a_bank_max")
        s_mx = sem("a_max_ready")
        s_ex = sem("a_exp_ready")
        s_eh = sem("a_exp_hi")
        s_el = sem("a_exp_lo")
        s_rr = sem("a_reciprocal")
        s_gh = sem("a_gt_hi")
        s_gs = sem("a_gt_scaled")
        s_pv = sem("a_pv_product")
        s_pa = sem("a_pv_added")
        SPLITS = 2 * NCH
        FILLS = 3 * NCH + CH * NCH
        EMPTIED = 2 * NCH + CH * NCH
        F = lambda ap: ap.bitcast(F32)
        block = ctx.enter_context(nc.Block())

        @block.sync
        def _(sp):
            sp.dma_start(wraw[:, 0:CH * 3 * IC].rearrange("p (h m) -> p h m", h=CH),
                         wproj.rearrange("(h p) m -> p h m", p=P)).then_inc(s_w, 16)
            sp.dma_start(wraw[:, CH * 3 * IC:CH * 3 * IC + C], wmask).then_inc(s_w, 16)

            def release(n):
                if n % SPLITS < NCH:
                    sp.wait_ge(s_lo, n + 1)
                else:
                    sp.wait_ge(s_st[n % XR], 16 * sum(m % XR == n % XR and m % SPLITS >= NCH for m in range(n + 1)))

            for n in range(SPLITS * B):
                if n >= XR:
                    release(n - XR)
                b, c = n // SPLITS, n % NCH
                sp.dma_start(xr[:, n % XR, :, :], x1[b].rearrange("(h p) n -> p h n", p=P)[
                    :, :, CHUNK * c:CHUNK * c + CHUNK]).then_inc(s_x[n % XR], 16)
            for n in range(SPLITS * B - XR, SPLITS * B):
                release(n)

        @block.tensor
        def _(pe):
            pe.wait_ge(s_wl, 2)

            def bank(b, n):
                m = n - 2 if n >= 2 else n - 2 + FILLS
                bb = b if n >= 2 else b - 1
                if bb < 0:
                    return
                if m >= 3 * NCH:
                    pe.wait_ge(s_ed, EMPTIED * bb + 2 * NCH + m - 3 * NCH + 1)
                elif m % 3 == 1:
                    pe.wait_ge(s_phi, NCH * bb + m // 3 + 1)
                else:
                    pe.wait_ge(s_ed, EMPTIED * bb + 2 * (m // 3) + m % 3 // 2 + 1)

            def products(out, terms):
                pairs = [(l[i], r[j]) for l, r in terms for i, j in ((1, 0), (0, 1), (0, 0))]
                for i, (l, r) in enumerate(pairs):
                    mm = nc.tensor.matmul(out, l, r, start=(i == 0), stop=(i == len(pairs) - 1))
                return mm

            def project(b, c):
                k = SPLITS * b + c
                pe.wait_ge(s_lo, k + 1)
                xs = lambda h, lo, n: [a[:, k % 2, h, lo:lo + n] for a in split]
                ws = lambda h, lo: [a[:, h, lo:lo + IC] for a in proj]
                for w in range(2):
                    bank(b, 3 * c + w)
                    products(mbank[(3 * c + w) % 2][:, :],
                             [(ws(h, w * IC), xs(h, 0, CHUNK)) for h in range(CH)]).then_inc(s_mm, 1)
                n = 3 * c + 2
                bank(b, n)
                for i in range(CHUNK // P):
                    mm = products(mbank[n % 2][:, IC * i:IC * i + IC],
                                  [(xs(h, P * i, P), ws(h, 2 * IC)) for h in range(CH)])
                mm.then_inc(s_mm, 1)

            def logits(b, j):
                pe.wait_ge(s_pj, JT * b + j + 1)
                if b or j:
                    pe.wait_ge(s_ex, JT * b + j)
                for c in range(NIC):
                    products(lbank[:, CHUNK * c:CHUNK * c + CHUNK],
                             [([a[:, j % 2, h, :] for a in phij],
                               [a[:, NKEY * h + CHUNK * c:NKEY * h + CHUNK * c + CHUNK] for a in theta])
                              for h in range(2)]).then_inc(s_lg, 1)

            def pv(b, k, u):
                h, c = u // NIC, u % NIC
                n = NCH * (NBLK * b + k) + u
                pe.wait_ge(s_gs, JT * b + BLK * (k + 1))
                pe.wait_ge(s_el, JT * b + BLK * (k + 1))
                if n >= 2:
                    pe.wait_ge(s_pa, n - 1)
                products(vbank[n % 2][:, :],
                         [([a[:, (BLK * k + i) % ER, h, :] for a in gs],
                           [a[:, (BLK * k + i) % ER, CHUNK * c:CHUNK * c + CHUNK] for a in ex])
                          for i in range(BLK)]).then_inc(s_pv, 1)

            def masked(b, u):
                k = SPLITS * b + NCH + u
                pe.wait_ge(s_lo, k + 1)
                for oh in range(CH):
                    n = 3 * NCH + CH * u + oh
                    bank(b, n)
                    products(mbank[n % 2][:, :], [([a[:, oh * P:(oh + 1) * P] for a in mask],
                                                   [a[:, 1, u % 2, :] for a in split])]).then_inc(s_mm, 1)

            for b in range(B):
                for c in range(NCH):
                    project(b, c)
                pe.wait_ge(s_ed, EMPTIED * b + 2 * NCH)
                for j in range(JT):
                    logits(b, j)
                    if j >= BLK:
                        for u in range(4 * (j % BLK), 4 * (j % BLK) + 4):
                            pv(b, j // BLK - 1, u)
                for u in range(NCH):
                    pv(b, NBLK - 1, u)
                    if u >= 2:
                        masked(b, u - 2)
                for u in (NCH - 2, NCH - 1):
                    masked(b, u)

        def split_free(eng, k):
            b, i = k // SPLITS, k % SPLITS
            if i >= NCH + 2:
                eng.wait_ge(s_mm, FILLS * b + 3 * NCH + CH * (i - NCH - 1))
            elif i >= NCH:
                eng.wait_ge(s_mm, FILLS * b + 3 * NCH)
            elif i >= 2:
                eng.wait_ge(s_mm, FILLS * b + 3 * (i - 1))
            elif i == 1 and b:
                eng.wait_ge(s_mm, FILLS * b)
            elif b:
                eng.wait_ge(s_mm, FILLS * (b - 1) + 3 * (NCH - 1))

        @block.scalar
        def _(act):
            act.wait_ge(s_w, 32)
            nc.scalar.activation(proj[0][:, :, :].rearrange("p h m -> p (h m)"), wraw[:, 0:CH * 3 * IC],
                                 ACT.Copy).then_inc(s_wh, 1)
            nc.scalar.activation(mask[0][:, :], wraw[:, CH * 3 * IC:CH * 3 * IC + C], ACT.Copy).then_inc(s_wh, 1)

            def split_x(b, c):
                k = SPLITS * b + c
                act.wait_ge(s_x[k % XR], 16 * (k // XR + 1))
                split_free(act, k)
                nc.scalar.activation(split[0][:, k % 2, :, :], xr[:, k % XR, :, :], ACT.Copy).then_inc(s_hi, 1)

            def keep(b, c):
                act.wait_ge(s_mm, FILLS * b + 3 * c + 1)
                at = CHUNK * c
                if b and c == 0:
                    act.wait_ge(s_lg, NIC * JT * b)
                nc.scalar.activation(theta[0][:, at:at + CHUNK], mbank[3 * c % 2][:, :], ACT.Copy).then_inc(s_th, 1)
                act.wait_ge(s_mm, FILLS * b + 3 * c + 2)
                if b and c == 0:
                    act.wait_ge(s_pj, JT * b)
                nc.scalar.activation(phi[:, c // NIC, at % NKEY:at % NKEY + CHUNK], mbank[(3 * c + 1) % 2][:, :],
                                     ACT.Copy).then_inc(s_phi, 1)

            split_x(0, 0)
            for b in range(B):
                for c in range(NCH):
                    if c + 1 < NCH:
                        split_x(b, c + 1)
                    keep(b, c)
                for j in range(JT):
                    n = JT * b + j
                    act.wait_ge(s_mx, n + 1)
                    if n >= 1:
                        act.wait_ge(s_el, n)
                    if n >= 2:
                        act.wait_ge(s_rr, n - 1)
                    nc.scalar.activation(expo[:, :], lbank[:, :], ACT.Exp, bias=nmx[:, j % 2:j % 2 + 1],
                                         accum_out=rs[:, j % 2:j % 2 + 1]).then_inc(s_ex, 1)
                    act.wait_ge(s_ex, n + 1)
                    if n >= ER:
                        act.wait_ge(s_pv, NCH * ((n - ER) // BLK + 1))
                    nc.scalar.activation(ex[0][:, j % ER, :], expo[:, :], ACT.Copy).then_inc(s_eh, 1)
                for u in range(NCH):
                    k = SPLITS * b + NCH + u
                    act.wait_ge(s_pa, NCH * (NBLK * (b + 1) - 1) + u + 1)
                    split_free(act, k)
                    nc.scalar.activation(split[0][:, 1, u % 2, :], att[:, CHUNK * u:CHUNK * u + CHUNK],
                                         ACT.Copy).then_inc(s_hi, 1)
                if b + 1 < B:
                    split_x(b + 1, 0)

        @block.gpsimd
        def _(pool):
            for b in range(B):
                for j in range(JT):
                    n = JT * b + j
                    pool.wait_ge(s_phi, NCH * b + NIC + j // 4 + 1)
                    if n >= 2:
                        pool.wait_ge(s_lg, NIC * (n - 1))
                    src = phi[:, :, P * j:P * j + P]
                    nc.gpsimd.tensor_copy(phij[0][:, j % 2, :, :], src).then_inc(s_pjh, 1)
                    pool.wait_ge(s_pjh, n + 1)
                    nc.gpsimd.tensor_tensor(phij[1][:, j % 2, :, :], src, F(phij[0][:, j % 2, :, :]),
                                            ALU.subtract).then_inc(s_pj, 1)
                for c in range(NCH):
                    n, at = SPLITS * b + NCH + c, PIX * b + CHUNK * c
                    pool.wait_ge(s_ed, EMPTIED * b + 2 * NCH + CH * (c + 1))
                    pool.dma_start(x2[:, at:at + CHUNK].rearrange("(h p) n -> p h n", p=P),
                                   xr[:, n % XR, :, :]).then_inc(s_st[n % XR], 16)

        @block.vector
        def _(dve):
            dve.wait_ge(s_wh, 2)
            nc.vector.tensor_tensor(proj[1][:, :, :].rearrange("p h m -> p (h m)"), wraw[:, 0:CH * 3 * IC],
                                    F(proj[0][:, :, :].rearrange("p h m -> p (h m)")), ALU.subtract).then_inc(s_wl, 1)
            nc.vector.tensor_tensor(mask[1][:, :], wraw[:, CH * 3 * IC:CH * 3 * IC + C], F(mask[0][:, :]),
                                    ALU.subtract).then_inc(s_wl, 1)

            def split_x(b, c):
                k = SPLITS * b + c
                dve.wait_ge(s_hi, k + 1)
                split_free(dve, k)
                nc.vector.tensor_tensor(split[1][:, k % 2, :, :], xr[:, k % XR, :, :], F(split[0][:, k % 2, :, :]),
                                        ALU.subtract).then_inc(s_lo, 1)

            def keep(b, c):
                dve.wait_ge(s_th, NCH * b + c + 1)
                at = CHUNK * c
                nc.vector.tensor_tensor(theta[1][:, at:at + CHUNK], mbank[3 * c % 2][:, :],
                                        F(theta[0][:, at:at + CHUNK]), ALU.subtract).then_inc(s_ed, 1)
                n, t = 3 * c + 2, 4 * c
                dve.wait_ge(s_mm, FILLS * b + n + 1)
                nc.vector.tensor_copy(gt[:, t // JT, t % JT:t % JT + 4, :].rearrange("p t n -> p (t n)"),
                                      mbank[n % 2][:, :]).then_inc(s_ed, 1)

            def bank_max(b, j, c):
                dve.wait_ge(s_lg, NIC * (JT * b + j) + c + 1)
                nc.vector.reduce_max(mx[:, j % 2, c:c + 1], lbank[:, CHUNK * c:CHUNK * c + CHUNK], AX_X).then_inc(s_bm, 1)

            def scaled(b, j):
                n = JT * b + j
                dve.wait_ge(s_ex, n + 1)
                nc.vector.reciprocal(rr[:, j % 2:j % 2 + 1], rs[:, j % 2:j % 2 + 1]).then_inc(s_rr, 1)
                dve.wait_ge(s_rr, n + 1)
                if n >= ER:
                    dve.wait_ge(s_pv, NCH * ((n - ER) // BLK + 1))
                r = rr[:, j % 2:j % 2 + 1]
                nc.vector.tensor_scalar(gs[0][:, j % ER, :, :], gt[:, :, j, :], r, None, ALU.mult).then_inc(s_gh, 1)
                dve.wait_ge(s_gh, n + 1)
                nc.vector.scalar_tensor_tensor(out=gs[1][:, j % ER, :, :], in0=gt[:, :, j, :], scalar=r,
                                               in1=F(gs[0][:, j % ER, :, :]), op0=ALU.mult,
                                               op1=ALU.subtract).then_inc(s_gs, 1)
                dve.wait_ge(s_eh, n + 1)
                nc.vector.tensor_tensor(ex[1][:, j % ER, :], expo[:, :], F(ex[0][:, j % ER, :]),
                                        ALU.subtract).then_inc(s_el, 1)

            def add(b, k, u):
                n = NCH * (NBLK * b + k) + u
                dve.wait_ge(s_pv, n + 1)
                dst = att[:, CHUNK * u:CHUNK * u + CHUNK]
                if k == 0:
                    nc.vector.tensor_copy(dst, vbank[n % 2][:, :]).then_inc(s_pa, 1)
                else:
                    dve.wait_ge(s_pa, n - 7)
                    nc.vector.tensor_tensor(dst, vbank[n % 2][:, :], dst, ALU.add).then_inc(s_pa, 1)

            def split_att(b, u):
                k = SPLITS * b + NCH + u
                dve.wait_ge(s_hi, k + 1)
                nc.vector.tensor_tensor(split[1][:, 1, u % 2, :], att[:, CHUNK * u:CHUNK * u + CHUNK],
                                        F(split[0][:, 1, u % 2, :]), ALU.subtract).then_inc(s_lo, 1)

            def add_masked(b, u):
                k = SPLITS * b + NCH + u
                dve.wait_ge(s_x[k % XR], 16 * (k // XR + 1))
                for oh in range(CH):
                    n = 3 * NCH + CH * u + oh
                    dve.wait_ge(s_mm, FILLS * b + n + 1)
                    dst = xr[:, k % XR, oh, :]
                    nc.vector.tensor_tensor(dst, mbank[n % 2][:, :], dst, ALU.add).then_inc(s_ed, 1)

            split_x(0, 0)
            for b in range(B):
                for c in range(NCH):
                    if c + 1 < NCH:
                        split_x(b, c + 1)
                    keep(b, c)
                for j in range(JT):
                    if JT * b + j >= 2:
                        dve.wait_ge(s_ex, JT * b + j - 1)
                    if j:
                        scaled(b, j - 1)
                    for c in range(NIC):
                        bank_max(b, j, c)
                    dve.wait_ge(s_bm, NIC * (JT * b + j + 1))
                    nc.vector.tensor_reduce(nmx[:, j % 2:j % 2 + 1], mx[:, j % 2, :], AX_X, ALU.max, negate=True).then_inc(s_mx, 1)
                    if j >= BLK:
                        for u in range(4 * (j % BLK), 4 * (j % BLK) + 4):
                            add(b, j // BLK - 1, u)
                scaled(b, JT - 1)
                for u in range(NCH + 3):
                    if u >= 3:
                        add_masked(b, u - 3)
                    if u < NCH:
                        add(b, NBLK - 1, u)
                        split_att(b, u)
                    if u == NCH and b + 1 < B:
                        split_x(b + 1, 0)


PATHS, HD = 32, 4
ALL = B * PIX
LOADW = 2048
NLOAD = ALL // LOADW
NFILL = ALL // CHUNK
PART3 = ((0, 0), (0, 1), (1, 0), (0, 2), (1, 1), (2, 0))
NCOPY = len(PART3)
KROWS = NCOPY * HD
KBIAS = 3


def squeeze_block(nc, x2, w1t, w2bd, vec128, w3r, bc3, masks, parts, wparts):
    with ExitStack() as ctx:
        def sb(name, shape, dt=F32):
            return ctx.enter_context(nc.sbuf_tensor(name, shape, dt))

        def sem(name):
            return ctx.enter_context(nc.semaphore(name))

        w1_sb = sb("w1_sb", [P, CH, P])
        w2_sb = sb("w2_sb", [P, TAPS, P])
        vec = sb("vec", [P, 6])
        w3_sb = sb("w3_sb", [P, C])
        g3_sb = sb("g3_sb", [P, 3, C])
        mk = sb("mk", [P, 2 * P])
        xc = sb("xc", [P, 2, CH, LOADW])
        y1 = sb("y1", [P, B, CELLS])
        y2 = sb("y2", [P, ALL])
        st1 = sb("st1", [P, NFILL, 6])
        st2 = sb("st2", [P, NFILL, 6])
        mv1 = sb("mv1", [P, 2])
        mv2 = sb("mv2", [P, 2])
        tiny = sb("tiny", [P, 12])
        sums = sb("sums", [P, NLOAD])
        xflat = xc[:, :, :, :].rearrange("p a h n -> p (a h n)")
        cen = xflat[:, 0:2 * CHUNK].rearrange("p (a n) -> p a n", a=2)
        yt = xflat[:, 2 * CHUNK:4 * CHUNK].rearrange("p (a n) -> p a n", a=2)
        rest = xflat[:, 4 * CHUNK:4 * CHUNK + LOADW]
        yflat = y1[:, :, :].rearrange("p b n -> p (b n)")
        yp = yflat[:, 0:3 * LOADW].bitcast(BF16).rearrange("p (a i n) -> p a i n", a=2, i=3)
        o = 3 * LOADW
        covm = yflat[:, o:o + P]
        tcov = yflat[:, o + P:o + P + C]
        tmean = yflat[:, o + P + C:o + P + 2 * C]
        s3 = yflat[:, o + P + 2 * C:o + P + 3 * C]
        a3 = yflat[:, o + P + 3 * C:o + P + 4 * C]
        b3 = yflat[:, o + P + 4 * C:o + P + 5 * C]
        o += P + 5 * C
        ap = yflat[:, o:o + 3 * C].bitcast(BF16).rearrange("p (k i n) -> p k i n", k=2, i=3)

        bank = [ctx.enter_context(nc.psum_tensor(f"qbank{i}", [P, CHUNK], F32)) for i in range(8)]

        s_w = sem("q_weights_loaded")
        s_x = [sem(f"q_x_loaded{i}") for i in range(2)]
        s_zero = sem("q_border_zeroed")
        s_c1 = sem("q_conv1_product")
        s_k1 = sem("q_conv1_kept")
        s_c2 = sem("q_conv2_product")
        s_k2 = sem("q_conv2_kept")
        s_var = sem("q_variance_ready")
        s_std = sem("q_deviation_ready")
        s_sc = sem("q_scale_ready")
        s_n1 = sem("q_y1_normalised")
        s_n2 = sem("q_y2_normalised")
        s_dv = sem("q_vector_step")
        s_mean = sem("q_mean_ready")
        s_cen = sem("q_centred")
        s_tp = sem("q_turned")
        s_tk = sem("q_turned_kept")
        s_cov = sem("q_covariance_product")
        s_p = [sem(f"q_part{i}") for i in range(3)]
        s_rest = sem("q_rest")
        s_pst = [sem(f"q_parts_stored{i}") for i in range(2)]
        s_cm = sem("q_covariance_masked")
        s_t = sem("q_cov_times_w")
        s_u = sem("q_w_cov_w")
        s_m3 = sem("q_moments3")
        s_v3 = sem("q_variance3")
        s_d3 = sem("q_deviation3")
        s_wp = sem("q_weight_parts")
        s_wst = sem("q_weight_parts_stored")
        block = ctx.enter_context(nc.Block())
        NW = 6

        @block.sync
        def _(sp):
            sp.dma_start(w1_sb[:, :, :], w1t.rearrange("(h p) m -> p h m", p=P)).then_inc(s_w, 16)
            sp.dma_start(w2_sb[:, :, :].rearrange("p k m -> p (k m)"), w2bd).then_inc(s_w, 16)
            sp.dma_start(vec[:, :], vec128).then_inc(s_w, 16)
            sp.dma_start(w3_sb[:, :], w3r).then_inc(s_w, 16)
            sp.dma_start(g3_sb[:, :, :].rearrange("p a c -> p (a c)"), bc3).then_inc(s_w, 16)
            sp.dma_start(mk[:, :], masks).then_inc(s_w, 16)
            for n in range(NLOAD):
                if n >= 2:
                    sp.wait_ge(s_c1, 4 * (n - 1))
                sp.dma_start(xc[:, n % 2, :, :], x2[:, LOADW * n:LOADW * n + LOADW].rearrange("(h p) n -> p h n", p=P)
                             ).then_inc(s_x[n % 2], 16)
            for n in range(NLOAD):
                for i in (0, 1, 2):
                    sp.wait_ge(s_p[i], n + 1)
                    for cp, (_, yi) in enumerate(PART3):
                        if yi != i:
                            continue
                        for h in range(HD):
                            sp.dma_start(parts[:, HD * cp + h, LOADW * n:LOADW * n + LOADW],
                                         yp[32 * h:32 * h + 32, n % 2, i, :]).then_inc(s_pst[n % 2], 16)
            sp.wait_ge(s_wp, 1)
            for cp, (wi, _) in enumerate(PART3):
                for h in range(HD):
                    sp.dma_start(wparts[:, HD * cp + h, :], ap[32 * h:32 * h + 32, 0, wi, :]).then_inc(s_wst, 16)
            for i in range(KBIAS):
                sp.dma_start(wparts[:, KROWS + i, :], ap[0:32, 1, i, :]).then_inc(s_wst, 16)
            sp.wait_ge(s_wst, 16 * (NCOPY * HD + KBIAS))
            for i in range(2):
                sp.wait_ge(s_pst[i], 16 * NCOPY * HD * NLOAD // 2)

        @block.gpsimd
        def _(pool):
            nc.gpsimd.memset(yflat[:, :], 0.0).then_inc(s_zero, 1)
            for n in range(NLOAD):
                src = y2[:, LOADW * n:LOADW * n + LOADW]
                if n == 0:
                    pool.wait_ge(s_c2, NFILL)
                pool.wait_ge(s_p[0], n + 1)
                if n:
                    pool.wait_ge(s_p[2], n)
                    pool.wait_ge(s_p[1], n)
                nc.gpsimd.tensor_tensor(rest, src, yp[:, n % 2, 0, :], ALU.subtract).then_inc(s_rest, 1)
                pool.wait_ge(s_p[1], n + 1)
                nc.gpsimd.tensor_tensor(yp[:, n % 2, 2, :], rest, yp[:, n % 2, 1, :], ALU.subtract).then_inc(s_p[2], 1)

        @block.tensor
        def _(pe):
            pe.wait_ge(s_w, 16 * NW)
            for n in range(NFILL):
                if n % 4 == 0:
                    pe.wait_ge(s_x[(n // 4) % 2], 16 * (n // 8 + 1))
                if n >= 4:
                    pe.wait_ge(s_k1, n - 3)
                for h in range(CH):
                    mm = nc.tensor.matmul(bank[n % 4][:, :], w1_sb[:, h, :],
                                          xc[:, (n // 4) % 2, h, CHUNK * (n % 4):CHUNK * (n % 4) + CHUNK],
                                          start=(h == 0), stop=(h == 1))
                mm.then_inc(s_c1, 1)
            for n in range(NFILL):
                b, y = n // 8, 8 * (n % 8)
                if n % 8 == 0:
                    pe.wait_ge(s_n1, b + 1)
                if n >= 4:
                    pe.wait_ge(s_k2, n - 3)
                rows = y1[:, b, :].rearrange("p (y x) -> p y x", x=PITCH)
                for k in range(TAPS):
                    mm = nc.tensor.matmul(bank[4 + n % 4][:, :], w2_sb[:, k, :],
                                          rows[:, y + k // 3:y + k // 3 + 8, k % 3:k % 3 + W],
                                          start=(k == 0), stop=(k == TAPS - 1))
                mm.then_inc(s_c2, 1)
            pe.wait_ge(s_k2, NFILL)

            def covary(n):
                pe.wait_ge(s_tk, n + 1)
                for i in range(4):
                    t = yt[:, n % 2, P * i:P * i + P]
                    mm = nc.tensor.matmul(bank[7][:, 0:P], t, t, start=(n == 0 and i == 0),
                                          stop=(n == NFILL - 1 and i == 3))
                mm.then_inc(s_cov, 1)

            for n in range(NFILL):
                pe.wait_ge(s_cen, n + 1)
                if n >= 2:
                    pe.wait_ge(s_tk, n - 1)
                for i in range(4):
                    mm = nc.tensor.transpose(bank[n % 2][:, P * i:P * i + P], cen[:, n % 2, P * i:P * i + P], mk[:, 0:P])
                mm.then_inc(s_tp, 1)
                if n:
                    covary(n - 1)
            covary(NFILL - 1)
            pe.wait_ge(s_cm, 1)
            nc.tensor.matmul(bank[2][:, 0:C], covm, w3_sb[:, :], start=True, stop=True).then_inc(s_t, 1)
            pe.wait_ge(s_u, 1)
            nc.tensor.matmul(bank[3][:, 0:C], mk[:, P:2 * P], tcov, start=True, stop=True)
            nc.tensor.matmul(bank[4][:, 0:C], mk[:, P:2 * P], tmean, start=True, stop=True).then_inc(s_m3, 1)

        @block.scalar
        def _(act):
            act.wait_ge(s_w, 16 * NW)
            act.wait_ge(s_zero, 1)
            for n in range(NFILL):
                act.wait_ge(s_c1, n + 1)
                rows = y1[:, n // 8, :].rearrange("p (y x) -> p y x", x=PITCH)
                y = 8 * (n % 8)
                nc.scalar.activation(rows[:, y + 1:y + 9, 1:W + 1], bank[n % 4][:, :].rearrange("p (y x) -> p y x", x=W),
                                     ACT.Identity, bias=vec[:, 0:1]).then_inc(s_k1, 1)
            act.wait_ge(s_var, 1)
            nc.scalar.activation(tiny[:, 1:2], tiny[:, 0:1], ACT.Sqrt).then_inc(s_std, 1)
            act.wait_ge(s_sc, 1)
            for b in range(B):
                rows = y1[:, b, :].rearrange("p (y x) -> p y x", x=PITCH)[:, 1:H + 1, 1:W + 1]
                nc.scalar.activation(rows, rows, ACT.Relu, scale=tiny[:, 2:3], bias=tiny[:, 3:4]).then_inc(s_n1, 1)
            for n in range(NFILL):
                act.wait_ge(s_c2, n + 1)
                nc.scalar.activation(y2[:, CHUNK * n:CHUNK * n + CHUNK], bank[4 + n % 4][:, :], ACT.Identity,
                                     bias=vec[:, 3:4]).then_inc(s_k2, 1)
            act.wait_ge(s_var, 2)
            nc.scalar.activation(tiny[:, 5:6], tiny[:, 4:5], ACT.Sqrt).then_inc(s_std, 1)
            act.wait_ge(s_sc, 2)
            for n in range(NLOAD):
                part = y2[:, LOADW * n:LOADW * n + LOADW]
                nc.scalar.activation(part, part, ACT.Relu, scale=tiny[:, 6:7], bias=tiny[:, 7:8],
                                     accum_out=sums[:, n:n + 1]).then_inc(s_n2, 1)

            def keep_turned(n):
                act.wait_ge(s_tp, n + 1)
                if n >= 2:
                    act.wait_ge(s_cov, n - 1)
                nc.scalar.activation(yt[:, n % 2, :], bank[n % 2][:, :], ACT.Copy).then_inc(s_tk, 1)

            for n in range(NLOAD):
                if n >= 2:
                    act.wait_ge(s_pst[n % 2], 16 * NCOPY * HD * (n // 2))
                act.wait_ge(s_n2, n + 1)
                nc.scalar.activation(yp[:, n % 2, 0, :], y2[:, LOADW * n:LOADW * n + LOADW], ACT.Copy).then_inc(s_p[0], 1)
                for i in range(4):
                    keep_turned(4 * n + i)
                act.wait_ge(s_rest, n + 1)
                nc.scalar.activation(yp[:, n % 2, 1, :], rest, ACT.Copy).then_inc(s_p[1], 1)
            act.wait_ge(s_v3, 1)
            nc.scalar.activation(s3, tcov, ACT.Sqrt).then_inc(s_d3, 1)

        @block.vector
        def _(dve):
            steps = [0]

            def link(ins):
                steps[0] += 1
                ins.then_inc(s_dv, 1)
                dve.wait_ge(s_dv, steps[0])

            def norm(n, st, mv, g, be):
                o = 4 * n
                link(nc.vector.memset(tiny[:, o:o + 1], 0.0))
                link(nc.vector.bn_aggr(mv[:, :], st[:, :, :].rearrange("p g s -> p (g s)")))
                nc.vector.tensor_scalar(tiny[:, o:o + 1], mv[:, 1:2], EPS, None, ALU.add).then_inc(s_var, 1)
                dve.wait_ge(s_std, n + 1)
                link(nc.vector.reciprocal(tiny[:, 8:9], tiny[:, o + 1:o + 2]))
                link(nc.vector.tensor_tensor(tiny[:, o + 2:o + 3], tiny[:, 8:9], vec[:, g:g + 1], ALU.mult))
                link(nc.vector.tensor_tensor(tiny[:, 9:10], mv[:, 0:1], tiny[:, o + 2:o + 3], ALU.mult))
                nc.vector.tensor_tensor(tiny[:, o + 3:o + 4], vec[:, be:be + 1], tiny[:, 9:10], ALU.subtract).then_inc(s_sc, 1)

            dve.wait_ge(s_w, 16 * NW)
            for n in range(NFILL):
                dve.wait_ge(s_k1, n + 1)
                rows = y1[:, n // 8, :].rearrange("p (y x) -> p y x", x=PITCH)
                y = 8 * (n % 8)
                nc.vector.bn_stats(st1[:, n, :], rows[:, y + 1:y + 9, 1:W + 1])
            norm(0, st1, mv1, 1, 2)
            for n in range(NFILL):
                dve.wait_ge(s_k2, n + 1)
                nc.vector.bn_stats(st2[:, n, :], y2[:, CHUNK * n:CHUNK * n + CHUNK])
            norm(1, st2, mv2, 4, 5)
            dve.wait_ge(s_n2, NLOAD)
            link(nc.vector.reduce_sum(tiny[:, 10:11], sums[:, :], AX_X))
            link(nc.vector.tensor_scalar(tiny[:, 11:12], tiny[:, 10:11], 1.0 / ALL, None, ALU.mult))
            for n in range(NFILL):
                if n >= 2:
                    dve.wait_ge(s_tp, n - 1)
                nc.vector.tensor_scalar(cen[:, n % 2, :], y2[:, CHUNK * n:CHUNK * n + CHUNK], tiny[:, 11:12], None,
                                        ALU.subtract).then_inc(s_cen, 1)
            dve.wait_ge(s_cov, NFILL)
            nc.vector.scalar_tensor_tensor(out=covm, in0=bank[7][:, 0:P], scalar=1.0 / ALL, in1=mk[:, P:2 * P],
                                           op0=ALU.mult, op1=ALU.mult).then_inc(s_cm, 1)
            nc.vector.tensor_scalar(tmean, w3_sb[:, :], tiny[:, 11:12], None, ALU.mult)
            dve.wait_ge(s_t, 1)
            nc.vector.tensor_tensor(tcov, bank[2][:, 0:C], w3_sb[:, :], ALU.mult).then_inc(s_u, 1)
            dve.wait_ge(s_m3, 1)
            nc.vector.tensor_scalar(tcov, bank[3][:, 0:C], EPS, None, ALU.add).then_inc(s_v3, 1)
            link(nc.vector.tensor_tensor(tmean, bank[4][:, 0:C], g3_sb[:, 2, :], ALU.add))
            link(nc.vector.tensor_tensor(b3, g3_sb[:, 2, :], tmean, ALU.subtract))
            dve.wait_ge(s_d3, 1)
            link(nc.vector.reciprocal(a3, s3))
            link(nc.vector.tensor_tensor(s3, a3, g3_sb[:, 0, :], ALU.mult))
            link(nc.vector.tensor_tensor(a3, w3_sb[:, :], s3, ALU.mult))
            link(nc.vector.tensor_tensor(tmean, b3, s3, ALU.mult))
            link(nc.vector.tensor_tensor(b3, tmean, g3_sb[:, 1, :], ALU.add))
            for k, v in enumerate((a3, b3)):
                link(nc.vector.tensor_copy(ap[:, k, 0, :], v))
                link(nc.vector.tensor_tensor(s3, v, ap[:, k, 0, :], ALU.subtract))
                link(nc.vector.tensor_copy(ap[:, k, 1, :], s3))
                ins = nc.vector.tensor_tensor(ap[:, k, 2, :], s3, ap[:, k, 1, :], ALU.subtract)
                if k == 0:
                    link(ins)
            ins.then_inc(s_wp, 1)


TILE = 1024
NT = ALL // TILE
UNITS = 2 * PATHS
SLOTS = 4
TMPS = 4


def by_pool(path):
    return path % 3 == 1


def expand_block(nc, x2, parts, wparts, total, st4):
    with ExitStack() as ctx:
        def sb(name, shape, dt=F32):
            return ctx.enter_context(nc.sbuf_tensor(name, shape, dt))

        def sem(name):
            return ctx.enter_context(nc.semaphore(name))

        wl = sb("wl", [P, PATHS // 4, C], BF16)
        yv = sb("yv", [P, 2, PATHS // 4, TILE], BF16)
        acc = sb("acc", [P, 2, CH, TILE])
        tmp = sb("tmp", [P, TMPS, TILE])
        slot = [ctx.enter_context(nc.psum_tensor(f"slot{i}", [P, TILE], F32)) for i in range(SLOTS)]

        s_w = sem("e_weights_loaded")
        s_one = sem("e_ones_set")
        s_y = [sem(f"e_parts_loaded{i}") for i in range(2)]
        s_x = [sem(f"e_x_loaded{i}") for i in range(2)]
        s_z = sem("e_product")
        s_vec = sem("e_added_by_vector")
        s_rel = sem("e_rectified")
        s_pool = sem("e_added_by_pool")
        s_mrg = sem("e_merged")
        block = ctx.enter_context(nc.Block())

        NV = 2 * sum(not by_pool(p) for p in range(PATHS))
        NP = 2 * sum(by_pool(p) for p in range(PATHS))
        first = [p for p in range(PATHS) if not by_pool(p)][0]
        MERGE = 6
        vec_before = [2 * sum(not by_pool(q) for q in range(p)) for p in range(PATHS)]
        pool_before = [2 * sum(by_pool(q) for q in range(p)) for p in range(PATHS)]

        @block.sync
        def _(sp):
            for pq in range(4):
                sp.dma_start(wl[32 * pq:32 * pq + KROWS + KBIAS, :, :],
                             wparts.rearrange("(q r) k c -> r k q c", r=4)[pq]).then_inc(s_w, 16)
            sp.wait_ge(s_one, 1)

            def load(t, a):
                src = parts.rearrange("(q r) k n -> r k q n", r=4)
                for pq in range(4):
                    sp.dma_start(yv[32 * pq:32 * pq + KROWS, a, :, :],
                                 src[pq, :, :, bass.ds(TILE * t, TILE)]).then_inc(s_y[a], 16)
                sp.dma_start(acc[:, a, :, :], x2.rearrange("(h p) n -> p h n", p=P)[:, :, bass.ds(TILE * t, TILE)]).then_inc(s_x[a], 16)

            load(0, 0)
            load(1, 1)
            with sp.Fori(1, NT // 2) as it:
                for a in range(2):
                    sp.wait_ge(s_z, UNITS * (2 * it + a - 1))
                    sp.nop(nofuse=True)
                    sp.wait_ge(s_mrg, 2 * (2 * it + a - 1))
                    sp.nop(nofuse=True)
                    load(2 * it + a, a)

        @block.tensor
        def _(pe):
            pe.wait_ge(s_w, 64)

            def tile(t, a, start):
                pe.wait_ge(s_y[a], 64 * ((t - a) // 2 + 1) if isinstance(t, int) else 32 * (t - a) + 64)
                for p in range(PATHS):
                    for h in range(CH):
                        u = 2 * p + h
                        v = (u - SLOTS) % UNITS
                        vp, tt = v // 2, (t if u >= SLOTS else t - 1)
                        if not (start and u < SLOTS):
                            if by_pool(vp):
                                pe.wait_ge(s_rel, NP * tt + pool_before[vp] + v % 2 + 1)
                            else:
                                pe.wait_ge(s_vec, NV * tt + vec_before[vp] + v % 2 + 1)
                        r = slice(32 * (p % 4), 32 * (p % 4) + KROWS + KBIAS)
                        for c in range(TILE // CHUNK):
                            mm = nc.tensor.matmul(slot[u % SLOTS][:, CHUNK * c:CHUNK * c + CHUNK],
                                                  wl[r, p // 4, h * P:(h + 1) * P],
                                                  yv[r, a, p // 4, CHUNK * c:CHUNK * c + CHUNK], start=True, stop=True)
                        mm.then_inc(s_z, 1)

            tile(0, 0, True)
            tile(1, 1, False)
            with pe.Fori(1, NT // 2) as it:
                for a in range(2):
                    tile(2 * it + a, a, False)

        @block.scalar
        def _(act):
            def tile(t, a, start):
                for p in range(PATHS):
                    if not by_pool(p):
                        continue
                    for h in range(CH):
                        n = pool_before[p] + h
                        act.wait_ge(s_z, UNITS * t + 2 * p + h + 1)
                        if not (start and n < TMPS):
                            act.wait_ge(s_pool, NP * t + n + 1 - TMPS)
                        nc.scalar.activation(tmp[:, (NP * a + n) % TMPS, :], slot[(2 * p + h) % SLOTS][:, :],
                                             ACT.Relu).then_inc(s_rel, 1)

            tile(0, 0, True)
            tile(1, 1, False)
            with act.Fori(1, NT // 2) as it:
                for a in range(2):
                    tile(2 * it + a, a, False)

        @block.gpsimd
        def _(pool):
            nc.gpsimd.memset(yv[:, :, :, :].rearrange("p a q n -> p (a q n)"), 1.0).then_inc(s_one, 1)

            def tile(t, a, start):
                pool.wait_ge(s_x[a], 16 * ((t - a) // 2 + 1) if isinstance(t, int) else 8 * (t - a) + 16)
                for n in range(NP):
                    pool.wait_ge(s_rel, NP * t + n + 1)
                    if n >= 2:
                        pool.wait_ge(s_pool, NP * t + n - 1)
                    nc.gpsimd.tensor_tensor(acc[:, a, n % 2, :], tmp[:, (NP * a + n) % TMPS, :], acc[:, a, n % 2, :],
                                            ALU.add).then_inc(s_pool, 1)

            tile(0, 0, True)
            tile(1, 1, False)
            with pool.Fori(1, NT // 2) as it:
                for a in range(2):
                    tile(2 * it + a, a, False)

        @block.vector
        def _(dve):
            def here(t, h, c0=0, n=TILE):
                return total[:, h, bass.ds(TILE * t + c0, n)]

            def merge(t, a):
                dve.wait_ge(s_pool, NP * (t + 1))
                dve.wait_ge(s_vec, NV * (t + 1))
                for h in range(CH):
                    nc.vector.tensor_tensor(here(t, h), here(t, h), acc[:, a, h, :], ALU.add).then_inc(s_mrg, 1)
                dve.wait_ge(s_mrg, 2 * (t + 1))
                for h in range(CH):
                    for c in range(TILE // CHUNK):
                        at = TILE // CHUNK * t + c
                        out = st4[:, h, at, :] if isinstance(at, int) else st4[:, h, bass.ds(at, 1), :].rearrange(
                            "p a s -> p (a s)")
                        nc.vector.bn_stats(out, here(t, h, CHUNK * c, CHUNK))

            def tile(t, a, start):
                i = 0
                for p in range(PATHS):
                    if by_pool(p):
                        continue
                    for h in range(CH):
                        if i == MERGE and not start:
                            merge(t - 1, 1 - a)
                        u = 2 * p + h
                        dve.wait_ge(s_z, UNITS * t + u + 1)
                        z = slot[u % SLOTS][:, :]
                        if p == first:
                            ins = nc.vector.tensor_scalar(here(t, h), z, 0.0, None, ALU.max)
                        else:
                            dve.wait_ge(s_vec, NV * t + i - 1)
                            ins = nc.vector.scalar_tensor_tensor(out=here(t, h), in0=z, scalar=0.0, in1=here(t, h),
                                                                 op0=ALU.max, op1=ALU.add)
                        ins.then_inc(s_vec, 1)
                        i += 1

            tile(0, 0, True)
            tile(1, 1, False)
            with dve.Fori(1, NT // 2) as it:
                for a in range(2):
                    tile(2 * it + a, a, False)
            merge(NT - 1, 1)


SC = 1024


def sequence_block(nc, total, st4, vec256, out):
    with ExitStack() as ctx:
        def sb(name, shape, dt=F32):
            return ctx.enter_context(nc.sbuf_tensor(name, shape, dt))

        def sem(name):
            return ctx.enter_context(nc.semaphore(name))

        vec = sb("seq_vec", [P, 6, CH])
        mv = sb("seq_mv", [P, CH, 2])
        sm = sb("seq_sm", [P, 10, CH])
        v = sb("seq_v", [P, 2, PIX + 2])
        u = sb("seq_u", [P, 2, PIX])
        keep = sb("seq_keep", [P, SC])
        s_w = sem("r_vectors_loaded")
        s_dv = sem("r_vector_step")
        s_var = sem("r_variance")
        s_std = sem("r_deviation")
        s_sc = sem("r_scales")
        s_edge = sem("r_edges_zeroed")
        s_v = sem("r_normalised")
        s_u = sem("r_tenth")
        s_c = sem("r_middle")
        s_e = sem("r_average_part")
        s_t = sem("r_taps")
        s_sum = sem("r_summed")
        s_out = sem("r_stored")
        block = ctx.enter_context(nc.Block())
        rows = [(h, b) for b in range(B) for h in range(CH)]
        NSC = PIX // SC

        @block.sync
        def _(sp):
            sp.dma_start(vec[:, :, :].rearrange("p a h -> p (a h)"), vec256).then_inc(s_w, 16)
            for r, (h, b) in enumerate(rows):
                sp.wait_ge(s_sum, r + 1)
                sp.dma_start(out[b, h * P:(h + 1) * P, :], total[:, h, PIX * b:PIX * b + PIX]).then_inc(s_out, 16)
            sp.wait_ge(s_out, 16 * len(rows))

        @block.gpsimd
        def _(pool):
            nc.gpsimd.memset(v[:, :, 0:1], 0.0).then_inc(s_edge, 1)
            nc.gpsimd.memset(v[:, :, PIX + 1:PIX + 2], 0.0).then_inc(s_edge, 1)
            nc.gpsimd.memset(keep[:, :], 0.9).then_inc(s_edge, 1)
            for r, (h, b) in enumerate(rows):
                pool.wait_ge(s_e, NSC * (r + 1))
                pool.wait_ge(s_t, 2 * (r + 1))
                dst = total[:, h, PIX * b:PIX * b + PIX]
                nc.gpsimd.tensor_tensor(dst, dst, u[:, r % 2, :], ALU.add).then_inc(s_sum, 1)

        @block.scalar
        def _(act):
            act.wait_ge(s_var, 1)
            nc.scalar.activation(sm[:, 1, :], sm[:, 0, :], ACT.Sqrt).then_inc(s_std, 1)
            act.wait_ge(s_sc, 1)
            for r, (h, b) in enumerate(rows):
                src = total[:, h, PIX * b:PIX * b + PIX]
                if r >= 2:
                    act.wait_ge(s_t, 2 * (r - 1))
                nc.scalar.activation(v[:, r % 2, 1:PIX + 1], src, ACT.Identity, scale=sm[:, 2, h:h + 1],
                                     bias=sm[:, 3, h:h + 1]).then_inc(s_v, 1)
                if r >= 2:
                    act.wait_ge(s_sum, r - 1)
                nc.scalar.activation(u[:, r % 2, :], src, ACT.Identity, scale=sm[:, 4, h:h + 1],
                                     bias=sm[:, 5, h:h + 1]).then_inc(s_u, 1)
                nc.scalar.activation(src, src, ACT.Identity, scale=sm[:, 6, h:h + 1],
                                     bias=sm[:, 7, h:h + 1]).then_inc(s_c, 1)

        @block.vector
        def _(dve):
            steps = [0]

            def link(ins):
                steps[0] += 1
                ins.then_inc(s_dv, 1)
                dve.wait_ge(s_dv, steps[0])

            dve.wait_ge(s_w, 16)
            link(nc.vector.memset(sm[:, :, :].rearrange("p a h -> p (a h)"), 0.0))
            for h in range(CH):
                ins = nc.vector.bn_aggr(mv[:, h, :], st4[:, h, :, :].rearrange("p g s -> p (g s)"))
            link(ins)
            nc.vector.tensor_scalar(sm[:, 0, :], mv[:, :, 1], EPS, None, ALU.add).then_inc(s_var, 1)
            dve.wait_ge(s_std, 1)
            link(nc.vector.reciprocal(sm[:, 8, :], sm[:, 1, :]))
            link(nc.vector.tensor_tensor(sm[:, 2, :], sm[:, 8, :], vec[:, 0, :], ALU.mult))
            link(nc.vector.tensor_tensor(sm[:, 9, :], mv[:, :, 0], sm[:, 2, :], ALU.mult))
            link(nc.vector.tensor_tensor(sm[:, 3, :], vec[:, 1, :], sm[:, 9, :], ALU.subtract))
            link(nc.vector.tensor_scalar(sm[:, 4:6, :], sm[:, 2:4, :], 0.1, None, ALU.mult))
            link(nc.vector.tensor_scalar(sm[:, 8, :], vec[:, 3, :], 1.0, None, ALU.add))
            link(nc.vector.tensor_tensor(sm[:, 6, :], sm[:, 2, :], sm[:, 8, :], ALU.mult))
            link(nc.vector.tensor_tensor(sm[:, 9, :], sm[:, 3, :], sm[:, 8, :], ALU.mult))
            nc.vector.tensor_tensor(sm[:, 7, :], sm[:, 9, :], vec[:, 5, :], ALU.add).then_inc(s_sc, 1)
            dve.wait_ge(s_edge, 3)
            for r, (h, b) in enumerate(rows):
                dst = total[:, h, PIX * b:PIX * b + PIX]
                a = r % 2
                dve.wait_ge(s_u, r + 1)
                for c in range(NSC):
                    part = u[:, a, SC * c:SC * c + SC]
                    if c:
                        dve.wait_ge(s_e, NSC * r + c)
                    start = u[:, a, SC * c - 1:SC * c] if c else v[:, a, 1:2]
                    nc.vector.tensor_tensor_scan(part, keep[:, :], part, start, ALU.mult, ALU.add).then_inc(s_e, 1)
                dve.wait_ge(s_c, r + 1)
                for i, (tap, at) in enumerate(((2, 0), (4, 2))):
                    if i:
                        dve.wait_ge(s_t, 2 * r + 1)
                    nc.vector.scalar_tensor_tensor(out=dst, in0=v[:, a, at:at + PIX], scalar=vec[:, tap, h:h + 1], in1=dst,
                                                   op0=ALU.mult, op1=ALU.add).then_inc(s_t, 1)


def layer23(nc, x2, a, parts, wparts, out):
    squeeze_block(nc, x2, a["w1t"], a["w2bd"], a["vec128"], a["w3r"], a["bc3"], a["masks"], parts, wparts)
    with ExitStack() as ctx:
        total = ctx.enter_context(nc.sbuf_tensor("total", [P, CH, ALL], F32))
        st4 = ctx.enter_context(nc.sbuf_tensor("st4", [P, CH, NFILL, 6], F32))
        expand_block(nc, x2, parts, wparts, total, st4)
        sequence_block(nc, total, st4, a["vec256"], out)


def host0(inputs):
    f = np.float32
    out = {"x": inputs["x"].reshape(B, C, PIX)}
    for l in range(2):
        n = str(l + 1)
        out[f"wdc{l}"] = np.ascontiguousarray(
            inputs["L0_conv_w_dc" + n].reshape(C, C, TAPS).transpose(1, 2, 0)).reshape(C, TAPS * C)
        w = np.concatenate([inputs["L0_conv_w_tm" + n], inputs["L0_conv_w_tr" + n]]).reshape(NOFF, C, TAPS)
        out[f"woff{l}"] = np.ascontiguousarray(w.transpose(1, 2, 0)).reshape(C, NPART)
        out[f"boff{l}"] = np.concatenate([inputs["L0_conv_b_tm" + n], inputs["L0_conv_b_tr" + n]]).reshape(NOFF, 1)
    gb = np.stack([np.stack([inputs[f"L0_conv_g{n}"], inputs[f"L0_conv_be{n}"]]) for n in (1, 2)])
    out["gb"] = np.ascontiguousarray(gb.reshape(2, 2, CH, P).transpose(3, 0, 1, 2)).reshape(P, 4 * CH)
    c = np.zeros((P, 2 * P + NPOS + NTILE * NPOS), f)
    c[:, 0:P] = np.eye(P, dtype=f)
    c[:, P:2 * P] = np.kron(np.eye(P // GN_GROUP, dtype=f), np.full((GN_GROUP, GN_GROUP), 1 / GN_GROUP, f))
    for k in range(TAPS):
        ry, rx = k // 3 - 1, k % 3 - 1
        for tap in range(TAPS):
            for o, col, v in ((0, k, ry), (1, k, rx), (4, k, 1), (2, TAPS + k, ry), (3, TAPS + k, rx), (5, TAPS + k, 1)):
                c[NOFF * tap + o, 2 * P + col] = v
    at = c[:, 2 * P + NPOS:].reshape(P, NTILE, 2, TAPS)
    at[:, :, 0, :] = (2 * np.arange(NTILE)[None, :, None] + (np.arange(P) // W)[:, None, None])
    at[:, :, 1, :] = (np.arange(P) % W)[:, None, None]
    out["consts"] = c
    return out


def host1(inputs):
    w = np.concatenate([inputs["L1_conv_w_theta"], inputs["L1_conv_w_phi"], inputs["L1_conv_w_g"]])
    return {"wproj": np.ascontiguousarray(w.T), "wmask": np.ascontiguousarray(inputs["L1_conv_w_mask"].T)}


def host2(inputs):
    f = np.float32
    hp = lambda a: np.ascontiguousarray(a.reshape(PATHS, HD, *a.shape[1:]).swapaxes(0, 1)).reshape(a.shape)
    g = lambda n: inputs["L2_conv_" + n]
    out = {"w1t": np.ascontiguousarray(g("w1").T)}
    w2 = g("w2").reshape(PATHS, HD, HD, TAPS)
    bd = np.zeros((PATHS, HD, TAPS, HD, PATHS), f)
    for p in range(PATHS):
        bd[p, :, :, :, p] = w2[p].transpose(1, 2, 0)
    out["w2bd"] = bd.reshape(P, TAPS * P)
    out["vec128"] = np.ascontiguousarray(np.stack(
        [g("b1"), g("g1"), g("be1"), hp(g("b2")), hp(g("g2")), hp(g("be2"))], axis=1))
    out["w3r"] = np.ascontiguousarray(g("w3").transpose(2, 0, 1)).reshape(P, C)
    bc = np.stack([g("g3"), g("be3"), g("b3")], axis=1)
    out["bc3"] = np.ascontiguousarray(np.broadcast_to(bc[None], (HD, PATHS, 3, C))).reshape(P, 3 * C)
    out["masks"] = np.concatenate([np.eye(P, dtype=f), np.kron(np.ones((HD, HD), f), np.eye(PATHS, dtype=f))], axis=1)
    k = inputs["L3_conv_conv_w"].reshape(C, 3)
    v = np.stack([g("g4"), g("be4"), k[:, 0], k[:, 1], k[:, 2], inputs["L3_conv_conv_b"]])
    out["vec256"] = np.ascontiguousarray(v.reshape(6, CH, P).transpose(2, 0, 1)).reshape(P, 6 * CH)
    return out


def build(nc, a, out):
    table = [nc.dram_tensor(f"table{b}", (CELLS, PATCH), F32).ap() for b in range(B)]
    x1 = nc.dram_tensor("x1", (B, C, PIX), F32).ap()
    x2 = nc.dram_tensor("x2", (C, ALL), F32).ap()
    parts = nc.dram_tensor("parts", (PATHS, KROWS, ALL), BF16).ap()
    wparts = nc.dram_tensor("wparts", (PATHS, KROWS + KBIAS, C), BF16).ap()
    deformable_block(nc, a["x"], [a["wdc0"], a["wdc1"]], [a["woff0"], a["woff1"]], [a["boff0"], a["boff1"]],
                     a["gb"], table, x1, a["consts"])
    attention_block(nc, x1, a["wproj"], a["wmask"], x2)
    layer23(nc, x2, a, parts, wparts, out)


def kernel(**inputs):
    import concourse.bacc as bacc
    from concourse.bass_utils import run_bass_kernel_spmd

    inputs = {k: np.asarray(v) for k, v in inputs.items()}
    arrays = {**host0(inputs), **host1(inputs), **host2(inputs)}
    nc = bacc.Bacc("TRN2", target_bir_lowering=False, num_devices=1)
    args = {n: nc.dram_tensor(n, v.shape, mybir.dt.from_np(v.dtype), kind="ExternalInput").ap() for n, v in arrays.items()}
    out = nc.dram_tensor("out", (B, C, PIX), F32, kind="ExternalOutput").ap()
    build(nc, args, out)
    r = run_bass_kernel_spmd(nc, [arrays], core_ids=[0])
    return r.results[0]["out"].reshape(B, C, H, W)
```

```python
from contextlib import ExitStack

import numpy as np

import concourse.bass as bass
from concourse import mybir

ALU = mybir.AluOpType
ACT = mybir.ActivationFunctionType
F32 = mybir.dt.float32
I32 = mybir.dt.int32
BF16 = mybir.dt.bfloat16

B, C, H, W = 4, 256, 64, 64
P = 128
CH = C // P
PIX = H * W
TAPS = 9
PITCH = W + 2
CELLS = PITCH * (H + 2)
PATCH = 4 * C
NTILE = PIX // P
GN_GROUP = 8
EPS = 1e-5
NOFF = 6
NPART = TAPS * NOFF
NPOS = 2 * TAPS

GROUP_TILES = 2
GROUP = GROUP_TILES * P
NGROUP = PIX // GROUP
GS = GROUP_TILES * TAPS
NS = NTILE * TAPS
SRING = 6
TRING = 3
IDX_AFTER = (4, 10, 16)
RESIDUAL_AT = ((0, 1, 12), (0, 1, 14), (1, 0, 8), (1, 1, 4))
NORMALISE_AT = ((0, 1, 15), (0, 1, 17), (1, 0, 12), (1, 1, 8))
LAG = 3


def order_of_phases():
    seq = [("P", 0, b) for b in range(B)]
    for b in range(B):
        seq.append(("G", 0, b))
        if b:
            seq.append(("P", 1, b - 1))
    seq.append(("P", 1, B - 1))
    return seq + [("G", 1, b) for b in range(B)]


def deformable_block(nc, x, wdc, woff, boff, gamma_beta, table, x1, consts):
    seq = order_of_phases()
    ordinal = {}
    for kind in "PG":
        for n, ph in enumerate([ph for ph in seq if ph[0] == kind]):
            ordinal[ph] = n
    loads = {ph: n for n, ph in enumerate([ph for ph in seq if ph[:2] in (("P", 0), ("G", 1))])}

    def previous(ph):
        n = seq.index(ph)
        return seq[n - 1] if n else None

    def following(ph):
        n = seq.index(ph) + 1
        return seq[n] if n < len(seq) else None

    def ended_by(ph):
        prev = previous(ph)
        return prev if prev and prev[0] == "G" else None

    def before(ph, kind):
        return sum(q[0] == kind for q in seq[:seq.index(ph)])

    with ExitStack() as ctx:
        def sb(name, shape, dt=F32):
            return ctx.enter_context(nc.sbuf_tensor(name, shape, dt))

        def sem(name):
            return ctx.enter_context(nc.semaphore(name))

        ident = sb("ident", [P, P])
        gavg = sb("gavg", [P, P])
        sel = sb("sel", [P, NPOS])
        posbase = sb("posbase", [P, NTILE, NPOS])
        wdc_sb = sb("wdc_sb", [P, CH, TAPS, C])
        woff_sb = sb("woff_sb", [P, 2, CH, NPART])
        boff_sb = sb("boff_sb", [NPART, 2])
        gb_sb = sb("gb_sb", [P, 2, 2, CH])
        eps_sb = sb("eps_sb", [P, 1])
        image = [sb(f"image{i}", [P, CH, PIX]) for i in range(2)]
        turned = sb("turned", [P, 2, 4, C])
        pos = sb("pos", [P, NTILE, NPOS])
        posi = sb("posi", [P, NTILE, NPOS], I32)
        low = sb("low", [P, NTILE, NPOS])
        over = sb("over", [P, NTILE, NPOS])
        idxf = sb("idxf", [P, NTILE, TAPS])
        idx = sb("idx", [P, B, NTILE, TAPS], I32)
        wgt = sb("wgt", [P, B, NTILE, TAPS, 4])
        patch = sb("patch", [P, TAPS, PATCH])
        idx_now = sb("idx_now", [P, 2, TAPS], I32)
        wgt_now = sb("wgt_now", [P, 2, TAPS, 4])
        blend = sb("blend", [P, SRING, C])
        cols = sb("cols", [P, 2, CH, TAPS, GROUP])
        cols_flat = cols[:, :, :, :, :].rearrange("p a h k q -> p a (h k q)")
        part = cols_flat[:, 0, :]
        aligned = cols_flat[:, 1, :]
        stats = sb("stats", [P, CH, NGROUP, 6])
        mv = sb("mv", [P, CH, 2])
        mom = sb("mom", [P, 2, CH])
        gstat = sb("gstat", [P, 2, CH])
        small = sb("small", [P, 4, CH])
        scale = sb("scale", [P, CH])
        shift = sb("shift", [P, CH])

        bank = [ctx.enter_context(nc.psum_tensor(f"bank{i}", [P, 512], F32)) for i in range(8)]
        tbank = bank[0:TRING]
        obank = bank[3:5]
        partbank = bank[5:7]
        turnbank = [bank[7], bank[2]]
        posbank = bank[5:7]
        gnbank = bank[6]

        def buffer_of(ph):
            return image[0] if ph[:2] == ("G", 1) else image[ph[2] % 2]

        quarters = [(h, at) for at in (0, PIX // 2) for h in range(CH)]

        s_const = sem("const_loaded")
        s_w = sem("wdc_loaded")
        s_border = sem("table_border_written")
        s_x = [sem(f"x_loaded{i}") for i in range(2)]
        s_tab = [sem(f"table_written{i}") for i in range(2)]
        s_aln = sem("partials_aligned")
        s_gat = [sem(f"patch_gathered{k}") for k in range(TAPS)]
        s_out = sem("x1_stored")
        s_zero = sem("part_border_zeroed")
        s_pmm = sem("part_product")
        s_pev = sem("part_emptied")
        s_tmm = sem("turned_product")
        s_tev = sem("turned_emptied")
        s_posmm = sem("pos_product")
        s_dv = sem("vector_step")
        s_idx = sem("indices_ready")
        s_ic = sem("idx_copied")
        s_wc = sem("wgt_copied")
        s_mul = sem("corner0_weighted")
        s_st = sem("corner_added")
        s_blend = sem("blend_ready")
        s_tr = sem("sample_transposed")
        s_cols = sem("columns_ready")
        s_cv = sem("conv_product")
        s_oev = sem("conv_emptied")
        s_agg = sem("channel_moments")
        s_gn = sem("group_moments")
        s_var = sem("variance_ready")
        s_std = sem("deviation_ready")
        s_sc = sem("scale_ready")
        s_norm = sem("image_normalised")
        s_res = sem("residual_added")

        NCONST = 9
        block = ctx.enter_context(nc.Block())

        @block.sync
        def _(sp):
            zero = cols_flat
            o = 0
            sp.dma_start(ident[:, :], consts[:, 0:P]).then_inc(s_const, 16)
            sp.dma_start(gavg[:, :], consts[:, P:2 * P]).then_inc(s_const, 16)
            sp.dma_start(sel[:, :], consts[:, 2 * P:2 * P + NPOS]).then_inc(s_const, 16)
            sp.dma_start(posbase[:, :, :], consts[:, 2 * P + NPOS:2 * P + NPOS + NTILE * NPOS].rearrange(
                "p (t n) -> p t n", t=NTILE)).then_inc(s_const, 16)
            for l in range(2):
                sp.dma_start(woff_sb[:, l, :, :], woff[l].rearrange("(h p) m -> p h m", p=P)).then_inc(s_const, 16)
            sp.dma_start(gb_sb[:, :, :, :].rearrange("p l g h -> p (l g h)"), gamma_beta).then_inc(s_const, 16)

            def load_x(ph):
                n = loads[ph]
                if ph[1]:
                    if ph[2] == 0:
                        sp.wait_ge(s_tmm, 16 * 2 * B)
                        sp.wait_ge(s_pmm, 8 * 2 * B)
                    else:
                        sp.wait_ge(s_out, 16 * 4 * ph[2])
                    dst = image[1]
                else:
                    if n >= 2:
                        sp.wait_ge(s_tmm, 16 * (n - 1))
                        sp.wait_ge(s_pmm, 8 * (n - 1))
                    dst = buffer_of(ph)
                sp.dma_start(dst[:, :, :], x[ph[2]].rearrange("(h p) n -> p h n", p=P)).then_inc(s_x[n % 2], 16)

            sp.wait_ge(s_zero, 1)
            for l in range(2):
                sp.dma_start(boff_sb[4 * NOFF:5 * NOFF, l:l + 1], boff[l]).then_inc(s_const, 16)
            load_x(seq[0])
            load_x(seq[1])
            sp.wait_ge(s_zero, 2)
            for b in range(B):
                t = table[b].rearrange("(y x) n -> y x n", y=H + 2)
                sp.dma_start(t[:, W + 1, :], zero[0:H + 2, 0, 0:PATCH]).then_inc(s_border, 16)
                for col, side in ((0, 0), (W, 1)):
                    sp.dma_start(t[:, col, :].rearrange("y (r c n) -> y r c n", r=2, c=2)[:, :, side, :],
                                 zero[0:H + 2, 0, 0:2 * C].rearrange("p (r n) -> p r n", r=2)).then_inc(s_border, 16)
                for row, r in ((0, 0), (H, 1), (H + 1, 0), (H + 1, 1)):
                    for side in range(2):
                        lo = (2 * r + side) * C
                        sp.dma_start(t[row, 1 - side:1 - side + W, lo:lo + C], zero[0:W, 0, 0:C]).then_inc(s_border, 16)

            for ph in seq:
                kind, l, b = ph
                if kind == "P":
                    n = ordinal[ph]
                    t = table[b].rearrange("(y x) n -> y x n", y=H + 2)
                    for bt in range(8):
                        sp.wait_ge(s_tev, 16 * n + 2 * bt + 2)
                        for hp in range(2):
                            y = 8 * bt + hp
                            for r in range(2):
                                for c in range(2):
                                    sp.dma_start(
                                        t[y + 1 - r:y + 1 - r + 7:2, 1 - c:1 - c + W,
                                          (2 * r + c) * C:(2 * r + c + 1) * C].rearrange("y x n -> x y n"),
                                        turned[64 * hp:64 * hp + 64, bt % 2, :, :]).then_inc(s_tab[bt % 2], 16)
                    if l == 0 and b + 2 < B:
                        load_x(("P", 0, b + 2))
                    if l == 1 and b == B - 1:
                        load_x(("G", 1, 0))
                else:
                    n = ordinal[ph]
                    if b == 0:
                        if l:
                            sp.wait_ge(s_cv, 2 * NGROUP * n)
                        sp.dma_start(wdc_sb[:, :, :, :].rearrange("p h k o -> p h (k o)"),
                                     wdc[l].rearrange("(h p) m -> p h m", p=P)).then_inc(s_w, 16)
                    if l:
                        for c, (h, at) in enumerate(quarters):
                            sp.wait_ge(s_norm, 4 * n + c + 1)
                            sp.dma_start(x1[b, h * P:(h + 1) * P, at:at + PIX // 2],
                                         image[1][:, h, at:at + PIX // 2]).then_inc(s_out, 16)
                        if b + 1 < B:
                            load_x(("G", 1, b + 1))
            sp.wait_ge(s_out, 16 * 4 * B)

        @block.gpsimd
        def _(pool):
            pool.wait_ge(s_border, 16 * 44)

            def tile(ph, t, tt, skip):
                q, b = ordinal[ph], ph[2]
                nc.gpsimd.tensor_copy(idx_now[:, tt, :], idx[:, b, t, :] if isinstance(t, int) else
                                      idx[:, b, bass.ds(t, 1), :].rearrange("p a k -> p (a k)")).then_inc(s_ic, 1)
                pool.wait_ge(s_ic, NTILE * q + t + 1)
                pool.nop(nofuse=True)
                for k in range(TAPS):
                    if not skip:
                        pool.wait_ge(s_blend, NS * q + 9 * t + k - 8)
                        pool.nop(nofuse=True)
                    nc.gpsimd.indirect_dma_start(
                        out=patch[:, k, :], out_offset=None, in_=table[ph[2]],
                        in_offset=bass.IndirectOffsetOnAxis(ap=idx_now[:, tt, k:k + 1], axis=0),
                    ).then_inc(s_gat[k], 16)

            for ph in seq:
                if ph[0] != "G":
                    continue
                q = ordinal[ph]
                p = ordinal[("P",) + ph[1:]]
                pool.wait_ge(s_idx, p + 1)
                for i in range(2):
                    pool.wait_ge(s_tab[i], 16 * 8 * 4 * (p + 1))
                tile(ph, 0, 0, q == 0)
                tile(ph, 1, 1, False)
                with pool.Fori(1, NTILE // 2) as i:
                    for tt in range(2):
                        tile(ph, 2 * i + tt, tt, False)

        @block.scalar
        def _(act):
            act.wait_ge(s_const, 16 * NCONST)

            def weigh(ph, it, j):
                q = ordinal[ph]
                tt, k = (j // TAPS) % 2, j % TAPS
                if k == 0:
                    act.wait_ge(s_wc, NTILE * q + 4 * it + j // TAPS + 1)
                act.wait_ge(s_gat[k], 16 * (NTILE * q + 4 * it + j // TAPS + 1))
                if not (q == 0 and isinstance(it, int) and it == 0 and j < SRING):
                    act.wait_ge(s_tr, NS * q + 36 * it + j + 1 - SRING)
                nc.scalar.activation(blend[:, j % SRING, :], patch[:, k, 0:C], ACT.Copy,
                                     scale=wgt_now[:, tt, k, 0:1]).then_inc(s_mul, 1)

            def empty(ph, it, j):
                q = ordinal[ph]
                act.wait_ge(s_tr, NS * q + 36 * it + j + 1)
                e, tt, k = j // GS, (j // TAPS) % 2, j % TAPS
                if isinstance(it, int) and it == 0 and j == 0 and not ended_by(ph):
                    act.wait_ge(s_aln, 16 * TAPS * before(ph, "P"))
                    act.wait_ge(s_posmm, 2 * before(ph, "P"))
                elif j % GS == 0 and not (isinstance(it, int) and it == 0 and not ended_by(ph)):
                    act.wait_ge(s_cv, 2 * (NGROUP * q + 2 * it + e - 1))
                nc.scalar.activation(cols[:, e, :, k, tt * P:(tt + 1) * P],
                                     tbank[j % TRING][:, 0:C].rearrange("p (h n) -> p h n", h=CH),
                                     ACT.Copy).then_inc(s_cols, 1)

            def keep(ph, g, oh):
                q = ordinal[ph]
                act.wait_ge(s_cv, 2 * (NGROUP * q + g) + oh + 1)
                dst, g = (buffer_of(previous(ph)), g + NGROUP) if isinstance(g, int) and g < 0 else (buffer_of(ph), g)
                nc.scalar.activation(dst[:, oh, bass.ds(GROUP * g, GROUP)], obank[oh][:, 0:GROUP],
                                     ACT.Copy).then_inc(s_oev, 1)

            def deviation(ph):
                act.wait_ge(s_var, ordinal[ph] + 1)
                nc.scalar.activation(small[:, 1, :], small[:, 0, :], ACT.Sqrt,
                                     bias=eps_sb[:, 0:1]).then_inc(s_std, 1)

            def normalise(ph, c):
                h, at = quarters[c]
                if ph[1] == 0:
                    act.wait_ge(s_sc, ordinal[ph] + 1)
                    buf = buffer_of(ph)[:, h, at:at + PIX // 2]
                    nc.scalar.activation(buf, buf, ACT.Relu, scale=scale[:, h:h + 1],
                                         bias=shift[:, h:h + 1]).then_inc(s_norm, 1)
                else:
                    act.wait_ge(s_res, 4 * ph[2] + c + 1)
                    buf = image[1][:, h, at:at + PIX // 2]
                    nc.scalar.activation(buf, buf, ACT.Relu, bias=shift[:, h:h + 1]).then_inc(s_norm, 1)

            def iteration(ph, it, first):
                ends = ended_by(ph) if isinstance(it, int) else None
                alone = first and not ends
                for j in range(2 * GS):
                    e, jj = j // GS, j % GS
                    weigh(ph, it, j)
                    if j >= LAG:
                        empty(ph, it, j - LAG)
                    elif not alone:
                        empty(ph, it - 1, 2 * GS + j - LAG)
                    if jj == 3 and not alone:
                        keep(ph, 2 * it + e - 2, 1)
                    if ends and (it, e, jj) == (0, 1, 10):
                        deviation(ends)
                    if ends and (it, e, jj) in NORMALISE_AT:
                        normalise(ends, NORMALISE_AT.index((it, e, jj)))
                    if jj == 16 and not (alone and e == 0):
                        keep(ph, 2 * it + e - 1, 0)

            for ph in seq:
                kind, l, b = ph
                if kind == "P":
                    n = ordinal[ph]
                    ends = ended_by(ph)
                    if ends:
                        keep(ends, NGROUP - 1, 0)
                        keep(ends, NGROUP - 1, 1)
                        deviation(ends)
                    act.wait_ge(s_zero, 5 + 3 * n)
                    rows = part[0:NPART, 0:CELLS].rearrange("m (y x) -> m y x", x=PITCH)
                    for c in range(8):
                        act.wait_ge(s_pmm, 8 * n + c + 1)
                        nc.scalar.activation(rows[:, 8 * c + 1:8 * c + 9, 1:W + 1],
                                             partbank[c % 2][0:NPART, :].rearrange("m (y x) -> m y x", x=W),
                                             ACT.Identity, bias=boff_sb[:, l:l + 1]).then_inc(s_pev, 1)
                        if ends and c % 2:
                            normalise(ends, c // 2)
                    act.wait_ge(s_pev, 8 * (n + 1))
                    if before(ph, "G"):
                        act.wait_ge(s_cv, 2 * NGROUP * before(ph, "G"))
                    if n > 0:
                        act.wait_ge(s_posmm, 2 * n)
                    for k in range(TAPS):
                        rows_k = slice(NOFF * k, NOFF * k + NOFF)
                        act.dma_start(aligned[rows_k, 0:PIX].rearrange("m (y x) -> m y x", x=W),
                                      part[rows_k, 0:CELLS].rearrange("m (y x) -> m y x", x=PITCH)[
                                          :, k // 3:k // 3 + H, k % 3:k % 3 + W]).then_inc(s_aln, 16)
                else:
                    iteration(ph, 0, True)
                    if ended_by(ph):
                        iteration(ph, 1, False)
                    with act.Fori(2 if ended_by(ph) else 1, NGROUP // 2) as it:
                        iteration(ph, it, False)
                    nxt = following(ph)
                    if not nxt or nxt[0] == "P":
                        for j in range(2 * GS - LAG, 2 * GS):
                            empty(ph, NGROUP // 2 - 1, j)
                        keep(ph, NGROUP - 2, 1)
                    if not nxt:
                        keep(ph, NGROUP - 1, 0)
                        keep(ph, NGROUP - 1, 1)
                        deviation(ph)
                        for c in range(4):
                            normalise(ph, c)

        @block.tensor
        def _(pe):
            pe.wait_ge(s_const, 16 * NCONST)

            def turn(ph, it, j):
                q = ordinal[ph]
                pe.wait_ge(s_blend, NS * q + 36 * it + j + 1)
                if not (q == 0 and isinstance(it, int) and it == 0 and j < TRING):
                    pe.wait_ge(s_cols, NS * q + 36 * it + j + 1 - TRING)
                for h in range(CH):
                    mm = nc.tensor.transpose(tbank[j % TRING][:, h * P:(h + 1) * P],
                                             blend[:, j % SRING, h * P:(h + 1) * P], ident[:, :])
                mm.then_inc(s_tr, 1)

            def conv(ph, g, e, oh, steps):
                q = ordinal[ph]
                for s in steps:
                    k, h = s // CH, s % CH
                    if s == 0:
                        if oh == 0:
                            pe.wait_ge(s_cols, NS * q + GS * (g + 1))
                        if not (q == 0 and isinstance(g, int) and g == 0):
                            pe.wait_ge(s_oev, 2 * (NGROUP * q + g - 1) + oh + 1)
                    mm = nc.tensor.matmul(obank[oh][:, 0:GROUP], wdc_sb[:, h, k, oh * P:(oh + 1) * P],
                                          cols[:, e, h, k, :], start=(s == 0), stop=(s == GS - 1))
                    if s == GS - 1:
                        mm.then_inc(s_cv, 1)

            def group_means(ph):
                pe.wait_ge(s_agg, ordinal[ph] + 1)
                pe.wait_ge(s_idx, before(ph, "P"))
                nc.tensor.matmul(gnbank[:, 0:4], gavg[:, :], mom[:, :, :].rearrange("p a h -> p (a h)"),
                                 start=True, stop=True).then_inc(s_gn, 1)

            def iteration(ph, it, first):
                ends = ended_by(ph) if isinstance(it, int) else None
                for j in range(2 * GS):
                    e, jj = j // GS, j % GS
                    turn(ph, it, j)
                    if 5 <= jj < 17 and not (first and not ends and e == 0):
                        oh = (jj - 5) // 6
                        s0 = 3 * ((jj - 5) % 6)
                        conv(ph, 2 * it + e - 1, 1 - e, oh, range(s0, s0 + 3))
                    if ends and (it, e, jj) == (0, 1, 7):
                        group_means(ends)

            for ph in seq:
                kind, l, b = ph
                ends = ended_by(ph)
                if kind == "P":
                    n = ordinal[ph]
                    src = buffer_of(ph)
                    if l == 0:
                        pe.wait_ge(s_x[loads[ph] % 2], 16 * (loads[ph] // 2 + 1))
                    if ends:
                        pe.wait_ge(s_cols, NS * (ordinal[ends] + 1))

                    def part_conv(c):
                        if n or c >= 2:
                            pe.wait_ge(s_pev, 8 * n + c - 1)
                        if ends and c == 0:
                            pe.wait_ge(s_var, ordinal[ends] + 1)
                        if n and c == 0:
                            pe.wait_ge(s_idx, n)
                        for h in range(CH):
                            mm = nc.tensor.matmul(partbank[c % 2][0:NPART, :], woff_sb[:, l, h, :],
                                                  src[:, h, 512 * c:512 * c + 512], start=(h == 0), stop=(h == CH - 1))
                        mm.then_inc(s_pmm, 1)

                    def positions(n):
                        pe.wait_ge(s_aln, 16 * TAPS * (n + 1))
                        pe.wait_ge(s_pev, 8 * (n + 1))
                        for t in range(NTILE):
                            mm = nc.tensor.matmul(posbank[t // 16][:, (t % 16) * NPOS:(t % 16 + 1) * NPOS],
                                                  aligned[0:NPART, P * t:P * t + P], sel[0:NPART, :], start=True, stop=True)
                            if t % 16 == 15:
                                mm.then_inc(s_posmm, 1)

                    for c in range(16):
                        if l and c % 8 == 0:
                            pe.wait_ge(s_norm, 4 * b + 2 + c // 4)
                        if n or c >= 2:
                            pe.wait_ge(s_tev, 16 * n + c - 1)
                        for i in range(4):
                            t, h = 2 * c + i // 2, i % 2
                            mm = nc.tensor.transpose(turnbank[c % 2][:, P * i:P * i + P],
                                                     src[:, h, P * t:P * t + P], ident[:, :])
                        mm.then_inc(s_tmm, 1)
                        if ends:
                            if c in (3, 5):
                                conv(ends, NGROUP - 1, 1, (c - 3) // 2, range(GS))
                            if c == 7:
                                group_means(ends)
                            if 8 <= c < 12:
                                part_conv(2 * (c - 8))
                                part_conv(2 * (c - 8) + 1)
                        else:
                            if c == 3 and n:
                                positions(n - 1)
                            if 4 <= c < 12:
                                part_conv(c - 4)
                    if following(ph)[0] == "G":
                        positions(n)
                else:
                    if b == 0:
                        pe.wait_ge(s_w, 16 * (l + 1))
                    pe.wait_ge(s_tev, 16 * before(ph, "P"))
                    iteration(ph, 0, True)
                    if ended_by(ph):
                        iteration(ph, 1, False)
                    with pe.Fori(2 if ended_by(ph) else 1, NGROUP // 2) as it:
                        iteration(ph, it, False)
                    if not following(ph):
                        for oh in range(2):
                            conv(ph, NGROUP - 1, 1, oh, range(GS))
                        group_means(ph)

        @block.vector
        def _(dve):
            steps = [0]

            def link(ins):
                steps[0] += 1
                ins.then_inc(s_dv, 1)
                dve.wait_ge(s_dv, steps[0])

            nc.vector.memset(boff_sb[:, :], 0.0).then_inc(s_zero, 1)
            nc.vector.memset(cols_flat[:, 0, 0:4 * PATCH], 0.0).then_inc(s_zero, 1)
            link(nc.vector.memset(eps_sb[:, :], EPS))
            dve.wait_ge(s_const, 16 * NCONST)
            dve.wait_ge(s_border, 16 * 44)

            def iteration(ph, it, first):
                q = ordinal[ph]
                ends = ended_by(ph) if isinstance(it, int) else None
                alone = first and not ends
                base = 2 * NS * q
                for j in range(0, 2 * GS, 2):
                    for i in (j, j + 1):
                        if i % TAPS == 0:
                            tl = i // TAPS
                            t = 4 * it + tl
                            w = wgt[:, ph[2], t, :, :] if isinstance(t, int) else wgt[:, ph[2], bass.ds(t, 1), :, :].rearrange(
                                "p a k c -> p (a k) c")
                            nc.vector.tensor_copy(wgt_now[:, tl % 2, :, :], w).then_inc(s_wc, 1)
                            dve.wait_ge(s_wc, NTILE * q + t + 1)
                    for corner in (1, 2, 3):
                        for i in (j, j + 1):
                            k, tt = i % TAPS, (i // TAPS) % 2
                            if corner == 1:
                                dve.wait_ge(s_mul, NS * q + 36 * it + i + 1)
                            else:
                                dve.wait_ge(s_st, base + 72 * it + 2 * j + (i - j) + 1 + 2 * (corner - 2))
                            nc.vector.scalar_tensor_tensor(
                                out=blend[:, i % SRING, :], in0=patch[:, k, corner * C:(corner + 1) * C],
                                scalar=wgt_now[:, tt, k, corner:corner + 1], in1=blend[:, i % SRING, :],
                                op0=ALU.mult, op1=ALU.add).then_inc(s_blend if corner == 3 else s_st, 1)
                    e, jj = j // GS, j % GS
                    if j in IDX_AFTER and first and not ends:
                        indices(previous(ph), IDX_AFTER.index(j))
                    if jj == 6 and not alone:
                        moments(ph, 2 * it + e - 2, 1)
                    if jj == 16 and not (alone and e == 0):
                        moments(ph, 2 * it + e - 1, 0)
                    if ends and (it, e) == (0, 1):
                        if jj == 6:
                            channel_moments()
                        if jj == 8:
                            variance(ends)
                        if jj == 10:
                            affine(ends)
                    if ends and ends[1] and (it, e, jj) in RESIDUAL_AT:
                        residual(ends, RESIDUAL_AT.index((it, e, jj)))

            def moments(ph, g, oh):
                dve.wait_ge(s_oev, 2 * (NGROUP * ordinal[ph] + g) + oh + 1)
                src, g = (buffer_of(previous(ph)), g + NGROUP) if isinstance(g, int) and g < 0 else (buffer_of(ph), g)
                out = stats[:, oh, g, :] if isinstance(g, int) else stats[:, oh, bass.ds(g, 1), :].rearrange("p a s -> p (a s)")
                nc.vector.bn_stats(out, src[:, oh, bass.ds(GROUP * g, GROUP)])

            def channel_moments():
                link(nc.vector.memset(small[:, 3, :], 0.0))
                for h in range(CH):
                    ins = nc.vector.bn_aggr(mv[:, h, :], stats[:, h, :, :].rearrange("p g s -> p (g s)"))
                link(ins)
                nc.vector.tensor_copy(mom[:, 0, :], mv[:, :, 0])
                link(nc.vector.tensor_tensor(small[:, 2, :], mv[:, :, 0], mv[:, :, 0], ALU.mult))
                nc.vector.tensor_tensor(mom[:, 1, :], small[:, 2, :], mv[:, :, 1], ALU.add).then_inc(s_agg, 1)

            def variance(ph):
                dve.wait_ge(s_gn, ordinal[ph] + 1)
                link(nc.vector.tensor_copy(gstat[:, :, :].rearrange("p a h -> p (a h)"), gnbank[:, 0:4]))
                link(nc.vector.tensor_tensor(small[:, 2, :], gstat[:, 0, :], gstat[:, 0, :], ALU.mult))
                nc.vector.tensor_tensor(small[:, 0, :], gstat[:, 1, :], small[:, 2, :],
                                        ALU.subtract).then_inc(s_var, 1)

            def affine(ph):
                dve.wait_ge(s_std, ordinal[ph] + 1)
                link(nc.vector.reciprocal(small[:, 2, :], small[:, 1, :]))
                link(nc.vector.tensor_tensor(scale[:, :], small[:, 2, :], gb_sb[:, ph[1], 0, :], ALU.mult))
                link(nc.vector.tensor_tensor(small[:, 3, :], gstat[:, 0, :], scale[:, :], ALU.mult))
                nc.vector.tensor_tensor(shift[:, :], gb_sb[:, ph[1], 1, :], small[:, 3, :],
                                        ALU.subtract).then_inc(s_sc, 1)

            def residual(ph, c):
                h, at = quarters[c]
                dve.wait_ge(s_x[loads[ph] % 2], 16 * (loads[ph] // 2 + 1))
                dve.wait_ge(s_sc, ordinal[ph] + 1)
                out = image[1][:, h, at:at + PIX // 2]
                nc.vector.scalar_tensor_tensor(out=out, in0=buffer_of(ph)[:, h, at:at + PIX // 2], scalar=scale[:, h:h + 1],
                                               in1=out, op0=ALU.mult, op1=ALU.add).then_inc(s_res, 1)

            def zero_borders(ph):
                n = ordinal[ph]
                if ended_by(ph):
                    dve.wait_ge(s_cv, 2 * NGROUP * before(ph, "G") - 2)
                if n:
                    dve.wait_ge(s_aln, 16 * TAPS * n)
                nc.vector.memset(part[0:NPART, 0:PITCH + 1], 0.0).then_inc(s_zero, 1)
                pairs = part[0:NPART, PITCH + W + 1:PITCH + W + 1 + H * PITCH].rearrange("m (y x) -> m y x", x=PITCH)
                nc.vector.memset(pairs[:, :, 0:2], 0.0).then_inc(s_zero, 1)
                nc.vector.memset(part[0:NPART, CELLS - PITCH + 1:CELLS], 0.0).then_inc(s_zero, 1)

            def indices(ph, stage):
                n, b = ordinal[ph], ph[2]
                flat = lambda a: a[:, :, :].rearrange("p t n -> p (t n)")
                if stage == 0:
                    half = NTILE // 2
                    for i in range(2):
                        dve.wait_ge(s_posmm, 2 * n + i + 1)
                        ins = nc.vector.tensor_tensor(
                            pos[:, half * i:half * i + half, :].rearrange("p t n -> p (t n)"),
                            posbank[i][:, 0:half * NPOS],
                            posbase[:, half * i:half * i + half, :].rearrange("p t n -> p (t n)"), ALU.add)
                    link(ins)
                    link(nc.vector.tensor_scalar(flat(pos), flat(pos), -1.0, float(H), ALU.max, ALU.min))
                    link(nc.vector.tensor_copy(flat(posi), flat(pos)))
                    link(nc.vector.tensor_copy(flat(low), flat(posi)))
                if stage == 1:
                    link(nc.vector.tensor_tensor(flat(over), flat(low), flat(pos), ALU.is_gt))
                    link(nc.vector.tensor_tensor(flat(low), flat(low), flat(over), ALU.subtract))
                    link(nc.vector.tensor_tensor(flat(pos), flat(pos), flat(low), ALU.subtract))
                    link(nc.vector.tensor_scalar(flat(over), flat(pos), -1.0, 1.0, ALU.mult, ALU.add))
                if stage == 2:
                    for r, wy in enumerate((over, pos)):
                        for c, wx in enumerate((over, pos)):
                            nc.vector.tensor_tensor(wgt[:, b, :, :, 2 * r + c], wy[:, :, 0:TAPS],
                                                    wx[:, :, TAPS:NPOS], ALU.mult)
                    link(nc.vector.scalar_tensor_tensor(out=idxf[:, :, :], in0=low[:, :, 0:TAPS], scalar=float(PITCH),
                                                        in1=low[:, :, TAPS:NPOS], op0=ALU.mult, op1=ALU.add))
                    nc.vector.tensor_scalar(idx[:, b, :, :], idxf[:, :, :], float(PITCH + 1), None,
                                            ALU.add).then_inc(s_idx, 1)
                    dve.wait_ge(s_idx, n + 1)

            for ph in seq:
                kind, l, b = ph
                ends = ended_by(ph)
                if kind == "P":
                    n = ordinal[ph]
                    if ends:
                        moments(ends, NGROUP - 2, 1)
                    for c in range(16):
                        dve.wait_ge(s_tmm, 16 * n + c + 1)
                        bt = c // 2
                        if n or bt >= 2:
                            dve.wait_ge(s_tab[bt % 2], 16 * 8 * (4 * n + bt // 2))
                        nc.vector.tensor_copy(
                            turned[:, bt % 2, 2 * (c % 2):2 * (c % 2) + 2, :].rearrange("p a n -> p (a n)"),
                            turnbank[c % 2][:, :]).then_inc(s_tev, 1)
                        if c == 3:
                            if n and not ends:
                                for stage in range(3):
                                    indices(previous(ph), stage)
                            zero_borders(ph)
                        if ends and c == 5:
                            moments(ends, NGROUP - 1, 0)
                        if ends and c == 7:
                            moments(ends, NGROUP - 1, 1)
                            channel_moments()
                            variance(ends)
                            affine(ends)
                else:
                    iteration(ph, 0, True)
                    if ended_by(ph):
                        iteration(ph, 1, False)
                    with dve.Fori(2 if ended_by(ph) else 1, NGROUP // 2) as it:
                        iteration(ph, it, False)
                    if not following(ph):
                        moments(ph, NGROUP - 2, 1)
                        moments(ph, NGROUP - 1, 0)
                        moments(ph, NGROUP - 1, 1)
                        channel_moments()
                        variance(ph)
                        affine(ph)
                        for c in range(4):
                            residual(ph, c)
IC = C // 2
NKEY = PIX // 2
JT = NKEY // P
BLK = 2
NBLK = JT // BLK
CHUNK = 512
NCH = PIX // CHUNK
NIC = NKEY // CHUNK
XR = 4
ER = 2 * BLK
AX_X = mybir.AxisListType.X
FR = mybir.dt.float32r


def attention_block(nc, x1, wproj, wmask, x2):
    with ExitStack() as ctx:
        def sb(name, shape, dt=F32):
            return ctx.enter_context(nc.sbuf_tensor(name, shape, dt))

        def sem(name):
            return ctx.enter_context(nc.semaphore(name))

        proj = [sb(f"proj_{part}", [P, CH, 3 * IC], FR) for part in ("hi", "lo")]
        mask = [sb(f"mask_{part}", [P, C], FR) for part in ("hi", "lo")]
        xr = sb("xr", [P, XR, CH, CHUNK])
        split = [sb(f"split_{part}", [P, 2, CH, CHUNK], FR) for part in ("hi", "lo")]
        theta = [sb(f"theta_{part}", [P, PIX], FR) for part in ("hi", "lo")]
        phi = sb("phi", [P, 2, NKEY])
        phij = [sb(f"phi_tile_{part}", [P, 2, 2, P], FR) for part in ("hi", "lo")]
        gt = sb("gt", [P, 2, JT, IC])
        gs = [sb(f"gs_{part}", [P, ER, 2, IC], FR) for part in ("hi", "lo")]
        expo = sb("expo", [P, NKEY])
        ex = [sb(f"ex_{part}", [P, ER, NKEY], FR) for part in ("hi", "lo")]
        att = sb("att", [P, PIX])
        mx = sb("mx", [P, 2, NIC])
        nmx = sb("nmx", [P, 2])
        rs = sb("rs", [P, 2])
        rr = sb("rr", [P, 2])
        wraw = att[:, 0:CH * 3 * IC + C]

        lbank = ctx.enter_context(nc.psum_tensor("lbank", [P, NKEY], F32))
        vbank = [ctx.enter_context(nc.psum_tensor(f"vbank{i}", [P, CHUNK], F32)) for i in range(2)]
        mbank = [ctx.enter_context(nc.psum_tensor(f"mbank{i}", [P, CHUNK], F32)) for i in range(2)]

        s_w = sem("a_weights_loaded")
        s_wh = sem("a_weights_hi")
        s_wl = sem("a_weights_lo")
        s_x = [sem(f"a_x_loaded{i}") for i in range(XR)]
        s_st = [sem(f"a_stored{i}") for i in range(XR)]
        s_hi = sem("a_split_hi")
        s_lo = sem("a_split_lo")
        s_mm = sem("a_product")
        s_th = sem("a_theta_hi")
        s_phi = sem("a_phi_kept")
        s_ed = sem("a_bank_emptied_by_vector")
        s_pjh = sem("a_phi_tile_hi")
        s_pj = sem("a_phi_tile_ready")
        s_lg = sem("a_logits")
        s_bm = sem("a_bank_max")
        s_mx = sem("a_max_ready")
        s_ex = sem("a_exp_ready")
        s_eh = sem("a_exp_hi")
        s_el = sem("a_exp_lo")
        s_rr = sem("a_reciprocal")
        s_gh = sem("a_gt_hi")
        s_gs = sem("a_gt_scaled")
        s_pv = sem("a_pv_product")
        s_pa = sem("a_pv_added")
        SPLITS = 2 * NCH
        FILLS = 3 * NCH + CH * NCH
        EMPTIED = 2 * NCH + CH * NCH
        F = lambda ap: ap.bitcast(F32)

        def slot(k):
            i = k % SPLITS
            return (0, 3, 1, 2)[i % XR] if i < NCH else 1 + (i - NCH) % (XR - 1)

        def uses(k):
            return sum(slot(m) == slot(k) for m in range(k + 1))

        block = ctx.enter_context(nc.Block())

        @block.sync
        def _(sp):
            sp.dma_start(wraw[:, 0:CH * 3 * IC].rearrange("p (h m) -> p h m", h=CH),
                         wproj.rearrange("(h p) m -> p h m", p=P)).then_inc(s_w, 16)
            sp.dma_start(wraw[:, CH * 3 * IC:CH * 3 * IC + C], wmask).then_inc(s_w, 16)

            def load(n):
                earlier = [m for m in range(n) if slot(m) == slot(n)]
                if earlier and earlier[-1] % SPLITS < NCH:
                    sp.wait_ge(s_lo, earlier[-1] + 1)
                elif earlier:
                    sp.wait_ge(s_st[slot(n)], 16 * sum(m % SPLITS >= NCH for m in earlier))
                b, c = n // SPLITS, n % NCH
                sp.dma_start(xr[:, slot(n), :, :], x1[b].rearrange("(h p) n -> p h n", p=P)[
                    :, :, CHUNK * c:CHUNK * c + CHUNK]).then_inc(s_x[slot(n)], 16)

            load(0)
            for b in range(B):
                for i in range(1, SPLITS):
                    load(SPLITS * b + i)
                    if i == NCH + XR - 2 and b + 1 < B:
                        load(SPLITS * (b + 1))
            for r in range(1, XR):
                sp.wait_ge(s_st[r], 16 * sum(slot(m) == r and m % SPLITS >= NCH for m in range(SPLITS * B)))

        @block.tensor
        def _(pe):
            pe.wait_ge(s_wl, 2)

            def bank(b, n):
                m = n - 2 if n >= 2 else n - 2 + FILLS
                bb = b if n >= 2 else b - 1
                if bb < 0:
                    return
                if m >= 3 * NCH:
                    pe.wait_ge(s_ed, EMPTIED * bb + 2 * NCH + m - 3 * NCH + 1)
                elif m % 3 == 1:
                    pe.wait_ge(s_phi, NCH * bb + m // 3 + 1)
                else:
                    pe.wait_ge(s_ed, EMPTIED * bb + 2 * (m // 3) + m % 3 // 2 + 1)

            def products(out, terms):
                pairs = [(l[i], r[j]) for l, r in terms for i, j in ((1, 0), (0, 1), (0, 0))]
                for i, (l, r) in enumerate(pairs):
                    mm = nc.tensor.matmul(out, l, r, start=(i == 0), stop=(i == len(pairs) - 1))
                return mm

            def project(b, c):
                k = SPLITS * b + c
                pe.wait_ge(s_lo, k + 1)
                xs = lambda h, lo, n: [a[:, k % 2, h, lo:lo + n] for a in split]
                ws = lambda h, lo: [a[:, h, lo:lo + IC] for a in proj]
                for w in range(2):
                    bank(b, 3 * c + w)
                    products(mbank[(3 * c + w) % 2][:, :],
                             [(ws(h, w * IC), xs(h, 0, CHUNK)) for h in range(CH)]).then_inc(s_mm, 1)
                n = 3 * c + 2
                bank(b, n)
                for i in range(CHUNK // P):
                    mm = products(mbank[n % 2][:, IC * i:IC * i + IC],
                                  [(xs(h, P * i, P), ws(h, 2 * IC)) for h in range(CH)])
                mm.then_inc(s_mm, 1)

            def logits(b, j):
                pe.wait_ge(s_pj, JT * b + j + 1)
                if b or j:
                    pe.wait_ge(s_ex, JT * b + j)
                for c in range(NIC):
                    products(lbank[:, CHUNK * c:CHUNK * c + CHUNK],
                             [([a[:, j % 2, h, :] for a in phij],
                               [a[:, NKEY * h + CHUNK * c:NKEY * h + CHUNK * c + CHUNK] for a in theta])
                              for h in range(2)]).then_inc(s_lg, 1)

            def pv(b, k, u):
                h, c = u // NIC, u % NIC
                n = NCH * (NBLK * b + k) + u
                pe.wait_ge(s_gs, JT * b + BLK * (k + 1))
                pe.wait_ge(s_el, JT * b + BLK * (k + 1))
                if n >= 2:
                    pe.wait_ge(s_pa, n - 1)
                products(vbank[n % 2][:, :],
                         [([a[:, (BLK * k + i) % ER, h, :] for a in gs],
                           [a[:, (BLK * k + i) % ER, CHUNK * c:CHUNK * c + CHUNK] for a in ex])
                          for i in range(BLK)]).then_inc(s_pv, 1)

            def masked(b, u):
                k = SPLITS * b + NCH + u
                pe.wait_ge(s_lo, k + 1)
                for oh in range(CH):
                    n = 3 * NCH + CH * u + oh
                    bank(b, n)
                    products(mbank[n % 2][:, :], [([a[:, oh * P:(oh + 1) * P] for a in mask],
                                                   [a[:, u % 4 // 2, u % 2, :] for a in split])]).then_inc(s_mm, 1)

            for b in range(B):
                for c in range(NCH):
                    project(b, c)
                pe.wait_ge(s_ed, EMPTIED * b + 2 * NCH)
                for j in range(JT):
                    logits(b, j)
                    if j >= BLK:
                        for u in range(4 * (j % BLK), 4 * (j % BLK) + 4):
                            pv(b, j // BLK - 1, u)
                for u in range(NCH):
                    pv(b, NBLK - 1, u)
                    if u >= 2:
                        masked(b, u - 2)
                for u in (NCH - 2, NCH - 1):
                    masked(b, u)

        def split_free(eng, k):
            b, i = k // SPLITS, k % SPLITS
            if i >= NCH + 4:
                eng.wait_ge(s_mm, FILLS * b + 3 * NCH + CH * (i - NCH - 3))
            elif i >= NCH:
                eng.wait_ge(s_mm, FILLS * b + 3 * (NCH - 1 + (i - NCH) // 2))
            elif i >= 2:
                eng.wait_ge(s_mm, FILLS * b + 3 * (i - 1))
            elif i == 1 and b:
                eng.wait_ge(s_mm, FILLS * b)
            elif b:
                eng.wait_ge(s_mm, FILLS * b - CH * 2)

        @block.scalar
        def _(act):
            act.wait_ge(s_w, 32)
            nc.scalar.activation(proj[0][:, :, :].rearrange("p h m -> p (h m)"), wraw[:, 0:CH * 3 * IC],
                                 ACT.Copy).then_inc(s_wh, 1)
            nc.scalar.activation(mask[0][:, :], wraw[:, CH * 3 * IC:CH * 3 * IC + C], ACT.Copy).then_inc(s_wh, 1)

            def split_x(b, c):
                k = SPLITS * b + c
                act.wait_ge(s_x[slot(k)], 16 * uses(k))
                split_free(act, k)
                nc.scalar.activation(split[0][:, k % 2, :, :], xr[:, slot(k), :, :], ACT.Copy).then_inc(s_hi, 1)

            def keep(b, c):
                act.wait_ge(s_mm, FILLS * b + 3 * c + 1)
                at = CHUNK * c
                if b and c == 0:
                    act.wait_ge(s_lg, NIC * JT * b)
                nc.scalar.activation(theta[0][:, at:at + CHUNK], mbank[3 * c % 2][:, :], ACT.Copy).then_inc(s_th, 1)
                act.wait_ge(s_mm, FILLS * b + 3 * c + 2)
                if b and c == 0:
                    act.wait_ge(s_pj, JT * b)
                nc.scalar.activation(phi[:, c // NIC, at % NKEY:at % NKEY + CHUNK], mbank[(3 * c + 1) % 2][:, :],
                                     ACT.Copy).then_inc(s_phi, 1)

            split_x(0, 0)
            for b in range(B):
                for c in range(NCH):
                    if c + 1 < NCH:
                        split_x(b, c + 1)
                    keep(b, c)
                for j in range(JT):
                    n = JT * b + j
                    act.wait_ge(s_mx, n + 1)
                    if n >= 1:
                        act.wait_ge(s_el, n)
                    if n >= 2:
                        act.wait_ge(s_rr, n - 1)
                    nc.scalar.activation(expo[:, :], lbank[:, :], ACT.Exp, bias=nmx[:, j % 2:j % 2 + 1],
                                         accum_out=rs[:, j % 2:j % 2 + 1]).then_inc(s_ex, 1)
                    act.wait_ge(s_ex, n + 1)
                    if n >= ER:
                        act.wait_ge(s_pv, NCH * ((n - ER) // BLK + 1))
                    nc.scalar.activation(ex[0][:, j % ER, :], expo[:, :], ACT.Copy).then_inc(s_eh, 1)
                for u in range(NCH):
                    k = SPLITS * b + NCH + u
                    act.wait_ge(s_pa, NCH * (NBLK * (b + 1) - 1) + u + 1)
                    split_free(act, k)
                    nc.scalar.activation(split[0][:, u % 4 // 2, u % 2, :], att[:, CHUNK * u:CHUNK * u + CHUNK],
                                         ACT.Copy).then_inc(s_hi, 1)
                if b + 1 < B:
                    split_x(b + 1, 0)

        @block.gpsimd
        def _(pool):
            for b in range(B):
                for j in range(JT):
                    n = JT * b + j
                    pool.wait_ge(s_phi, NCH * b + NIC + j // 4 + 1)
                    if n >= 2:
                        pool.wait_ge(s_lg, NIC * (n - 1))
                    src = phi[:, :, P * j:P * j + P]
                    nc.gpsimd.tensor_copy(phij[0][:, j % 2, :, :], src).then_inc(s_pjh, 1)
                    pool.wait_ge(s_pjh, n + 1)
                    nc.gpsimd.tensor_tensor(phij[1][:, j % 2, :, :], src, F(phij[0][:, j % 2, :, :]),
                                            ALU.subtract).then_inc(s_pj, 1)
                for c in range(NCH):
                    n, at = SPLITS * b + NCH + c, PIX * b + CHUNK * c
                    pool.wait_ge(s_ed, EMPTIED * b + 2 * NCH + CH * (c + 1))
                    pool.dma_start(x2[:, at:at + CHUNK].rearrange("(h p) n -> p h n", p=P),
                                   xr[:, slot(n), :, :]).then_inc(s_st[slot(n)], 16)

        @block.vector
        def _(dve):
            dve.wait_ge(s_wh, 2)
            nc.vector.tensor_tensor(proj[1][:, :, :].rearrange("p h m -> p (h m)"), wraw[:, 0:CH * 3 * IC],
                                    F(proj[0][:, :, :].rearrange("p h m -> p (h m)")), ALU.subtract).then_inc(s_wl, 1)
            nc.vector.tensor_tensor(mask[1][:, :], wraw[:, CH * 3 * IC:CH * 3 * IC + C], F(mask[0][:, :]),
                                    ALU.subtract).then_inc(s_wl, 1)

            def split_x(b, c):
                k = SPLITS * b + c
                dve.wait_ge(s_hi, k + 1)
                split_free(dve, k)
                nc.vector.tensor_tensor(split[1][:, k % 2, :, :], xr[:, slot(k), :, :], F(split[0][:, k % 2, :, :]),
                                        ALU.subtract).then_inc(s_lo, 1)

            def keep(b, c):
                dve.wait_ge(s_th, NCH * b + c + 1)
                at = CHUNK * c
                nc.vector.tensor_tensor(theta[1][:, at:at + CHUNK], mbank[3 * c % 2][:, :],
                                        F(theta[0][:, at:at + CHUNK]), ALU.subtract).then_inc(s_ed, 1)
                n, t = 3 * c + 2, 4 * c
                dve.wait_ge(s_mm, FILLS * b + n + 1)
                nc.vector.tensor_copy(gt[:, t // JT, t % JT:t % JT + 4, :].rearrange("p t n -> p (t n)"),
                                      mbank[n % 2][:, :]).then_inc(s_ed, 1)

            def bank_max(b, j, c):
                dve.wait_ge(s_lg, NIC * (JT * b + j) + c + 1)
                nc.vector.reduce_max(mx[:, j % 2, c:c + 1], lbank[:, CHUNK * c:CHUNK * c + CHUNK], AX_X).then_inc(s_bm, 1)

            def scaled(b, j):
                n = JT * b + j
                dve.wait_ge(s_ex, n + 1)
                nc.vector.reciprocal(rr[:, j % 2:j % 2 + 1], rs[:, j % 2:j % 2 + 1]).then_inc(s_rr, 1)
                dve.wait_ge(s_rr, n + 1)
                if n >= ER:
                    dve.wait_ge(s_pv, NCH * ((n - ER) // BLK + 1))
                r = rr[:, j % 2:j % 2 + 1]
                nc.vector.tensor_scalar(gs[0][:, j % ER, :, :], gt[:, :, j, :], r, None, ALU.mult).then_inc(s_gh, 1)
                dve.wait_ge(s_gh, n + 1)
                nc.vector.scalar_tensor_tensor(out=gs[1][:, j % ER, :, :], in0=gt[:, :, j, :], scalar=r,
                                               in1=F(gs[0][:, j % ER, :, :]), op0=ALU.mult,
                                               op1=ALU.subtract).then_inc(s_gs, 1)
                dve.wait_ge(s_eh, n + 1)
                nc.vector.tensor_tensor(ex[1][:, j % ER, :], expo[:, :], F(ex[0][:, j % ER, :]),
                                        ALU.subtract).then_inc(s_el, 1)

            def add(b, k, u):
                n = NCH * (NBLK * b + k) + u
                dve.wait_ge(s_pv, n + 1)
                dst = att[:, CHUNK * u:CHUNK * u + CHUNK]
                if k == 0:
                    nc.vector.tensor_copy(dst, vbank[n % 2][:, :]).then_inc(s_pa, 1)
                else:
                    dve.wait_ge(s_pa, n - 7)
                    nc.vector.tensor_tensor(dst, vbank[n % 2][:, :], dst, ALU.add).then_inc(s_pa, 1)

            def split_att(b, u):
                k = SPLITS * b + NCH + u
                dve.wait_ge(s_hi, k + 1)
                nc.vector.tensor_tensor(split[1][:, u % 4 // 2, u % 2, :], att[:, CHUNK * u:CHUNK * u + CHUNK],
                                        F(split[0][:, u % 4 // 2, u % 2, :]), ALU.subtract).then_inc(s_lo, 1)

            def add_masked(b, u):
                k = SPLITS * b + NCH + u
                dve.wait_ge(s_x[slot(k)], 16 * uses(k))
                for oh in range(CH):
                    n = 3 * NCH + CH * u + oh
                    dve.wait_ge(s_mm, FILLS * b + n + 1)
                    dst = xr[:, slot(k), oh, :]
                    nc.vector.tensor_tensor(dst, mbank[n % 2][:, :], dst, ALU.add).then_inc(s_ed, 1)

            split_x(0, 0)
            for b in range(B):
                for c in range(NCH):
                    if c + 1 < NCH:
                        split_x(b, c + 1)
                    keep(b, c)
                for j in range(JT):
                    if JT * b + j >= 2:
                        dve.wait_ge(s_ex, JT * b + j - 1)
                    if j:
                        scaled(b, j - 1)
                    for c in range(NIC):
                        bank_max(b, j, c)
                    dve.wait_ge(s_bm, NIC * (JT * b + j + 1))
                    nc.vector.tensor_reduce(nmx[:, j % 2:j % 2 + 1], mx[:, j % 2, :], AX_X, ALU.max, negate=True).then_inc(s_mx, 1)
                    if j >= BLK:
                        for u in range(4 * (j % BLK), 4 * (j % BLK) + 4):
                            add(b, j // BLK - 1, u)
                scaled(b, JT - 1)
                for u in range(NCH + 3):
                    if u >= 3:
                        add_masked(b, u - 3)
                    if u < NCH:
                        add(b, NBLK - 1, u)
                        split_att(b, u)
                    if u == NCH and b + 1 < B:
                        split_x(b + 1, 0)


PATHS, HD = 32, 4
ALL = B * PIX
LOADW = 2048
NLOAD = ALL // LOADW
NFILL = ALL // CHUNK
PART3 = ((0, 0), (1, 0), (2, 0), (0, 1), (1, 1), (0, 2))
NPARTS = 3
NCOPY = len(PART3)
KROWS = NCOPY * HD
KBIAS = 3


def squeeze_block(nc, x2, w1t, w2bd, vec128, w3r, bc3, masks, parts, wparts):
    with ExitStack() as ctx:
        def sb(name, shape, dt=F32):
            return ctx.enter_context(nc.sbuf_tensor(name, shape, dt))

        def sem(name):
            return ctx.enter_context(nc.semaphore(name))

        w1_sb = sb("w1_sb", [P, CH, P])
        w2 = [sb(f"w2_{part}", [P, TAPS, P], FR) for part in ("hi", "lo")]
        vec = sb("vec", [P, 6])
        w3_sb = sb("w3_sb", [P, C])
        g3_sb = sb("g3_sb", [P, 3, C])
        mk = sb("mk", [P, 2 * P])
        xc = sb("xc", [P, 2, CH, LOADW])
        y2 = sb("y2", [P, ALL])
        y1 = [sb(f"y1_{part}", [P, 2, CELLS], FR) for part in ("hi", "lo")]
        yp_sb = sb("yp_sb", [P, 3 * LOADW])
        st1 = sb("st1", [P, NFILL, 6])
        st2 = sb("st2", [P, NFILL, 6])
        mv1 = sb("mv1", [P, 2])
        mv2 = sb("mv2", [P, 2])
        tiny = sb("tiny", [P, 12])
        sums = sb("sums", [P, NLOAD])
        xflat = xc[:, :, :, :].rearrange("p a h n -> p (a h n)")
        cen = xflat[:, 0:2 * CHUNK].rearrange("p (a n) -> p a n", a=2)
        yt = xflat[:, 2 * CHUNK:4 * CHUNK].rearrange("p (a n) -> p a n", a=2)
        rest = xflat[:, 4 * CHUNK:4 * CHUNK + 2 * LOADW].rearrange("p (a n) -> p a n", a=2)
        w2_raw = yp_sb[:, 0:TAPS * P]
        yp = yp_sb[:, :].bitcast(BF16).rearrange("p (a i n) -> p a i n", a=2, i=3)
        yflat, o = xflat, 4 * CHUNK + 2 * LOADW
        covm = w1_sb[:, 0, :]
        tcov, tmean, s3, a3, b3 = [yflat[:, o + C * i:o + C * (i + 1)] for i in range(5)]
        o += 5 * C
        ap = yflat[:, o:o + 3 * C].bitcast(BF16).rearrange("p (k i n) -> p k i n", k=2, i=3)

        bank = [ctx.enter_context(nc.psum_tensor(f"qbank{i}", [P, CHUNK], F32)) for i in range(8)]

        s_w = sem("q_weights_loaded")
        s_x = [sem(f"q_x_loaded{i}") for i in range(2)]
        s_zero = sem("q_border_zeroed")
        s_c1 = sem("q_conv1_product")
        s_k1 = sem("q_conv1_kept")
        s_c2 = sem("q_conv2_product")
        s_k2 = sem("q_conv2_kept")
        s_var = sem("q_variance_ready")
        s_std = sem("q_deviation_ready")
        s_sc = sem("q_scale_ready")
        s_w2 = sem("q_w2_hi")
        s_w2l = sem("q_w2_lo")
        s_n1 = sem("q_y1_normalised")
        s_yh = sem("q_y1_hi")
        s_yl = sem("q_y1_lo")
        s_n2 = sem("q_y2_normalised")
        s_dv = sem("q_vector_step")
        s_cen = sem("q_centred")
        s_tp = sem("q_turned")
        s_tk = sem("q_turned_kept")
        s_cov = sem("q_covariance_product")
        s_p = [sem(f"q_part{i}") for i in range(3)]
        s_rest = sem("q_rest")
        s_pst = [sem(f"q_parts_stored{i}") for i in range(2)]
        s_cm = sem("q_covariance_masked")
        s_t = sem("q_cov_times_w")
        s_u = sem("q_w_cov_w")
        s_m3 = sem("q_moments3")
        s_v3 = sem("q_variance3")
        s_d3 = sem("q_deviation3")
        s_wp = sem("q_weight_parts")
        s_wst = sem("q_weight_parts_stored")
        block = ctx.enter_context(nc.Block())
        NW = 6

        def half_rows(part, b, q):
            y = 1 + H // 2 * q
            return part[:, b % 2, :].rearrange("p (y x) -> p y x", x=PITCH)[:, y:y + H // 2, 1:W + 1]

        @block.sync
        def _(sp):
            sp.dma_start(w1_sb[:, :, :], w1t.rearrange("(h p) m -> p h m", p=P)).then_inc(s_w, 16)
            sp.dma_start(w2_raw, w2bd).then_inc(s_w, 16)
            sp.dma_start(vec[:, :], vec128).then_inc(s_w, 16)
            sp.dma_start(w3_sb[:, :], w3r).then_inc(s_w, 16)
            sp.dma_start(g3_sb[:, :, :].rearrange("p a c -> p (a c)"), bc3).then_inc(s_w, 16)
            sp.dma_start(mk[:, :], masks).then_inc(s_w, 16)
            for n in range(NLOAD):
                if n >= 2:
                    sp.wait_ge(s_c1, 4 * (n - 1))
                sp.dma_start(xc[:, n % 2, :, :], x2[:, LOADW * n:LOADW * n + LOADW].rearrange("(h p) n -> p h n", p=P)
                             ).then_inc(s_x[n % 2], 16)
            for n in range(NLOAD):
                for i in range(NPARTS):
                    sp.wait_ge(s_p[i], n + 1)
                    for h in range(HD):
                        sp.dma_start(parts[:, HD * i + h, LOADW * n:LOADW * n + LOADW],
                                     yp[32 * h:32 * h + 32, n % 2, i, :]).then_inc(s_pst[n % 2], 16)
            sp.wait_ge(s_wp, 1)
            for h in range(HD):
                for cp, count in ((0, 3), (3, 2), (5, 1)):
                    rows = wparts[:, HD * cp + h:HD * (cp + count - 1) + h + 1:HD, :]
                    sp.dma_start(rows, ap[32 * h:32 * h + 32, 0, 0:count, :]).then_inc(s_wst, 16)
            sp.dma_start(wparts[:, KROWS:KROWS + KBIAS, :], ap[0:32, 1, :, :]).then_inc(s_wst, 16)
            sp.wait_ge(s_wst, 16 * (3 * HD + 1))
            for i in range(2):
                sp.wait_ge(s_pst[i], 16 * NPARTS * HD * NLOAD // 2)

        @block.gpsimd
        def _(pool):
            for part in y1:
                nc.gpsimd.memset(part[:, :, :].rearrange("p a n -> p (a n)").bitcast(F32), 0.0).then_inc(s_zero, 1)
            for n in range(NLOAD):
                pool.wait_ge(s_p[1], n + 1)
                nc.gpsimd.tensor_tensor(yp[:, n % 2, 2, :], rest[:, n % 2, :], yp[:, n % 2, 1, :], ALU.subtract).then_inc(s_p[2], 1)

        @block.tensor
        def _(pe):
            pe.wait_ge(s_w, 16 * NW)
            for n in range(NFILL):
                if n % 4 == 0:
                    pe.wait_ge(s_x[(n // 4) % 2], 16 * (n // 8 + 1))
                if n >= 4:
                    pe.wait_ge(s_k1, n - 3)
                for h in range(CH):
                    mm = nc.tensor.matmul(bank[n % 4][:, :], w1_sb[:, h, :],
                                          xc[:, (n // 4) % 2, h, CHUNK * (n % 4):CHUNK * (n % 4) + CHUNK],
                                          start=(h == 0), stop=(h == 1))
                mm.then_inc(s_c1, 1)
            for n in range(NFILL):
                b, y = n // 8, 8 * (n % 8)
                if n == 0:
                    pe.wait_ge(s_w2l, 1)
                if n % 8 in (0, 3):
                    pe.wait_ge(s_yl, 2 * b + 1 + (n % 8) // 3)
                if n >= 4:
                    pe.wait_ge(s_k2, n - 3)
                rows = [part[:, b % 2, :].rearrange("p (y x) -> p y x", x=PITCH) for part in y1]
                terms = [(k, i, j) for k in range(TAPS) for i, j in ((1, 0), (0, 1), (0, 0))]
                for k, i, j in terms:
                    mm = nc.tensor.matmul(bank[4 + n % 4][:, :], w2[i][:, k, :],
                                          rows[j][:, y + k // 3:y + k // 3 + 8, k % 3:k % 3 + W],
                                          start=((k, i, j) == terms[0]), stop=((k, i, j) == terms[-1]))
                mm.then_inc(s_c2, 1)
            pe.wait_ge(s_k2, NFILL)

            def covary(n):
                pe.wait_ge(s_tk, n + 1)
                for i in range(4):
                    t = yt[:, n % 2, P * i:P * i + P]
                    mm = nc.tensor.matmul(bank[7][:, 0:P], t, t, start=(n == 0 and i == 0),
                                          stop=(n == NFILL - 1 and i == 3))
                mm.then_inc(s_cov, 1)

            for n in range(NFILL):
                pe.wait_ge(s_cen, n + 1)
                if n >= 2:
                    pe.wait_ge(s_tk, n - 1)
                for i in range(4):
                    mm = nc.tensor.transpose(bank[n % 2][:, P * i:P * i + P], cen[:, n % 2, P * i:P * i + P], mk[:, 0:P])
                mm.then_inc(s_tp, 1)
                if n:
                    covary(n - 1)
            covary(NFILL - 1)
            pe.wait_ge(s_cm, 1)
            nc.tensor.matmul(bank[2][:, 0:C], covm, w3_sb[:, :], start=True, stop=True).then_inc(s_t, 1)
            pe.wait_ge(s_u, 1)
            nc.tensor.matmul(bank[3][:, 0:C], mk[:, P:2 * P], tcov, start=True, stop=True)
            nc.tensor.matmul(bank[4][:, 0:C], mk[:, P:2 * P], tmean, start=True, stop=True).then_inc(s_m3, 1)

        @block.scalar
        def _(act):
            act.wait_ge(s_w, 16 * NW)
            nc.scalar.activation(w2[0][:, :, :].rearrange("p k m -> p (k m)"), w2_raw, ACT.Copy).then_inc(s_w2, 1)
            for n in range(NFILL):
                act.wait_ge(s_c1, n + 1)
                nc.scalar.activation(y2[:, CHUNK * n:CHUNK * n + CHUNK], bank[n % 4][:, :],
                                     ACT.Identity, bias=vec[:, 0:1]).then_inc(s_k1, 1)
            act.wait_ge(s_var, 1)
            nc.scalar.activation(tiny[:, 1:2], tiny[:, 0:1], ACT.Sqrt).then_inc(s_std, 1)
            act.wait_ge(s_sc, 1)
            act.wait_ge(s_zero, 2)

            def normalise(b):
                if b >= 2:
                    act.wait_ge(s_c2, 8 * (b - 1))
                for q in range(2):
                    half = y2[:, LOADW * (2 * b + q):LOADW * (2 * b + q + 1)]
                    nc.scalar.activation(half, half, ACT.Relu, scale=tiny[:, 2:3], bias=tiny[:, 3:4]).then_inc(s_n1, 1)
                    act.wait_ge(s_n1, 2 * b + q + 1)
                    nc.scalar.activation(half_rows(y1[0], b, q), half.rearrange("p (y x) -> p y x", x=W),
                                         ACT.Copy).then_inc(s_yh, 1)

            normalise(0)
            for n in range(NFILL):
                if n % 8 == 0 and n // 8 + 1 < B:
                    normalise(n // 8 + 1)
                act.wait_ge(s_c2, n + 1)
                nc.scalar.activation(y2[:, CHUNK * n:CHUNK * n + CHUNK], bank[4 + n % 4][:, :], ACT.Identity,
                                     bias=vec[:, 3:4]).then_inc(s_k2, 1)
            act.wait_ge(s_var, 2)
            nc.scalar.activation(tiny[:, 5:6], tiny[:, 4:5], ACT.Sqrt).then_inc(s_std, 1)
            act.wait_ge(s_sc, 2)
            for n in range(NLOAD):
                part = y2[:, LOADW * n:LOADW * n + LOADW]
                nc.scalar.activation(part, part, ACT.Relu, scale=tiny[:, 6:7], bias=tiny[:, 7:8],
                                     accum_out=sums[:, n:n + 1]).then_inc(s_n2, 1)

            def keep_turned(n):
                act.wait_ge(s_tp, n + 1)
                if n >= 2:
                    act.wait_ge(s_cov, n - 1)
                nc.scalar.activation(yt[:, n % 2, :], bank[n % 2][:, :], ACT.Copy).then_inc(s_tk, 1)

            def first_part(n):
                if n >= 2:
                    act.wait_ge(s_pst[n % 2], 16 * NPARTS * HD * (n // 2))
                act.wait_ge(s_n2, n + 1)
                nc.scalar.activation(yp[:, n % 2, 0, :], y2[:, LOADW * n:LOADW * n + LOADW], ACT.Copy).then_inc(s_p[0], 1)

            first_part(0)
            for n in range(NLOAD):
                for i in range(4):
                    if i == 2:
                        act.wait_ge(s_rest, n + 1)
                        nc.scalar.activation(yp[:, n % 2, 1, :], rest[:, n % 2, :], ACT.Copy).then_inc(s_p[1], 1)
                    keep_turned(4 * n + i)
                if n + 1 < NLOAD:
                    first_part(n + 1)
            act.wait_ge(s_v3, 1)
            nc.scalar.activation(s3, tcov, ACT.Sqrt).then_inc(s_d3, 1)

        @block.vector
        def _(dve):
            steps = [0]

            def link(ins):
                steps[0] += 1
                ins.then_inc(s_dv, 1)
                dve.wait_ge(s_dv, steps[0])

            def norm(n, st, mv, g, be):
                o = 4 * n
                link(nc.vector.memset(tiny[:, o:o + 1], 0.0))
                link(nc.vector.bn_aggr(mv[:, :], st[:, :, :].rearrange("p g s -> p (g s)")))
                nc.vector.tensor_scalar(tiny[:, o:o + 1], mv[:, 1:2], EPS, None, ALU.add).then_inc(s_var, 1)
                dve.wait_ge(s_std, n + 1)
                link(nc.vector.reciprocal(tiny[:, 8:9], tiny[:, o + 1:o + 2]))
                link(nc.vector.tensor_tensor(tiny[:, o + 2:o + 3], tiny[:, 8:9], vec[:, g:g + 1], ALU.mult))
                link(nc.vector.tensor_tensor(tiny[:, 9:10], mv[:, 0:1], tiny[:, o + 2:o + 3], ALU.mult))
                nc.vector.tensor_tensor(tiny[:, o + 3:o + 4], vec[:, be:be + 1], tiny[:, 9:10], ALU.subtract).then_inc(s_sc, 1)

            dve.wait_ge(s_w, 16 * NW)
            dve.wait_ge(s_w2, 1)
            nc.vector.tensor_tensor(w2[1][:, :, :].rearrange("p k m -> p (k m)"), w2_raw,
                                    w2[0][:, :, :].rearrange("p k m -> p (k m)").bitcast(F32),
                                    ALU.subtract).then_inc(s_w2l, 1)
            for n in range(NFILL):
                dve.wait_ge(s_k1, n + 1)
                nc.vector.bn_stats(st1[:, n, :], y2[:, CHUNK * n:CHUNK * n + CHUNK])
            norm(0, st1, mv1, 1, 2)
            dve.wait_ge(s_zero, 2)

            def split(b):
                for q in range(2):
                    dve.wait_ge(s_yh, 2 * b + q + 1)
                    half = y2[:, LOADW * (2 * b + q):LOADW * (2 * b + q + 1)]
                    nc.vector.tensor_tensor(half_rows(y1[1], b, q), half.rearrange("p (y x) -> p y x", x=W),
                                            half_rows(y1[0], b, q).bitcast(F32), ALU.subtract).then_inc(s_yl, 1)

            split(0)
            for n in range(NFILL):
                if n % 8 == 0 and n // 8 + 1 < B:
                    split(n // 8 + 1)
                dve.wait_ge(s_k2, n + 1)
                nc.vector.bn_stats(st2[:, n, :], y2[:, CHUNK * n:CHUNK * n + CHUNK])
            norm(1, st2, mv2, 4, 5)
            dve.wait_ge(s_n2, NLOAD)
            link(nc.vector.reduce_sum(tiny[:, 10:11], sums[:, :], AX_X))
            link(nc.vector.tensor_scalar(tiny[:, 11:12], tiny[:, 10:11], 1.0 / ALL, None, ALU.mult))
            def subtract_first_part(m):
                dve.wait_ge(s_p[0], m + 1)
                if m >= 2:
                    dve.wait_ge(s_p[2], m - 1)
                nc.vector.tensor_tensor(rest[:, m % 2, :], y2[:, LOADW * m:LOADW * m + LOADW], yp[:, m % 2, 0, :],
                                        ALU.subtract).then_inc(s_rest, 1)

            for n in range(NFILL):
                if n % 4 == 2:
                    subtract_first_part(n // 4)
                if n >= 2:
                    dve.wait_ge(s_tp, n - 1)
                nc.vector.tensor_scalar(cen[:, n % 2, :], y2[:, CHUNK * n:CHUNK * n + CHUNK], tiny[:, 11:12], None,
                                        ALU.subtract).then_inc(s_cen, 1)
            dve.wait_ge(s_cov, NFILL)
            nc.vector.scalar_tensor_tensor(out=covm, in0=bank[7][:, 0:P], scalar=1.0 / ALL, in1=mk[:, P:2 * P],
                                           op0=ALU.mult, op1=ALU.mult).then_inc(s_cm, 1)
            nc.vector.tensor_scalar(tmean, w3_sb[:, :], tiny[:, 11:12], None, ALU.mult)
            dve.wait_ge(s_t, 1)
            nc.vector.tensor_tensor(tcov, bank[2][:, 0:C], w3_sb[:, :], ALU.mult).then_inc(s_u, 1)
            dve.wait_ge(s_m3, 1)
            nc.vector.tensor_scalar(tcov, bank[3][:, 0:C], EPS, None, ALU.add).then_inc(s_v3, 1)
            link(nc.vector.tensor_tensor(tmean, bank[4][:, 0:C], g3_sb[:, 2, :], ALU.add))
            link(nc.vector.tensor_tensor(b3, g3_sb[:, 2, :], tmean, ALU.subtract))
            dve.wait_ge(s_d3, 1)
            link(nc.vector.reciprocal(a3, s3))
            link(nc.vector.tensor_tensor(s3, a3, g3_sb[:, 0, :], ALU.mult))
            link(nc.vector.tensor_tensor(a3, w3_sb[:, :], s3, ALU.mult))
            link(nc.vector.tensor_tensor(tmean, b3, s3, ALU.mult))
            link(nc.vector.tensor_tensor(b3, tmean, g3_sb[:, 1, :], ALU.add))
            for k, v in enumerate((a3, b3)):
                link(nc.vector.tensor_copy(ap[:, k, 0, :], v))
                link(nc.vector.tensor_tensor(s3, v, ap[:, k, 0, :], ALU.subtract))
                link(nc.vector.tensor_copy(ap[:, k, 1, :], s3))
                ins = nc.vector.tensor_tensor(ap[:, k, 2, :], s3, ap[:, k, 1, :], ALU.subtract)
                if k == 0:
                    link(ins)
            ins.then_inc(s_wp, 1)


TILE = 1024
NT = ALL // TILE
PIECES = TILE // CHUNK
GRING = 2
VSLOTS = 3
KIND = ["G" if p % 3 == 1 else "V" for p in range(PATHS)]
VUNITS = [(p, h) for p in range(PATHS) if KIND[p] == "V" for h in range(CH)]
GUNITS = [(p, h) for p in range(PATHS) if KIND[p] == "G" for h in range(CH)]
NV, NG, NA = len(VUNITS), len(GUNITS), PIECES * len(GUNITS)
NADD = NG - CH
STATS_AT = (8, 11, 14, 17)
MERGE_G = 7


def tensor_schedule():
    steps, k = [], 0
    for i in range(NV):
        steps.append(("V", i))
        while k * NV < NA * (i + 1):
            steps.append(("A", k))
            k += 1
    return steps


def expand_block(nc, x2, parts, wparts, total, sums, centre):
    with ExitStack() as ctx:
        def sb(name, shape, dt=F32):
            return ctx.enter_context(nc.sbuf_tensor(name, shape, dt))

        def sem(name):
            return ctx.enter_context(nc.semaphore(name))

        wl = sb("wl", [P, PATHS, C], BF16)
        yv = sb("yv", [P, 2, PATHS // 4, TILE], BF16)
        acc = sb("acc", [P, 2, CH, TILE])
        spent = sb("spent", [P, TILE])
        first_stats = sb("first_stats", [P, CH, PIECES, 6])
        first_mv = sb("first_mv", [P, CH, 2])
        tmpg = sb("tmpg", [P, GRING, TILE])
        vslot = [ctx.enter_context(nc.psum_tensor(f"vslot{i}", [P, TILE], F32)) for i in range(VSLOTS)]
        abank = [ctx.enter_context(nc.psum_tensor(f"abank{i}", [P, CHUNK], F32)) for i in range(2)]

        s_w = sem("e_weights_loaded")
        s_wz = sem("e_weights_zeroed")
        s_one = sem("e_ones_set")
        s_y = [sem(f"e_parts_loaded{i}") for i in range(2)]
        s_x = [sem(f"e_x_loaded{i}") for i in range(2)]
        s_zv = sem("e_product_for_vector")
        s_za = sem("e_product_for_scalar")
        s_vec = sem("e_added_by_vector")
        s_rel = sem("e_rectified")
        s_pool = sem("e_added_by_pool")
        s_mrg = sem("e_merged")
        s_fm = sem("e_first_tile_moments")
        s_ctr = sem("e_centre_ready")
        s_stat = sem("e_statistics_summed")
        schedule = tensor_schedule()
        block = ctx.enter_context(nc.Block())

        def tiles(eng, tile):
            tile(0, 0)
            tile(1, 1)
            with eng.Fori(1, NT // 2) as it:
                for a in range(2):
                    tile(2 * it + a, a)

        def first(t):
            return isinstance(t, int) and t == 0

        def loaded(t, a, each):
            return each * ((t - a) // 2 + 1) if isinstance(t, int) else each // 2 * (t - a) + each

        @block.sync
        def _(sp):
            sp.wait_ge(s_wz, 1)
            for pq in range(4):
                sp.dma_start(wl[:, :, :].rearrange("p (q r) c -> p r q c", r=4)[32 * pq:32 * pq + KROWS + KBIAS, pq],
                             wparts.rearrange("(q r) k c -> r k q c", r=4)[pq]).then_inc(s_w, 16)

            def load(t, a):
                src = parts.rearrange("(q r) k n -> r k q n", r=4)
                for pq in range(4):
                    for cp, (_, i) in enumerate(PART3):
                        row = 32 * pq + HD * cp
                        sp.dma_start(yv[row:row + HD, a, :, :],
                                     src[pq, HD * i:HD * (i + 1), :, bass.ds(TILE * t, TILE)]).then_inc(s_y[a], 16)
                sp.dma_start(total[:, :, bass.ds(TILE * t, TILE)], x2.rearrange("(h p) n -> p h n", p=P)[:, :, bass.ds(TILE * t, TILE)]).then_inc(s_x[a], 16)

            for a in range(2):
                sp.wait_ge(s_one, a + 1)
                load(a, a)
            with sp.Fori(1, NT // 2) as it:
                for a in range(2):
                    sp.wait_ge(s_zv, NV * (2 * it + a - 1))
                    sp.nop(nofuse=True)
                    sp.wait_ge(s_za, NA * (2 * it + a - 1))
                    sp.nop(nofuse=True)
                    load(2 * it + a, a)

        @block.tensor
        def _(pe):
            pe.wait_ge(s_w, 16 * 4)

            def product(out, a, p, h, at):
                return nc.tensor.matmul(out, wl[:, p, h * P:(h + 1) * P], yv[:, a, p // 4, at:at + CHUNK],
                                        start=True, stop=True)

            def tile(t, a):
                pe.wait_ge(s_y[a], loaded(t, a, 16 * 4 * NCOPY))
                for kind, i in schedule:
                    if kind == "V":
                        if not (first(t) and i < VSLOTS):
                            pe.wait_ge(s_vec, NV * t + i + 1 - VSLOTS)
                        for c in range(PIECES):
                            mm = product(vslot[i % VSLOTS][:, CHUNK * c:CHUNK * c + CHUNK], a, *VUNITS[i], CHUNK * c)
                        mm.then_inc(s_zv, 1)
                    if kind == "A":
                        if not (first(t) and i < 2):
                            pe.wait_ge(s_rel, NA * t + i - 1)
                        product(abank[i % 2][:, :], a, *GUNITS[i // PIECES], CHUNK * (i % PIECES)).then_inc(s_za, 1)

            tiles(pe, tile)

        @block.scalar
        def _(act):
            def tile(t, a):
                for i, (p, h) in enumerate(GUNITS):
                    if i < CH:
                        dst = acc[:, a, h, :]
                        if not isinstance(t, int):
                            act.wait_ge(s_mrg, 2 * (t - 1))
                    else:
                        dst = tmpg[:, i % GRING, :]
                        if not (first(t) and i < CH + GRING):
                            act.wait_ge(s_pool, NADD * t + i + 1 - CH - GRING)
                    for c in range(PIECES):
                        k = PIECES * i + c
                        act.wait_ge(s_za, NA * t + k + 1)
                        nc.scalar.activation(dst[:, CHUNK * c:CHUNK * c + CHUNK], abank[k % 2][:, :],
                                             ACT.Relu).then_inc(s_rel, 1)
                    if i in STATS_AT and not first(t):
                        statistics(t - 1, STATS_AT.index(i))

            def statistics(t, n):
                h = n % CH
                if n == 0:
                    act.wait_ge(s_ctr, 1)
                    act.wait_ge(s_mrg, CH * (t + 1))
                if not (first(t) and n == 0):
                    act.wait_ge(s_stat, 2 * CH * t + n)
                column = sums[:, n, t:t + 1] if isinstance(t, int) else sums[:, n, bass.ds(t, 1)]
                nc.scalar.activation(spent[:, :], total[:, h, bass.ds(TILE * t, TILE)], ACT.Square if n >= CH else ACT.Identity,
                                     bias=centre[:, h:h + 1], accum_out=column).then_inc(s_stat, 1)

            tiles(act, tile)
            for n in range(2 * CH):
                statistics(NT - 1, n)

        @block.gpsimd
        def _(pool):
            for a in range(2):
                nc.gpsimd.memset(yv[:, a, :, :].rearrange("p q n -> p (q n)"), 1.0).then_inc(s_one, 1)

            def tile(t, a):
                for i, (p, h) in list(enumerate(GUNITS))[CH:]:
                    pool.wait_ge(s_rel, NA * t + PIECES * (i + 1))
                    if i >= 2 * CH:
                        pool.wait_ge(s_pool, NADD * t + i - CH - 1)
                    nc.gpsimd.tensor_tensor(acc[:, a, h, :], tmpg[:, i % GRING, :], acc[:, a, h, :],
                                            ALU.add).then_inc(s_pool, 1)

            tiles(pool, tile)

        @block.vector
        def _(dve):
            nc.vector.memset(wl[:, :, :].rearrange("p q c -> p (q c)"), 0.0).then_inc(s_wz, 1)

            def here(t, h, c0=0, n=TILE):
                return total[:, h, bass.ds(TILE * t + c0, n)]

            def merge_pool(t, a):
                dve.wait_ge(s_pool, NADD * (t + 1))
                dve.wait_ge(s_vec, NV * (t + 1))
                for h in range(CH):
                    nc.vector.tensor_tensor(here(t, h), here(t, h), acc[:, a, h, :], ALU.add).then_inc(s_mrg, 1)
                if first(t):
                    dve.wait_ge(s_mrg, CH)
                    for h in range(CH):
                        for c in range(PIECES):
                            ins = nc.vector.bn_stats(first_stats[:, h, c, :], here(t, h, CHUNK * c, CHUNK))
                    ins.then_inc(s_fm, 1)
                    dve.wait_ge(s_fm, 1)
                    for h in range(CH):
                        ins = nc.vector.bn_aggr(first_mv[:, h, :], first_stats[:, h, :, :].rearrange("p g s -> p (g s)"))
                    ins.then_inc(s_fm, 1)
                    dve.wait_ge(s_fm, 2)
                    nc.vector.tensor_scalar(centre[:, :], first_mv[:, :, 0], -1.0, None, ALU.mult).then_inc(s_ctr, 1)

            def tile(t, a):
                for i, (p, h) in enumerate(VUNITS):
                    if i == MERGE_G and not first(t):
                        merge_pool(t - 1, 1 - a)
                    dve.wait_ge(s_zv, NV * t + i + 1)
                    z = vslot[i % VSLOTS][:, :]
                    if i == 0:
                        dve.wait_ge(s_x[a], loaded(t, a, 16))
                    if i >= CH:
                        dve.wait_ge(s_vec, NV * t + i - 1)
                    nc.vector.scalar_tensor_tensor(out=here(t, h), in0=z, scalar=0.0, in1=here(t, h),
                                                   op0=ALU.max, op1=ALU.add).then_inc(s_vec, 1)

            tiles(dve, tile)
            merge_pool(NT - 1, 1)


SC = 1024


def sequence_block(nc, total, sums, centre, vec256, out):
    with ExitStack() as ctx:
        def sb(name, shape, dt=F32):
            return ctx.enter_context(nc.sbuf_tensor(name, shape, dt))

        def sem(name):
            return ctx.enter_context(nc.semaphore(name))

        vec = sb("seq_vec", [P, 6, CH])
        mom = sb("seq_mom", [P, 2, CH])
        mean = sb("seq_mean", [P, CH])
        sm = sb("seq_sm", [P, 10, CH])
        v = sb("seq_v", [P, 2, PIX + 2])
        u = sb("seq_u", [P, 2, PIX])
        keep = sb("seq_keep", [P, SC])
        s_w = sem("r_vectors_loaded")
        s_dv = sem("r_vector_step")
        s_var = sem("r_variance")
        s_std = sem("r_deviation")
        s_sc = sem("r_scales")
        s_edge = sem("r_edges_zeroed")
        s_v = sem("r_normalised")
        s_u = sem("r_tenth")
        s_c = sem("r_middle")
        s_e = sem("r_average_part")
        s_t = sem("r_taps")
        s_sum = sem("r_summed")
        s_out = sem("r_stored")
        block = ctx.enter_context(nc.Block())
        rows = [(h, b) for b in range(B) for h in range(CH)]
        NSC = PIX // SC

        @block.sync
        def _(sp):
            sp.dma_start(vec[:, :, :].rearrange("p a h -> p (a h)"), vec256).then_inc(s_w, 16)
            for r, (h, b) in enumerate(rows):
                sp.wait_ge(s_sum, r + 1)
                sp.dma_start(out[b, h * P:(h + 1) * P, :], total[:, h, PIX * b:PIX * b + PIX]).then_inc(s_out, 16)
            sp.wait_ge(s_out, 16 * len(rows))

        @block.gpsimd
        def _(pool):
            nc.gpsimd.memset(v[:, :, 0:1], 0.0).then_inc(s_edge, 1)
            nc.gpsimd.memset(v[:, :, PIX + 1:PIX + 2], 0.0).then_inc(s_edge, 1)
            nc.gpsimd.memset(keep[:, :], 0.9).then_inc(s_edge, 1)
            for r, (h, b) in enumerate(rows):
                pool.wait_ge(s_e, NSC * (r + 1))
                pool.wait_ge(s_t, 2 * (r + 1))
                dst = total[:, h, PIX * b:PIX * b + PIX]
                nc.gpsimd.tensor_tensor(dst, dst, u[:, r % 2, :], ALU.add).then_inc(s_sum, 1)

        @block.scalar
        def _(act):
            act.wait_ge(s_var, 1)
            nc.scalar.activation(sm[:, 1, :], sm[:, 0, :], ACT.Sqrt).then_inc(s_std, 1)
            act.wait_ge(s_sc, 1)
            for r, (h, b) in enumerate(rows):
                src = total[:, h, PIX * b:PIX * b + PIX]
                if r >= 2:
                    act.wait_ge(s_t, 2 * (r - 1))
                nc.scalar.activation(v[:, r % 2, 1:PIX + 1], src, ACT.Identity, scale=sm[:, 2, h:h + 1],
                                     bias=sm[:, 3, h:h + 1]).then_inc(s_v, 1)
                if r >= 2:
                    act.wait_ge(s_sum, r - 1)
                nc.scalar.activation(u[:, r % 2, :], src, ACT.Identity, scale=sm[:, 4, h:h + 1],
                                     bias=sm[:, 5, h:h + 1]).then_inc(s_u, 1)
                nc.scalar.activation(src, src, ACT.Identity, scale=sm[:, 6, h:h + 1],
                                     bias=sm[:, 7, h:h + 1]).then_inc(s_c, 1)

        @block.vector
        def _(dve):
            steps = [0]

            def link(ins):
                steps[0] += 1
                ins.then_inc(s_dv, 1)
                dve.wait_ge(s_dv, steps[0])

            dve.wait_ge(s_w, 16)
            link(nc.vector.memset(sm[:, :, :].rearrange("p a h -> p (a h)"), 0.0))
            flat = mom[:, :, :].rearrange("p a h -> p (a h)")
            link(nc.vector.reduce_sum(flat, sums[:, :, :], AX_X))
            link(nc.vector.tensor_scalar(flat, flat, 1.0 / ALL, None, ALU.mult))
            link(nc.vector.tensor_tensor(mean[:, :], mom[:, 0, :], centre[:, :], ALU.subtract))
            link(nc.vector.tensor_tensor(sm[:, 9, :], mom[:, 0, :], mom[:, 0, :], ALU.mult))
            link(nc.vector.tensor_tensor(sm[:, 8, :], mom[:, 1, :], sm[:, 9, :], ALU.subtract))
            nc.vector.tensor_scalar(sm[:, 0, :], sm[:, 8, :], EPS, None, ALU.add).then_inc(s_var, 1)
            dve.wait_ge(s_std, 1)
            link(nc.vector.reciprocal(sm[:, 8, :], sm[:, 1, :]))
            link(nc.vector.tensor_tensor(sm[:, 2, :], sm[:, 8, :], vec[:, 0, :], ALU.mult))
            link(nc.vector.tensor_tensor(sm[:, 9, :], mean[:, :], sm[:, 2, :], ALU.mult))
            link(nc.vector.tensor_tensor(sm[:, 3, :], vec[:, 1, :], sm[:, 9, :], ALU.subtract))
            link(nc.vector.tensor_scalar(sm[:, 4:6, :], sm[:, 2:4, :], 0.1, None, ALU.mult))
            link(nc.vector.tensor_scalar(sm[:, 8, :], vec[:, 3, :], 1.0, None, ALU.add))
            link(nc.vector.tensor_tensor(sm[:, 6, :], sm[:, 2, :], sm[:, 8, :], ALU.mult))
            link(nc.vector.tensor_tensor(sm[:, 9, :], sm[:, 3, :], sm[:, 8, :], ALU.mult))
            nc.vector.tensor_tensor(sm[:, 7, :], sm[:, 9, :], vec[:, 5, :], ALU.add).then_inc(s_sc, 1)
            dve.wait_ge(s_edge, 3)
            for r, (h, b) in enumerate(rows):
                dst = total[:, h, PIX * b:PIX * b + PIX]
                a = r % 2
                dve.wait_ge(s_u, r + 1)
                for c in range(NSC):
                    part = u[:, a, SC * c:SC * c + SC]
                    if c:
                        dve.wait_ge(s_e, NSC * r + c)
                    start = u[:, a, SC * c - 1:SC * c] if c else v[:, a, 1:2]
                    nc.vector.tensor_tensor_scan(part, keep[:, :], part, start, ALU.mult, ALU.add).then_inc(s_e, 1)
                dve.wait_ge(s_c, r + 1)
                for i, (tap, at) in enumerate(((2, 0), (4, 2))):
                    if i:
                        dve.wait_ge(s_t, 2 * r + 1)
                    nc.vector.scalar_tensor_tensor(out=dst, in0=v[:, a, at:at + PIX], scalar=vec[:, tap, h:h + 1], in1=dst,
                                                   op0=ALU.mult, op1=ALU.add).then_inc(s_t, 1)


def layer23(nc, x2, a, parts, wparts, out):
    squeeze_block(nc, x2, a["w1t"], a["w2bd"], a["vec128"], a["w3r"], a["bc3"], a["masks"], parts, wparts)
    with ExitStack() as ctx:
        total = ctx.enter_context(nc.sbuf_tensor("total", [P, CH, ALL], F32))
        sums = ctx.enter_context(nc.sbuf_tensor("value_sums", [P, 2 * CH, NT], F32))
        centre = ctx.enter_context(nc.sbuf_tensor("centre", [P, CH], F32))
        expand_block(nc, x2, parts, wparts, total, sums, centre)
        sequence_block(nc, total, sums, centre, a["vec256"], out)


def host0(inputs):
    f = np.float32
    out = {"x": inputs["x"].reshape(B, C, PIX)}
    for l in range(2):
        n = str(l + 1)
        out[f"wdc{l}"] = np.ascontiguousarray(
            inputs["L0_conv_w_dc" + n].reshape(C, C, TAPS).transpose(1, 2, 0)).reshape(C, TAPS * C)
        w = np.concatenate([inputs["L0_conv_w_tm" + n], inputs["L0_conv_w_tr" + n]]).reshape(NOFF, C, TAPS)
        out[f"woff{l}"] = np.ascontiguousarray(w.transpose(1, 2, 0)).reshape(C, NPART)
        out[f"boff{l}"] = np.concatenate([inputs["L0_conv_b_tm" + n], inputs["L0_conv_b_tr" + n]]).reshape(NOFF, 1)
    gb = np.stack([np.stack([inputs[f"L0_conv_g{n}"], inputs[f"L0_conv_be{n}"]]) for n in (1, 2)])
    out["gb"] = np.ascontiguousarray(gb.reshape(2, 2, CH, P).transpose(3, 0, 1, 2)).reshape(P, 4 * CH)
    c = np.zeros((P, 2 * P + NPOS + NTILE * NPOS), f)
    c[:, 0:P] = np.eye(P, dtype=f)
    c[:, P:2 * P] = np.kron(np.eye(P // GN_GROUP, dtype=f), np.full((GN_GROUP, GN_GROUP), 1 / GN_GROUP, f))
    for k in range(TAPS):
        ry, rx = k // 3 - 1, k % 3 - 1
        for tap in range(TAPS):
            for o, col, v in ((0, k, ry), (1, k, rx), (4, k, 1), (2, TAPS + k, ry), (3, TAPS + k, rx), (5, TAPS + k, 1)):
                c[NOFF * tap + o, 2 * P + col] = v
    at = c[:, 2 * P + NPOS:].reshape(P, NTILE, 2, TAPS)
    at[:, :, 0, :] = (2 * np.arange(NTILE)[None, :, None] + (np.arange(P) // W)[:, None, None])
    at[:, :, 1, :] = (np.arange(P) % W)[:, None, None]
    out["consts"] = c
    return out


def host1(inputs):
    w = np.concatenate([inputs["L1_conv_w_theta"], inputs["L1_conv_w_phi"], inputs["L1_conv_w_g"]])
    return {"wproj": np.ascontiguousarray(w.T), "wmask": np.ascontiguousarray(inputs["L1_conv_w_mask"].T)}


def host2(inputs):
    f = np.float32
    hp = lambda a: np.ascontiguousarray(a.reshape(PATHS, HD, *a.shape[1:]).swapaxes(0, 1)).reshape(a.shape)
    g = lambda n: inputs["L2_conv_" + n]
    out = {"w1t": np.ascontiguousarray(g("w1").T)}
    w2 = g("w2").reshape(PATHS, HD, HD, TAPS)
    bd = np.zeros((PATHS, HD, TAPS, HD, PATHS), f)
    for p in range(PATHS):
        bd[p, :, :, :, p] = w2[p].transpose(1, 2, 0)
    out["w2bd"] = bd.reshape(P, TAPS * P)
    out["vec128"] = np.ascontiguousarray(np.stack(
        [g("b1"), g("g1"), g("be1"), hp(g("b2")), hp(g("g2")), hp(g("be2"))], axis=1))
    out["w3r"] = np.ascontiguousarray(g("w3").transpose(2, 0, 1)).reshape(P, C)
    bc = np.stack([g("g3"), g("be3"), g("b3")], axis=1)
    out["bc3"] = np.ascontiguousarray(np.broadcast_to(bc[None], (HD, PATHS, 3, C))).reshape(P, 3 * C)
    out["masks"] = np.concatenate([np.eye(P, dtype=f), np.kron(np.ones((HD, HD), f), np.eye(PATHS, dtype=f))], axis=1)
    k = inputs["L3_conv_conv_w"].reshape(C, 3)
    v = np.stack([g("g4"), g("be4"), k[:, 0], k[:, 1], k[:, 2], inputs["L3_conv_conv_b"]])
    out["vec256"] = np.ascontiguousarray(v.reshape(6, CH, P).transpose(2, 0, 1)).reshape(P, 6 * CH)
    return out


def build(nc, a, out):
    table = [nc.dram_tensor(f"table{b}", (CELLS, PATCH), F32).ap() for b in range(B)]
    x1 = nc.dram_tensor("x1", (B, C, PIX), F32).ap()
    x2 = nc.dram_tensor("x2", (C, ALL), F32).ap()
    parts = nc.dram_tensor("parts", (PATHS, NPARTS * HD, ALL), BF16).ap()
    wparts = nc.dram_tensor("wparts", (PATHS, KROWS + KBIAS, C), BF16).ap()
    deformable_block(nc, a["x"], [a["wdc0"], a["wdc1"]], [a["woff0"], a["woff1"]], [a["boff0"], a["boff1"]],
                     a["gb"], table, x1, a["consts"])
    attention_block(nc, x1, a["wproj"], a["wmask"], x2)
    layer23(nc, x2, a, parts, wparts, out)


def kernel(**inputs):
    import concourse.bacc as bacc
    from concourse.bass_utils import run_bass_kernel_spmd

    inputs = {k: np.asarray(v) for k, v in inputs.items()}
    arrays = {**host0(inputs), **host1(inputs), **host2(inputs)}
    nc = bacc.Bacc("TRN2", target_bir_lowering=False, num_devices=1)
    args = {n: nc.dram_tensor(n, v.shape, mybir.dt.from_np(v.dtype), kind="ExternalInput").ap() for n, v in arrays.items()}
    out = nc.dram_tensor("out", (B, C, PIX), F32, kind="ExternalOutput").ap()
    build(nc, args, out)
    r = run_bass_kernel_spmd(nc, [arrays], core_ids=[0])
    return r.results[0]["out"].reshape(B, C, H, W)
```
